# Optimizing a Trainium2 kernel written in Bass

```python
import numpy as np
import jax
import jax.numpy as jnp

def _softmax(x, axis=-1):
    return jax.nn.softmax(x, axis=axis)

def _gelu(x):
    return jax.nn.gelu(x, approximate=True)

def _silu(x):
    return jax.nn.silu(x)

def _sigmoid(x):
    return jax.nn.sigmoid(x)

def _layernorm(x, axis=-1, eps=1e-05):
    m = jnp.mean(x, axis=axis, keepdims=True)
    v = jnp.var(x, axis=axis, keepdims=True)
    return (x - m) / jnp.sqrt(v + eps)

def _scatter_add(tgt, idx, src, axis=0):
    return tgt.at[idx].add(src)

def _segment_sum(src, seg, n):
    return jax.ops.segment_sum(src, seg, n)
kernel_name = 'mk_gnn_preln_d2_gnn_r32_cbff90'

def setup_inputs(seed: int=0):
    np.random.seed(seed)
    _w = jnp.asarray

    def _rec_inputs():
        import jax
        import jax.numpy as jnp
        _gk = jax.random.key(seed)
        x = -0.000202 + 1 * jax.random.normal(jax.random.fold_in(_gk, 1), (50000, 128), jnp.float32)
        src = jax.random.randint(jax.random.fold_in(_gk, 2), (25000,), 0, 50000, jnp.int32)
        dst = jax.random.randint(jax.random.fold_in(_gk, 3), (25000,), 0, 50000, jnp.int32)
        _o = jnp.argsort(dst, stable=True)
        src = src[_o]
        dst = dst[_o]
        edge_attr_128 = -4.21973e-05 + 0.999841 * jax.random.normal(jax.random.fold_in(_gk, 12), (25000, 128), jnp.float32)
        edge_type_8 = jax.random.randint(jax.random.fold_in(_gk, 14), (25000,), 0, 8, jnp.int32)
        return (x, src, dst, edge_attr_128, edge_type_8)
    x, src, dst, edge_attr_128, edge_type_8 = _rec_inputs()

    def _L0_gnn_setup():
        import jax, jax.numpy as jnp
        import numpy as np
        N = 50000
        E = 50000
        C = 128
        R = 8

        def _rgcn_layer(h, src, dst, et, W, SW, b, activate, residual):
            xw = jnp.einsum('nc,rco->rno', h, W)
            msg = xw[et, src]
            agg = jax.ops.segment_sum(msg, dst, num_segments=N)
            out = h @ SW + agg
            if residual:
                out = out + h
            if activate:
                out = jax.nn.relu(out)
            return out + b
        key = jax.random.key(seed)
        ks = jax.random.split(key, 9)
        scale = 1.0 / np.sqrt(C)
        return {'x': jax.random.normal(ks[0], (N, C), dtype=jnp.float32), 'edge_index': jax.random.randint(ks[1], (2, E), 0, N, dtype=jnp.int32), 'edge_type': jax.random.randint(ks[2], (E,), 0, R, dtype=jnp.int32), 'w1': jax.random.normal(ks[3], (R, C, C), dtype=jnp.float32) * scale, 'sw1': jax.random.normal(ks[4], (C, C), dtype=jnp.float32) * scale, 'b1': jnp.zeros((C,), dtype=jnp.float32), 'w2': jax.random.normal(ks[5], (R, C, C), dtype=jnp.float32) * scale, 'sw2': jax.random.normal(ks[6], (C, C), dtype=jnp.float32) * scale, 'b2': jnp.zeros((C,), dtype=jnp.float32)}
    _L0_gnn_all = _L0_gnn_setup()
    _L0_gnn_in = {k: v for k, v in _L0_gnn_all.items() if k in ('w1', 'sw1', 'b1', 'w2', 'sw2', 'b2')}
    del _L0_gnn_all

    def _L1_gnn_setup():
        import jax, jax.numpy as jnp
        import numpy as np
        N_NODES = 50000
        N_EDGES = 18750
        D = 128

        def _graph_conv(h, edge_fea, src, dst, inv_sqrt_deg, W, b, residual, act):
            m = h[src] + edge_fea
            agg = jax.ops.segment_sum(m, dst, num_segments=h.shape[0])
            rst = agg @ W + b
            rst = rst * inv_sqrt_deg
            if residual:
                rst = rst + h
            if act:
                rst = jax.nn.relu(rst)
            return rst
        key = jax.random.key(seed)
        ks = jax.random.split(key, 10)
        inp = {'node_fea': jax.random.normal(ks[0], (N_NODES, D), dtype=jnp.float32), 'edge_fea': jax.random.normal(ks[1], (N_EDGES, D), dtype=jnp.float32), 'src': jax.random.randint(ks[2], (N_EDGES,), 0, N_NODES), 'dst': jax.random.randint(ks[3], (N_EDGES,), 0, N_NODES), 'W0': jax.random.normal(ks[4], (D, D), dtype=jnp.float32) * 0.02, 'b0': jnp.zeros((D,), dtype=jnp.float32), 'W1': jax.random.normal(ks[5], (D, D), dtype=jnp.float32) * 0.02, 'b1': jnp.zeros((D,), dtype=jnp.float32), 'W2': jax.random.normal(ks[6], (D, D), dtype=jnp.float32) * 0.02, 'b2': jnp.zeros((D,), dtype=jnp.float32)}
        return inp
    _L1_gnn_all = _L1_gnn_setup()
    _L1_gnn_in = {k: v for k, v in _L1_gnn_all.items() if k in ('W0', 'b0', 'W1', 'b1', 'W2', 'b2')}
    del _L1_gnn_all
    return {'x': x, 'src': src, 'dst': dst, 'edge_attr_128': edge_attr_128, 'edge_type_8': edge_type_8, 'L0_gnn_w1': _L0_gnn_in['w1'], 'L0_gnn_sw1': _L0_gnn_in['sw1'], 'L0_gnn_b1': _L0_gnn_in['b1'], 'L0_gnn_w2': _L0_gnn_in['w2'], 'L0_gnn_sw2': _L0_gnn_in['sw2'], 'L0_gnn_b2': _L0_gnn_in['b2'], 'L1_gnn_W0': _L1_gnn_in['W0'], 'L1_gnn_b0': _L1_gnn_in['b0'], 'L1_gnn_W1': _L1_gnn_in['W1'], 'L1_gnn_b1': _L1_gnn_in['b1'], 'L1_gnn_W2': _L1_gnn_in['W2'], 'L1_gnn_b2': _L1_gnn_in['b2']}

def reference(x, src, dst, edge_attr_128, edge_type_8, L0_gnn_w1, L0_gnn_sw1, L0_gnn_b1, L0_gnn_w2, L0_gnn_sw2, L0_gnn_b2, L1_gnn_W0, L1_gnn_b0, L1_gnn_W1, L1_gnn_b1, L1_gnn_W2, L1_gnn_b2):
    import jax
    import jax.numpy as jnp

    def _L0_gnn_ref(x, edge_index, edge_type, w1, sw1, b1, w2, sw2, b2):
        import jax, jax.numpy as jnp
        import numpy as np
        N = 50000
        E = 50000
        C = 128
        R = 8

        def _rgcn_layer(h, src, dst, et, W, SW, b, activate, residual):
            xw = jnp.einsum('nc,rco->rno', h, W)
            msg = xw[et, src]
            agg = jax.ops.segment_sum(msg, dst, num_segments=N)
            out = h @ SW + agg
            if residual:
                out = out + h
            if activate:
                out = jax.nn.relu(out)
            return out + b
        src, dst = (edge_index[0], edge_index[1])
        h = _rgcn_layer(x, src, dst, edge_type, w1, sw1, b1, activate=True, residual=True)
        h = _rgcn_layer(h, src, dst, edge_type, w2, sw2, b2, activate=False, residual=False)
        return h

    def _L1_gnn_ref(node_fea, edge_fea, src, dst, W0, b0, W1, b1, W2, b2):
        import jax, jax.numpy as jnp
        import numpy as np
        N_NODES = 50000
        N_EDGES = 18750
        D = 128

        def _graph_conv(h, edge_fea, src, dst, inv_sqrt_deg, W, b, residual, act):
            m = h[src] + edge_fea
            agg = jax.ops.segment_sum(m, dst, num_segments=h.shape[0])
            rst = agg @ W + b
            rst = rst * inv_sqrt_deg
            if residual:
                rst = rst + h
            if act:
                rst = jax.nn.relu(rst)
            return rst
        N = node_fea.shape[0]
        deg_in = jax.ops.segment_sum(jnp.ones_like(dst, dtype=node_fea.dtype), dst, num_segments=N)
        inv_sqrt_deg = jnp.clip(deg_in, 1.0) ** (-0.5)
        inv_sqrt_deg = inv_sqrt_deg[:, None]
        h = _graph_conv(node_fea, edge_fea, src, dst, inv_sqrt_deg, W0, b0, True, True)
        h = _graph_conv(h, edge_fea, src, dst, inv_sqrt_deg, W1, b1, True, True)
        h = _graph_conv(h, edge_fea, src, dst, inv_sqrt_deg, W2, b2, False, False)
        return h
    edge_index = jnp.stack([src, dst])
    h = jnp.maximum(_layernorm(x, axis=-1), 0.0)
    x = x + _L0_gnn_ref(h, edge_index, edge_type_8, L0_gnn_w1, L0_gnn_sw1, L0_gnn_b1, L0_gnn_w2, L0_gnn_sw2, L0_gnn_b2)
    h = jnp.maximum(_layernorm(x, axis=-1), 0.0)
    x = x + _L1_gnn_ref(h, edge_attr_128, src, dst, L1_gnn_W0, L1_gnn_b0, L1_gnn_W1, L1_gnn_b1, L1_gnn_W2, L1_gnn_b2)
    return x

_drawn_inputs = setup_inputs


def setup_inputs(seed=0):
    import zlib

    import numpy as np

    out = dict(_drawn_inputs(seed))
    spreads = {'L0_gnn_b1': (0.0, 0.1),
     'L0_gnn_b2': (0.0, 0.1),
     'L1_gnn_b0': (0.0, 0.8),
     'L1_gnn_b1': (0.0, 0.8),
     'L1_gnn_b2': (0.0, 0.1)}
    factors = {'L1_gnn_W0': 4.923, 'L1_gnn_W1': 4.399}
    for name, (base, spread) in spreads.items():
        noise = np.random.default_rng([zlib.crc32(name.encode()), seed]).standard_normal(out[name].shape)
        drawn = base * np.exp(spread * noise) if base else spread * noise
        out[name] = jnp.asarray(drawn.astype(out[name].dtype))
    for name, factor in factors.items():
        out[name] = (out[name] * factor).astype(out[name].dtype)
    return out
```

```python
from contextlib import ExitStack

import concourse.bass as bass
from concourse import mybir
from concourse.alu_op_type import AluOpType as ALU

ACT = mybir.ActivationFunctionType
F32 = mybir.dt.float32
I32 = mybir.dt.int32

P = 128
N = 50000
E = 25000
R = 8
TILES = 196
EP = TILES * P
U = 7
RING = 2 * U
TURNS = TILES // RING
DG = 4
DRING = 14
DGROUPS = 98
DTURNS = DGROUPS // DRING
NP = DGROUPS * DG * P
PAD_NODE = N
HALF = TILES // 2
SKIP = float(1 << 20)
EPS = 1e-5
assert TILES % RING == 0 and EP >= E and NP > N and DGROUPS % DRING == 0


def turns(eng, count, ring, step, drain):
    for j in range(ring):
        step(0, j)
    with eng.Fori(1, count) as it:
        for j in range(ring):
            step(it, j)
    for j in range(drain):
        step(count, j)


def tile_at(it, j, skew, ring, total):
    n = ring * it + (j - skew)
    if isinstance(n, int) and not 0 <= n < total:
        return None
    return n


def use_of(it, j, skew, ring, turn):
    return (turn // ring) * it + (j - skew) // ring


def wait_for(eng, sem, value):
    if isinstance(value, int) and value <= 0:
        return
    eng.wait_ge(sem, value)


def wait_apart(eng, sem, value):
    wait_for(eng, sem, value)
    eng.nop(nofuse=True)


class Program:
    def __init__(self, nc, ins, out):
        self.nc, self.ins, self.out = nc, ins, out
        dram = lambda name, shape, dt=F32: nc.dram_tensor(name, shape, dt, kind="Internal").ap()
        self.h1_table = dram("h1_table", [NP + EP, P])
        self.h2_table = dram("h2_table", [NP + EP, P])
        self.h3_table = dram("h3_table", [2 * EP, P])
        self.h4_table = dram("h4_table", [2 * EP, P])
        self.x_slots = dram("x_slots", [EP, P])
        self.x2_slots = dram("x2_slots", [EP, P])
        self.row_of_node = dram("row_of_node", [NP, 1], I32)
        self.dst_f = dram("dst_f", [EP + 1])
        self.half_f = dram("half_f", [EP])
        self.count_f = dram("count_f", [EP])

    def free(self, sems):
        self.nc.clear_and_free_semaphores(sems)
        self.nc.all_engine_barrier()

    def build(self):
        nc = self.nc
        with ExitStack() as ctx:
            def sb(name, shape, dt=F32):
                return ctx.enter_context(nc.sbuf_tensor(name, shape, dt))
            self.ident = sb("ident", [P, P])
            self.ones = sb("ones", [P, P])
            self.eps = sb("eps", [P, 1])
            self.sw1 = sb("sw1", [P, P])
            self.sw2 = sb("sw2", [P, P])
            self.w1 = sb("w1", [P, R, P])
            self.w2 = sb("w2", [P, R, P])
            self.gw = [sb(f"gw{i}", [P, P]) for i in range(3)]
            self.gb_row = sb("gb_row", [1, 3, P])
            self.b1 = sb("b1", [P, P])
            self.b2 = sb("b2", [P, P])
            self.gb = [sb(f"gb{i}", [P, P]) for i in range(3)]
            self.dst_col = sb("dst_col", [P, TILES])
            self.end_idx = sb("end_idx", [P, TILES], I32)
            self.ends_idx = sb("ends_idx", [P, TILES, 2], I32)
            self.slot_row = sb("slot_row", [P, TILES], I32)
            self.state_idx = sb("state_idx", [P, TILES], I32)
            self.local_idx = sb("local_idx", [P, TILES], I32)
            self.odd_col = sb("odd_col", [P, TILES])
            self.even_col = sb("even_col", [P, TILES])
            self.isd_col = sb("isd_col", [P, TILES])
            self.setup()
            self.dense_and_slots()
            self.dst_bc = sb("dst_bc", [P, EP + 1])
            self.relational(1)
            self.relational(2)
            self.conv(3)
            self.conv(4)
            self.conv(5)

    def setup(self):
        nc, ins = self.nc, self.ins
        with ExitStack() as ctx:
            def sb(name, shape, dt=F32):
                return ctx.enter_context(nc.sbuf_tensor(name, shape, dt))

            sems = []

            def sem(name):
                sems.append(nc.alloc_semaphore(name))
                return sems[-1]

            dst_r = sb("dst_r", [HALF, 2, P], I32)
            next_r = sb("next_r", [HALF, 2, P], I32)
            src_r = sb("src_r", [HALF, 2, P], I32)
            typ_r = sb("typ_r", [HALF, 2, P], I32)
            half_i = sb("half_i", [HALF, 2, P], I32)
            odd_i = sb("odd_i", [HALF, 2, P], I32)
            dst_rf = sb("dst_rf", [HALF, 2, P])
            next_rf = sb("next_rf", [HALF, 2, P])
            end_rf = sb("end_rf", [HALF, 2, P])
            inner = sb("inner", [HALF, 2, P])
            src_rf = sb("src_rf", [HALF, 2, P])
            half_rf = sb("half_rf", [HALF, 2, P])
            odd_rf = sb("odd_rf", [HALF, 2, P])
            count_rf = sb("count_rf", [HALF, 2, P])
            dst_q = sb("dst_q", [P, TILES], I32)
            prev_q = sb("prev_q", [P, TILES], I32)
            dst_qf = sb("dst_qf", [P, TILES])
            prev_qf = sb("prev_qf", [P, TILES])
            same_q = sb("same_q", [P, TILES])
            ones_q = sb("ones_q", [P, TILES])
            count_q = sb("count_q", [P, TILES])
            firsts = sb("firsts", [P, P])
            later = sb("later", [P, P])
            reach = sb("reach", [P, P])
            carried = sb("carried", [P, P])
            carry = sb("carry", [P, 1])
            in_first = sb("in_first", [P, TILES])
            count_all = sb("count_all", [P, TILES])
            least_one = sb("least_one", [P, TILES])
            root = sb("root", [P, TILES])
            front = sb("front", [1, 1])
            node_ids = sb("node_ids", [P, NP // P], I32)
            cols_ps = [ctx.enter_context(nc.psum_tensor(f"cols_ps{i}", [P, 512], F32)) for i in range(6)]

            edges_loaded, weights_loaded = sem("edges_loaded"), sem("weights_loaded")
            ident_set, ready_rows, cols_done = sem("ident_set"), sem("ready_rows"), sem("cols_done")
            dve = sem("setup_dve")
            firsts_set, firsts_done, reach_set, carry_done = (
                sem("firsts_set"), sem("firsts_done"), sem("reach_set"), sem("carry_done"))
            rows_stored, count_set, count_stored, count_loaded = (
                sem("rows_stored"), sem("count_set"), sem("count_stored"), sem("count_loaded"))
            count_cols, ids_set, later_set, ones_set = (
                sem("count_cols"), sem("ids_set"), sem("later_set"), sem("ones_set"))
            ids_stored = sem("ids_stored")
            least_set, root_set = sem("least_set"), sem("root_set")
            ctx.callback(self.free, sems)
            block = ctx.enter_context(nc.Block())

            def rows(a):
                return a.rearrange("(i q f) -> q i f", i=2, q=HALF)

            def bc(a):
                return a.rearrange("(a c) -> a c", a=1).broadcast_to([P, P])

            dstp = ins["dst"]

            @block.sync
            def _(sp):
                for to, of in ((dst_r, rows(dstp[1:EP + 1])), (next_r, rows(dstp[2:EP + 2])),
                               (src_r, rows(ins["src"])), (typ_r, rows(ins["typ"]))):
                    sp.dma_start(to[:, :, :], of).then_inc(edges_loaded, 16)
                sp.dma_start(dst_q[:, :], dstp[1:EP + 1].rearrange("(p j) -> p j", p=P)).then_inc(edges_loaded, 16)
                sp.dma_start(prev_q[:, :], dstp[0:EP].rearrange("(p j) -> p j", p=P)).then_inc(edges_loaded, 16)
                sp.wait_ge(ready_rows, 1)
                sp.dma_start(self.dst_f[1:EP + 1].rearrange("(i q f) -> q i f", i=2, q=HALF),
                             dst_rf[:, :, :]).then_inc(rows_stored, 16)
                sp.dma_start(self.dst_f[0:1].rearrange("(a c) -> a c", a=1), front[:, :]).then_inc(rows_stored, 16)
                sp.dma_start(rows(self.half_f), half_rf[:, :, :]).then_inc(rows_stored, 16)
                sp.wait_ge(count_set, 1)
                sp.dma_start(self.count_f.rearrange("(p j) -> p j", p=P), count_all[:, :]).then_inc(count_stored, 16)
                sp.wait_ge(count_stored, 16)
                sp.dma_start(count_rf[:, :, :], rows(self.count_f)).then_inc(count_loaded, 16)
                sp.wait_ge(rows_stored, 3 * 16)
                sp.wait_ge(weights_loaded, 15 * 16)

            @block.scalar
            def _(act):
                for to, of in ((self.sw1, ins["sw1"]), (self.sw2, ins["sw2"]), (self.gw[0], ins["W0"]),
                               (self.gw[1], ins["W1"]), (self.gw[2], ins["W2"])):
                    act.dma_start(to[:, :], of).then_inc(weights_loaded, 16)
                act.dma_start(self.w1[:, :, :], ins["w1"].rearrange("r c o -> c r o")).then_inc(weights_loaded, 16)
                act.dma_start(self.w2[:, :, :], ins["w2"].rearrange("r c o -> c r o")).then_inc(weights_loaded, 16)
                for to, of in ((self.b1, ins["b1"]), (self.b2, ins["b2"]), (self.gb[0], ins["g0"]),
                               (self.gb[1], ins["g1"]), (self.gb[2], ins["g2"])):
                    act.dma_start(to[:, :], bc(of)).then_inc(weights_loaded, 16)
                for i in range(3):
                    act.dma_start(self.gb_row[0:1, i, :], ins[f"g{i}"].rearrange("(a c) -> a c", a=1)).then_inc(weights_loaded, 16)
                act.wait_ge(least_set, 1)
                nc.scalar.activation(root[:, :], least_one[:, :], ACT.Sqrt).then_inc(root_set, 1)

            @block.gpsimd
            def _(pool):
                pool.memset(self.ident[:, :], 0.0).then_inc(ident_set, 1)
                pool.memset(self.eps[:, :], EPS)
                pool.memset(self.ones[:, :], 1.0).then_inc(ones_set, 1)
                pool.wait_ge(ident_set, 1)
                pool.affine_select(out=self.ident[:, :], in_=self.ident[:, :], compare_op=ALU.not_equal, fill=1.0,
                                   base=0, pattern=[[-1, P]], channel_multiplier=1).then_inc(ident_set, 1)
                pool.wait_ge(ones_set, 1)
                pool.affine_select(out=later[:, :], in_=self.ones[:, :], compare_op=ALU.is_gt, fill=0.0,
                                   base=0, pattern=[[1, P]], channel_multiplier=-1).then_inc(later_set, 1)
                pool.iota(self.slot_row[:, :].rearrange("p (g k) -> p g k", k=U), pattern=[[P * U, TILES // U], [1, U]],
                          base=NP, channel_multiplier=U)
                pool.iota(node_ids[:, :], pattern=[[1, NP // P]], base=0, channel_multiplier=NP // P).then_inc(ids_set, 1)
                pool.wait_ge(ids_set, 1)
                pool.dma_start(self.row_of_node.rearrange("(p j) a -> p (j a)", p=P), node_ids[:, :]).then_inc(ids_stored, 16)
                pool.wait_ge(ids_stored, 16)

            @block.vector
            def _(v):
                done = [0]

                def link(ins_):
                    done[0] += 1
                    ins_.then_inc(dve, 1)
                    v.wait_ge(dve, done[0])

                v.wait_ge(edges_loaded, 6 * 16)
                nc.vector.memset(front[:, :], -1.0)
                nc.vector.memset(ones_q[:, :], 1.0)
                nc.vector.tensor_scalar(odd_i[:, :, :], typ_r[:, :, :], 1, None, ALU.bitwise_and)
                nc.vector.tensor_scalar(half_i[:, :, :], typ_r[:, :, :], 1, None, ALU.arith_shift_right)
                nc.vector.tensor_copy(dst_rf[:, :, :], dst_r[:, :, :])
                nc.vector.tensor_copy(next_rf[:, :, :], next_r[:, :, :])
                nc.vector.tensor_copy(src_rf[:, :, :], src_r[:, :, :])
                nc.vector.tensor_copy(dst_qf[:, :], dst_q[:, :])
                link(nc.vector.tensor_copy(prev_qf[:, :], prev_q[:, :]))
                nc.vector.tensor_copy(odd_rf[:, :, :], odd_i[:, :, :])
                nc.vector.tensor_copy(half_rf[:, :, :], half_i[:, :, :])
                nc.vector.tensor_tensor(inner[:, :, :], dst_rf[:, :, :], next_rf[:, :, :], ALU.is_equal)
                nc.vector.tensor_copy(firsts[:, :], dst_qf[:, 0:1].broadcast_to([P, P])).then_inc(firsts_set, 1)
                link(nc.vector.tensor_tensor(same_q[:, :], dst_qf[:, :], prev_qf[:, :], ALU.is_equal))
                nc.vector.scalar_tensor_tensor(out=end_rf[:, :, :], in0=inner[:, :, :], scalar=SKIP, in1=dst_rf[:, :, :],
                                               op0=ALU.mult, op1=ALU.add).then_inc(ready_rows, 1)
                link(nc.vector.tensor_tensor_scan(count_q[:, :], same_q[:, :], ones_q[:, :], 0.0, ALU.mult, ALU.add))
                v.wait_ge(firsts_done, 1)
                v.wait_ge(later_set, 1)
                link(nc.vector.scalar_tensor_tensor(out=reach[:, :], in0=cols_ps[5][:, 0:P], scalar=dst_qf[:, TILES - 1:TILES],
                                                    in1=later[:, :], op0=ALU.is_equal, op1=ALU.mult))
                nc.vector.tensor_copy(carried[:, :], count_q[:, TILES - 1:TILES].broadcast_to([P, P])).then_inc(reach_set, 1)
                nc.vector.tensor_scalar(in_first[:, :], dst_qf[:, :], dst_qf[:, 0:1], None, ALU.is_equal)
                v.wait_ge(carry_done, 1)
                link(nc.vector.tensor_copy(carry[:, :], cols_ps[4][:, 256:257]))
                nc.vector.scalar_tensor_tensor(out=count_all[:, :], in0=in_first[:, :], scalar=carry[:, :], in1=count_q[:, :],
                                               op0=ALU.mult, op1=ALU.add).then_inc(count_set, 1)
                v.wait_ge(cols_done, 4)
                nc.vector.tensor_copy(self.dst_col[:, :], cols_ps[0][:, 0:TILES])
                nc.vector.tensor_copy(self.ends_idx[:, :, 1], cols_ps[0][:, 0:TILES])
                nc.vector.tensor_copy(self.end_idx[:, :], cols_ps[1][:, 0:TILES])
                nc.vector.tensor_copy(self.ends_idx[:, :, 0], cols_ps[2][:, 0:TILES])
                nc.vector.tensor_copy(self.odd_col[:, :], cols_ps[3][:, 0:TILES])
                nc.vector.tensor_scalar(self.even_col[:, :], cols_ps[3][:, 0:TILES], -1.0, 1.0, ALU.mult, ALU.add)
                v.wait_ge(count_cols, 1)
                nc.vector.tensor_scalar(least_one[:, :], cols_ps[4][:, 0:TILES], 1.0, None, ALU.max).then_inc(least_set, 1)
                v.wait_ge(root_set, 1)
                nc.vector.reciprocal(self.isd_col[:, :], root[:, :])
                v.wait_ge(weights_loaded, 15 * 16)
                v.wait_ge(ident_set, 2)
                nc.vector.tensor_tensor(self.sw1[:, :], self.sw1[:, :], self.ident[:, :], ALU.add)

            @block.tensor
            def _(pe):
                pe.wait_ge(ident_set, 2)
                pe.wait_ge(firsts_set, 1)
                nc.tensor.transpose(cols_ps[5][:, 0:P], firsts[:, :], self.ident[:, :]).then_inc(firsts_done, 1)
                pe.wait_ge(ready_rows, 1)
                for n, rows_f in enumerate((dst_rf, end_rf, src_rf, odd_rf)):
                    for i in range(2):
                        last = nc.tensor.transpose(cols_ps[n][:, i * HALF:(i + 1) * HALF], rows_f[:, i, :],
                                                   self.ident[0:HALF, 0:HALF])
                    last.then_inc(cols_done, 1)
                pe.wait_ge(reach_set, 1)
                nc.tensor.matmul(cols_ps[4][:, 256:256 + P], reach[:, :], carried[:, :], start=True, stop=True).then_inc(carry_done, 1)
                pe.wait_ge(count_loaded, 16)
                pe.wait_ge(count_set, 1)
                for i in range(2):
                    last = nc.tensor.transpose(cols_ps[4][:, i * HALF:(i + 1) * HALF], count_rf[:, i, :],
                                               self.ident[0:HALF, 0:HALF])
                last.then_inc(count_cols, 1)

    def dense_and_slots(self):
        nc = self.nc
        with ExitStack() as ctx:
            def sb(name, shape, dt=F32):
                return ctx.enter_context(nc.sbuf_tensor(name, shape, dt))

            sems = []

            def sem(name):
                sems.append(nc.alloc_semaphore(name))
                return sems[-1]

            W = DG * P
            x = sb("x_ring", [P, DRING, DG, P])
            stats = sb("stats", [P, 2, DG, 6])
            mv = sb("mv", [P, 2, DG, 2])
            std = sb("std", [P, 2, DG])
            rstd = sb("rstd", [P, 2, DG])
            stats2 = sb("stats2", [P, 2, DG, 6])
            mv2 = sb("mv2", [P, 2, DG, 2])
            std2 = sb("std2", [P, 2, DG])
            rstd2 = sb("rstd2", [P, 2, DG])
            h0 = sb("h0_ring", [P, 7, W])
            h0t = sb("h0t_ring", [P, 2, W])
            h1 = sb("h1_ring", [P, 7, W])
            h1t = sb("h1t_ring", [P, 2, W])
            x2 = sb("x2_ring", [P, 2, DG, P])
            h2 = sb("h2_ring", [P, 7, W])
            res = sb("res_ring", [P, 7, W])
            t1 = [ctx.enter_context(nc.psum_tensor(f"t1_ps{i}", [P, W], F32)) for i in range(2)]
            p1 = [ctx.enter_context(nc.psum_tensor(f"p1_ps{i}", [P, W], F32)) for i in range(2)]
            t2 = [ctx.enter_context(nc.psum_tensor(f"t2_ps{i}", [P, W], F32)) for i in range(2)]
            p2 = [ctx.enter_context(nc.psum_tensor(f"p2_ps{i}", [P, W], F32)) for i in range(2)]
            id_now = sb("id_now", [P, 2, U], I32)
            row_now = sb("row_now", [P, 2, U], I32)
            row_got = sb("row_got", [P, 2, U], I32)
            is_slot = sb("is_slot", [P, TILES])
            own_f = sb("own_f", [P, TILES])
            slot_f = sb("slot_f", [P, TILES])
            step_f = sb("step_f", [P, TILES])
            pick_f = sb("pick_f", [P, TILES])

            x_loaded = [sem(f"x_loaded{i}") for i in range(DRING)]
            stats_set, mv_set, std_set, rstd_set, norm_set, relu_set, std2_set = (
                sem("d_stats"), sem("d_mv"), sem("d_std"), sem("d_rstd"), sem("d_norm"), sem("d_relu"), sem("d_std2"))
            t1_done, h0t_set, p1_done, h1_set, t2_done, h1t_set, p2_done = (
                sem("d_t1"), sem("d_h0t"), sem("d_p1"), sem("d_h1"), sem("d_t2"), sem("d_h1t"), sem("d_p2"))
            xb_set, x2_set, stats2_set, mv2_set, rstd2_set, norm2_set, relu2_set, res_set = (
                sem("d_xb"), sem("d_x2"), sem("d_stats2"), sem("d_mv2"), sem("d_rstd2"), sem("d_norm2"),
                sem("d_relu2"), sem("d_res"))
            h1_stored = [sem(f"h1_stored{i}") for i in range(7)]
            h2_stored = [sem(f"h2_stored{i}") for i in range(7)]
            res_stored = [sem(f"res_stored{i}") for i in range(7)]
            staged = sem("staged")
            slots_put = [sem(f"slots_put{i}") for i in range(2)]
            slots_got = [sem(f"slots_got{i}") for i in range(2)]
            rows_copied, state_rows, pick = sem("rows_copied"), sem("state_rows"), sem("pick")
            ctx.callback(self.free, sems)
            block = ctx.enter_context(nc.Block())

            D = DGROUPS
            LN, NORM, RELU, T1, H0T, P1, H1, T2, H1T, P2, LN2, NORM2, STORE2 = 2, 3, 4, 5, 6, 7, 8, 9, 10, 11, 12, 13, 14
            DRAIN = STORE2 + 1
            at = lambda it, j, skew: tile_at(it, j, skew, DRING, D)
            used = lambda it, j, skew, ring: use_of(it, j, skew, ring, DRING)

            def node_rows(table, g):
                return table[bass.ds(g * (DG * P), DG * P), :].rearrange("(p k) c -> p (k c)", k=DG)

            @block.sync
            def _(sp):
                def step(it, j):
                    g = at(it, j, 0)
                    if g is not None:
                        wait_apart(sp, x2_set, g - DRING + 1)
                        sp.dma_start(x[:, j % DRING, :, :].rearrange("p k c -> p (k c)"), node_rows(self.ins["x"], g)).then_inc(x_loaded[j % DRING], 16)
                    for skew, ready, ring, stored, table in (
                            (T2, h1_set, h1, h1_stored, self.h1_table),
                            (NORM2, res_set, res, res_stored, self.out),
                            (STORE2, relu2_set, h2, h2_stored, self.h2_table)):
                        g = at(it, j, skew)
                        if g is None:
                            continue
                        s = (j - skew) % 7
                        wait_apart(sp, ready, g + 1)
                        sp.dma_start(node_rows(table, g), ring[:, s, :]).then_inc(stored[s], 16)

                turns(sp, DTURNS, DRING, step, DRAIN)
                for stored in (h1_stored, h2_stored, res_stored):
                    for s in range(7):
                        sp.wait_ge(stored[s], 16 * D // 7)

            @block.vector
            def _(v):
                def step(it, j):
                    g = at(it, j, NORM)
                    if g is not None:
                        b = (j - NORM) % 2
                        wait_for(v, std_set, g + 1)
                        nc.vector.reciprocal(rstd[:, b, :], std[:, b, :]).then_inc(rstd_set, 1)
                    q = at(it, j, NORM2)
                    if q is not None:
                        b2 = (j - NORM2) % 2
                        wait_for(v, std2_set, q + 1)
                        nc.vector.reciprocal(rstd2[:, b2, :], std2[:, b2, :]).then_inc(rstd2_set, 1)
                    h = at(it, j, H1)
                    if h is not None:
                        r1 = (j - H1) % 7
                        wait_for(v, p1_done, h + 1)
                        wait_for(v, h1_stored[r1], 16 * used(it, j, H1, 7))
                        wait_for(v, t2_done, h - 6)
                        nc.vector.scalar_tensor_tensor(
                            out=h1[:, r1, :].rearrange("p (k c) -> p k c", k=DG),
                            in0=p1[(j - H1) % 2][:, :].rearrange("p (k c) -> p k c", k=DG),
                            scalar=0.0, in1=self.b1[:, None, :].broadcast_to([P, DG, P]), op0=ALU.max, op1=ALU.add).then_inc(h1_set, 1)
                    if g is not None:
                        s, r = (j - NORM) % DRING, (j - NORM) % 7
                        wait_for(v, rstd_set, g + 1)
                        wait_for(v, t1_done, g - 6)
                        for k in range(DG):
                            last = nc.vector.tensor_scalar(h0[:, r, k * P:(k + 1) * P], x[:, s, k, :], mv[:, b, k, 0:1],
                                                           rstd[:, b, k:k + 1], ALU.subtract, ALU.mult)
                        last.then_inc(norm_set, 1)
                        wait_for(v, norm_set, g + 1)
                        nc.vector.tensor_tensor(x[:, s, :, :], x[:, s, :, :],
                                                self.b2[:, None, :].broadcast_to([P, DG, P]), ALU.add).then_inc(xb_set, 1)
                    if q is not None:
                        r2 = (j - NORM2) % 7
                        wait_for(v, rstd2_set, q + 1)
                        wait_for(v, h2_stored[r2], 16 * used(it, j, NORM2, 7))
                        for k in range(DG):
                            last = nc.vector.tensor_scalar(h2[:, r2, k * P:(k + 1) * P], x2[:, b2, k, :], mv2[:, b2, k, 0:1],
                                                           rstd2[:, b2, k:k + 1], ALU.subtract, ALU.mult)
                        last.then_inc(norm2_set, 1)
                    q = at(it, j, LN2)
                    if q is not None:
                        s2, r2 = (j - LN2) % 2, (j - LN2) % 7
                        wait_for(v, p2_done, q + 1)
                        wait_for(v, xb_set, q + 1)
                        nc.vector.tensor_tensor(x2[:, s2, :, :], p2[s2][:, :].rearrange("p (k c) -> p k c", k=DG),
                                                x[:, (j - LN2) % DRING, :, :], ALU.add).then_inc(x2_set, 1)
                    g = at(it, j, LN)
                    if g is not None:
                        s, b = (j - LN) % DRING, (j - LN) % 2
                        wait_for(v, x_loaded[s], 16 * used(it, j, LN, DRING) + 16)
                        for k in range(DG):
                            last = nc.vector.bn_stats(stats[:, b, k, :], x[:, s, k, :])
                        last.then_inc(stats_set, 1)
                    if q is not None:
                        wait_for(v, x2_set, q + 1)
                        for k in range(DG):
                            last = nc.vector.bn_stats(stats2[:, s2, k, :], x2[:, s2, k, :])
                        last.then_inc(stats2_set, 1)
                    if g is not None:
                        wait_apart(v, stats_set, g + 1)
                        for k in range(DG):
                            last = nc.vector.bn_aggr(mv[:, b, k, :], stats[:, b, k, :])
                        last.then_inc(mv_set, 1)
                    if q is not None:
                        wait_for(v, res_stored[r2], 16 * used(it, j, LN2, 7))
                        nc.vector.tensor_tensor(res[:, r2, :].rearrange("p (k c) -> p k c", k=DG), x2[:, s2, :, :],
                                                self.gb[2][:, None, :].broadcast_to([P, DG, P]), ALU.add).then_inc(res_set, 1)
                        wait_apart(v, stats2_set, q + 1)
                        for k in range(DG):
                            last = nc.vector.bn_aggr(mv2[:, s2, k, :], stats2[:, s2, k, :])
                        last.then_inc(mv2_set, 1)

                turns(v, DTURNS, DRING, step, DRAIN)
                v.wait_ge(rows_copied, TILES // U)
                nc.vector.tensor_scalar(is_slot[:, :], self.state_idx[:, :], float(NP), None, ALU.is_ge)
                nc.vector.tensor_scalar(own_f[:, :], self.slot_row[:, :], -float(NP), None, ALU.add)
                nc.vector.tensor_scalar(slot_f[:, :], self.state_idx[:, :], float(EP - NP), None, ALU.add).then_inc(pick, 1)
                v.wait_ge(pick, 1)
                nc.vector.tensor_tensor(step_f[:, :], slot_f[:, :], own_f[:, :], ALU.subtract).then_inc(pick, 1)
                v.wait_ge(pick, 2)
                nc.vector.tensor_tensor(pick_f[:, :], step_f[:, :], is_slot[:, :], ALU.mult).then_inc(pick, 1)
                v.wait_ge(pick, 3)
                nc.vector.tensor_tensor(self.local_idx[:, :], pick_f[:, :], own_f[:, :], ALU.add).then_inc(pick, 1)

            @block.scalar
            def _(act):
                def step(it, j):
                    g = at(it, j, RELU)
                    if g is not None:
                        s = (j - RELU) % 7
                        wait_for(act, norm_set, g + 1)
                        nc.scalar.activation(h0[:, s, :], h0[:, s, :], ACT.Relu).then_inc(relu_set, 1)
                    g = at(it, j, H0T)
                    if g is not None:
                        s = (j - H0T) % 2
                        wait_for(act, t1_done, g + 1)
                        wait_for(act, p1_done, g - 1)
                        nc.scalar.activation(h0t[:, s, :], t1[s][:, :], ACT.Copy).then_inc(h0t_set, 1)
                    g = at(it, j, H1T)
                    if g is not None:
                        s = (j - H1T) % 2
                        wait_for(act, t2_done, g + 1)
                        wait_for(act, p2_done, g - 1)
                        nc.scalar.activation(h1t[:, s, :], t2[s][:, :], ACT.Copy).then_inc(h1t_set, 1)
                    for skew, ready, of, to, set_ in ((LN, mv_set, mv, std, std_set), (LN2, mv2_set, mv2, std2, std2_set)):
                        g = at(it, j, skew)
                        if g is not None:
                            s = (j - skew) % 2
                            wait_for(act, ready, g + 1)
                            nc.scalar.activation(to[:, s, :], of[:, s, :, 1], ACT.Sqrt, bias=self.eps[:, :]).then_inc(set_, 1)
                    g = at(it, j, NORM2)
                    if g is not None:
                        s = (j - NORM2) % 7
                        wait_for(act, norm2_set, g + 1)
                        nc.scalar.activation(h2[:, s, :], h2[:, s, :], ACT.Relu).then_inc(relu2_set, 1)

                turns(act, DTURNS, DRING, step, DRAIN)

            @block.tensor
            def _(pe):
                def step(it, j):
                    g = at(it, j, T1)
                    if g is not None:
                        s = (j - T1) % 2
                        wait_for(pe, relu_set, g + 1)
                        wait_for(pe, h0t_set, g - 1)
                        for k in range(DG):
                            last = nc.tensor.transpose(t1[s][:, k * P:(k + 1) * P], h0[:, (j - T1) % 7, k * P:(k + 1) * P], self.ident[:, :])
                        last.then_inc(t1_done, 1)
                    g = at(it, j, P1)
                    if g is not None:
                        s = (j - P1) % 2
                        wait_for(pe, h0t_set, g + 1)
                        wait_for(pe, h1_set, g - 1)
                        for k in range(DG):
                            last = nc.tensor.matmul(p1[s][:, k * P:(k + 1) * P], h0t[:, s, k * P:(k + 1) * P], self.sw1[:, :],
                                                    start=True, stop=True)
                        last.then_inc(p1_done, 1)
                    g = at(it, j, T2)
                    if g is not None:
                        s = (j - T2) % 2
                        wait_for(pe, h1_set, g + 1)
                        wait_for(pe, h1t_set, g - 1)
                        for k in range(DG):
                            last = nc.tensor.transpose(t2[s][:, k * P:(k + 1) * P], h1[:, (j - T2) % 7, k * P:(k + 1) * P], self.ident[:, :])
                        last.then_inc(t2_done, 1)
                    g = at(it, j, P2)
                    if g is not None:
                        s = (j - P2) % 2
                        wait_for(pe, h1t_set, g + 1)
                        wait_for(pe, x2_set, g - 1)
                        for k in range(DG):
                            last = nc.tensor.matmul(p2[s][:, k * P:(k + 1) * P], h1t[:, s, k * P:(k + 1) * P], self.sw2[:, :],
                                                    start=True, stop=True)
                        last.then_inc(p2_done, 1)

                turns(pe, DTURNS, DRING, step, DRAIN)

            @block.gpsimd
            def _(pool):
                G = TILES // U

                def put(it, h):
                    g = 2 * it + h
                    wait_for(pool, slots_put[h], 16 * U * it)
                    pool.tensor_copy(id_now[:, h, :], self.end_idx[:, bass.ds(g * U, U)])
                    pool.tensor_copy(row_now[:, h, :], self.slot_row[:, bass.ds(g * U, U)]).then_inc(staged, 1)
                    pool.wait_ge(staged, g + 1)
                    pool.nop(nofuse=True)
                    for k in range(U):
                        pool.indirect_dma_start(self.row_of_node[:, :], bass.IndirectOffsetOnAxis(ap=id_now[:, h, k:k + 1], axis=0),
                                                row_now[:, h, k:k + 1], None, bounds_check=NP - 1, oob_is_err=False).then_inc(slots_put[h], 16)

                def keep(it, h):
                    g = 2 * it + h
                    wait_for(pool, slots_got[h], 16 * U * it + 16 * U)
                    pool.tensor_copy(self.state_idx[:, bass.ds(g * U, U)], row_got[:, h, :]).then_inc(rows_copied, 1)

                def get(it, h):
                    g = 2 * it + h
                    wait_for(pool, rows_copied, g - 1)
                    pool.tensor_copy(id_now[:, h, :], self.ends_idx[:, bass.ds(g * U, U), 0]).then_inc(staged, 1)
                    pool.wait_ge(staged, G + g + 1)
                    pool.nop(nofuse=True)
                    for k in range(U):
                        pool.indirect_dma_start(row_got[:, h, k:k + 1], None, self.row_of_node[:, :],
                                                bass.IndirectOffsetOnAxis(ap=id_now[:, h, k:k + 1], axis=0)).then_inc(slots_got[h], 16)

                put(0, 0)
                put(0, 1)
                with pool.Fori(1, TURNS) as it:
                    put(it, 0)
                    put(it, 1)
                for h in range(2):
                    pool.wait_ge(slots_put[h], 16 * U * TURNS)
                get(0, 0)
                get(0, 1)
                with pool.Fori(1, TURNS) as it:
                    keep(it - 1, 0)
                    get(it, 0)
                    keep(it - 1, 1)
                    get(it, 1)
                keep(TURNS - 1, 0)
                keep(TURNS - 1, 1)

    def relational(self, layer):
        nc, first = self.nc, layer == 1
        with ExitStack() as ctx:
            def sb(name, shape, dt=F32):
                return ctx.enter_context(nc.sbuf_tensor(f"r{layer}_{name}", shape, dt))

            sems = []

            def sem(name):
                sems.append(nc.alloc_semaphore(f"r{layer}_{name}"))
                return sems[-1]

            src_x = sb("src_x", [P, RING, P])
            dst_x = sb("dst_x", [P, RING, P])
            x_res = None if first else sb("x_res", [P, RING, P])
            half_bc = sb("half_bc", [P, RING, P])
            stats = sb("stats", [P, 2, 2, 6])
            mv = sb("mv", [P, 2, 2, 2])
            std = sb("std", [P, 2, 2])
            rstd = sb("rstd", [P, 2, 2])
            h = sb("h", [P, 7, 2, P]) if first else None
            ht_masked = sb("ht_masked", [P, 2, R // 2, P])
            ht_dst = sb("ht_dst", [P, 7, P])
            odd = sb("odd", [P, 2, P])
            msg = sb("msg", [P, 2, P])
            same = sb("same", [P, 2, P])
            joins = sb("joins", [P, 7, P])
            agg_t = sb("agg_t", [P, 2, P])
            out_x = sb("out_x", [P, RING, P])
            out_h = None if first else sb("out_h", [P, RING, P])
            idx_now = sb("idx_now", [P, RING, 2], I32)
            t_ps = [ctx.enter_context(nc.psum_tensor(f"r{layer}_t_ps{i}", [P, 512], F32)) for i in range(2)]
            y_ps = [ctx.enter_context(nc.psum_tensor(f"r{layer}_y_ps{i}", [P, 512], F32)) for i in range(2)]
            a_ps = [ctx.enter_context(nc.psum_tensor(f"r{layer}_a_ps{i}", [P, 512], F32)) for i in range(2)]
            p_ps = [ctx.enter_context(nc.psum_tensor(f"r{layer}_p_ps{i}", [P, 512], F32)) for i in range(2)]

            gathered = [sem(f"gathered{i}") for i in range(RING)]
            loaded = [sem(f"loaded{i}") for i in range(2)]
            res_loaded = [sem(f"res_loaded{i}") for i in range(2)]
            half_loaded = [sem(f"half_loaded{i}") for i in range(2)]
            x_stored = [sem(f"x_stored{i}") for i in range(2)]
            h_stored = [sem(f"h_stored{i}") for i in range(2)]
            dst_loaded, staged = sem("dst_loaded"), sem("staged")
            stats_set, mv_set, std_set, rstd_set, norm_set, relu_set = (
                sem("stats"), sem("mv"), sem("std"), sem("rstd"), sem("norm"), sem("relu"))
            t_done, masked_set, dst_t_set, y_done, odd_set, msg_set, masks_set = (
                sem("t_done"), sem("masked"), sem("dst_t"), sem("y_done"), sem("odd"), sem("msg"), sem("masks"))
            agg_done, agg_set, p_done, out_set, xb_set, out_relu = (
                sem("agg_done"), sem("agg_set"), sem("p_done"), sem("out"), sem("xb"), sem("out_relu"))
            ctx.callback(self.free, sems)
            block = ctx.enter_context(nc.Block())

            w = self.w1 if first else self.w2
            sw = self.sw1 if first else self.sw2
            STATS, NORM, RELU, T, MASK, Y, PICK, AGG, CARRY, SELF, OUT = (
                (4, 5, 6, 7, 8, 9, 10, 11, 12, 13, 14) if first else (12, 13, 14, 5, 6, 7, 8, 9, 10, 11, 12))
            TAIL = 14
            DRAIN = TAIL + 1
            used = lambda it, j, skew, ring: use_of(it, j, skew, ring, RING)
            at = lambda it, j, skew: tile_at(it, j, skew, RING, TILES)

            def half_of(j):
                return (j % RING) // U

            def slot_rows(table, g):
                return table[bass.ds(g * (U * P), U * P), :].rearrange("(p k) c -> p (k c)", k=U)

            def slots(t, hf):
                return t[:, hf * U:(hf + 1) * U, :].rearrange("p k c -> p (k c)")

            h_out = (self.h1_table if first else self.h2_table)[NP:NP + EP, :]
            h1_slots = self.h1_table[NP:NP + EP, :]

            PARTS = 2 if first else 1
            GOT = (2 if first else 1) * 16

            @block.gpsimd
            def _(pool):
                table = self.ins["x"] if first else self.h1_table

                def step(it, j):
                    n = at(it, j, 0)
                    if n is None:
                        return
                    wait_for(pool, staged, n + 1)
                    pool.nop(nofuse=True)
                    pool.indirect_dma_start(src_x[:, j, :], None, table[:, :],
                                            bass.IndirectOffsetOnAxis(ap=idx_now[:, j, 0:1], axis=0)).then_inc(gathered[j], 16)
                    if first:
                        pool.indirect_dma_start(dst_x[:, j, :], None, table[:, :],
                                                bass.IndirectOffsetOnAxis(ap=idx_now[:, j, 1:2], axis=0)).then_inc(gathered[j], 16)

                turns(pool, TURNS, RING, step, 0)

            @block.sync
            def _(sp):
                if first:
                    sp.dma_start(self.dst_bc[:, :], self.dst_f.rearrange("(a e) -> a e", a=1).broadcast_to([P, EP + 1])).then_inc(dst_loaded, 16)

                def load(it, hf):
                    g = 2 * it + hf
                    if not first:
                        wait_apart(sp, t_done, U * g - U)
                        sp.dma_start(slots(dst_x, hf), slot_rows(h1_slots, g)).then_inc(loaded[hf], 16)
                    wait_apart(sp, masked_set, U * g - U)
                    sp.dma_start(slots(half_bc, hf), self.half_f[bass.ds(g * (U * P), U * P)].rearrange("(a e) -> a e", a=1)
                                 .broadcast_to([P, U * P])).then_inc(half_loaded[hf], 16)
                    if first:
                        for k in range(hf * U, hf * U + U):
                            wait_apart(sp, gathered[k], GOT * it + GOT)
                        sp.dma_start(slot_rows(self.x_slots, g), slots(dst_x, hf)).then_inc(x_stored[hf], 16)
                    else:
                        wait_apart(sp, out_set, U * g - U)
                        sp.dma_start(slots(x_res, hf), slot_rows(self.x_slots, g)).then_inc(res_loaded[hf], 16)

                def store(it, hf):
                    g = 2 * it + hf
                    wait_apart(sp, out_set, U * g + U)
                    if first:
                        sp.dma_start(slot_rows(h_out, g), slots(out_x, hf)).then_inc(h_stored[hf], 16)
                    else:
                        sp.dma_start(slot_rows(self.x2_slots, g), slots(out_x, hf)).then_inc(x_stored[hf], 16)
                        wait_apart(sp, out_relu, U * g + U)
                        sp.dma_start(slot_rows(h_out, g), slots(out_h, hf)).then_inc(h_stored[hf], 16)

                load(0, 0)
                load(0, 1)
                with sp.Fori(1, TURNS) as it:
                    load(it, 0)
                    store(it - 1, 0)
                    load(it, 1)
                    store(it - 1, 1)
                store(TURNS - 1, 0)
                store(TURNS - 1, 1)
                for hf in range(2):
                    sp.wait_ge(x_stored[hf], 16 * TURNS)
                    sp.wait_ge(h_stored[hf], 16 * TURNS)

            @block.vector
            def _(v):
                def step(it, j):
                    k = at(it, j, NORM)
                    if k is not None:
                        kb, kc = (j - NORM) % 2, (j - NORM) % RING
                        wait_for(v, std_set, k + 1)
                        nc.vector.reciprocal(rstd[:, kb, 0:PARTS], std[:, kb, 0:PARTS]).then_inc(rstd_set, 1)
                    m = at(it, j, STATS) if first else None
                    if m is not None:
                        b, c = (j - STATS) % 2, (j - STATS) % RING
                        wait_for(v, gathered[c], GOT * used(it, j, STATS, RING) + GOT)
                        nc.vector.bn_stats(stats[:, b, 0, :], src_x[:, c, :])
                        nc.vector.bn_stats(stats[:, b, 1, :], dst_x[:, c, :]).then_inc(stats_set, 1)
                    n = at(it, j, MASK)
                    if n is not None:
                        s, r = (j - MASK) % 2, (j - MASK) % RING
                        wait_for(v, t_done, n + 1)
                        wait_for(v, y_done, n - 1)
                        wait_for(v, half_loaded[r // U], 16 * used(it, j, MASK, RING) + 16)
                        for q in range(R // 2):
                            last = nc.vector.scalar_tensor_tensor(out=ht_masked[:, s, q, :], in0=half_bc[:, r, :], scalar=float(q),
                                                                  in1=t_ps[s][:, 0:P], op0=ALU.is_equal, op1=ALU.mult)
                        last.then_inc(masked_set, 1)
                    if m is not None:
                        wait_apart(v, stats_set, m + 1)
                        nc.vector.bn_aggr(mv[:, b, 0, :], stats[:, b, 0, :])
                        nc.vector.bn_aggr(mv[:, b, 1, :], stats[:, b, 1, :]).then_inc(mv_set, 1)
                    n = at(it, j, PICK)
                    if n is not None:
                        s = (j - PICK) % 2
                        wait_for(v, agg_done, n - 1)
                        if first and isinstance(n, int) and n == 0:
                            v.wait_ge(dst_loaded, 16)
                        nc.vector.tensor_scalar(same[:, s, :], self.dst_bc[:, bass.ds(n * P + 1, P)], self.dst_col[:, bass.ds(n, 1)],
                                                None, ALU.is_equal)
                        nc.vector.tensor_scalar(joins[:, (j - PICK) % 7, :], self.dst_bc[:, bass.ds(n * P + 1, P)], self.dst_bc[:, bass.ds(n * P, 1)],
                                                None, ALU.is_equal).then_inc(masks_set, 1)
                    if n is not None:
                        wait_for(v, odd_set, n + 1)
                        nc.vector.scalar_tensor_tensor(out=msg[:, s, :], in0=y_ps[s][:, 0:P], scalar=self.even_col[:, bass.ds(n, 1)],
                                                       in1=odd[:, s, :], op0=ALU.mult, op1=ALU.add).then_inc(msg_set, 1)
                    if k is not None:
                        wait_for(v, rstd_set, k + 1)
                        if first:
                            wait_for(v, t_done, k - 6)
                            pairs = ((h[:, kc % 7, 0, :], src_x), (h[:, kc % 7, 1, :], dst_x))
                        else:
                            wait_for(v, h_stored[kc // U], 16 * used(it, j, NORM, RING))
                            pairs = ((out_h[:, kc, :], out_x),)
                        for i, (to, of) in enumerate(pairs):
                            last = nc.vector.tensor_scalar(to, of[:, kc, :], mv[:, kb, i, 0:1], rstd[:, kb, i:i + 1],
                                                           ALU.subtract, ALU.mult)
                        last.then_inc(norm_set, 1)
                    n = at(it, j, CARRY)
                    if n is not None:
                        s = (j - CARRY) % 2
                        if isinstance(n, int) and n == 0:
                            nc.vector.memset(agg_t[:, 1, :], 0.0).then_inc(agg_set, 1)
                        wait_for(v, agg_done, n + 1)
                        wait_for(v, masks_set, n + 1)
                        wait_for(v, agg_set, n + 1)
                        wait_for(v, p_done, n - 1)
                        nc.vector.scalar_tensor_tensor(out=agg_t[:, s, :], in0=joins[:, (j - CARRY) % 7, :], scalar=agg_t[:, 1 - s, P - 1:P],
                                                       in1=a_ps[s][:, 0:P], op0=ALU.mult, op1=ALU.add).then_inc(agg_set, 1)
                    n = at(it, j, OUT)
                    if n is not None:
                        s, r = (j - OUT) % 2, (j - OUT) % RING
                        turn = used(it, j, OUT, RING)
                        wait_for(v, p_done, n + 1)
                        if first:
                            wait_for(v, h_stored[r // U], 16 * turn)
                            nc.vector.scalar_tensor_tensor(out=out_x[:, r, :], in0=p_ps[s][:, 0:P], scalar=0.0, in1=self.b1[:, :],
                                                           op0=ALU.max, op1=ALU.add).then_inc(out_set, 1)
                        else:
                            wait_for(v, x_stored[r // U], 16 * turn)
                            wait_for(v, res_loaded[r // U], 16 * turn + 16)
                            nc.vector.tensor_tensor(x_res[:, r, :], x_res[:, r, :], self.b2[:, :], ALU.add).then_inc(xb_set, 1)
                            wait_for(v, xb_set, n + 1)
                            nc.vector.tensor_tensor(out_x[:, r, :], p_ps[s][:, 0:P], x_res[:, r, :], ALU.add).then_inc(out_set, 1)
                            wait_for(v, out_set, n + 1)
                            nc.vector.bn_stats(stats[:, s, 0, :], out_x[:, r, :]).then_inc(stats_set, 1)
                            wait_apart(v, stats_set, n + 1)
                            nc.vector.bn_aggr(mv[:, s, 0, :], stats[:, s, 0, :]).then_inc(mv_set, 1)

                turns(v, TURNS, RING, step, DRAIN)

            @block.scalar
            def _(act):
                def step(it, j):
                    n = at(it, j, 0)
                    if n is not None:
                        if first:
                            wait_for(act, norm_set, n - RING + 1)
                            wait_for(act, x_stored[j // U], 16 * it)
                            nc.scalar.copy(idx_now[:, j, :], self.ends_idx[:, bass.ds(n, 1), :].rearrange("p a k -> p (a k)")).then_inc(staged, 1)
                        else:
                            wait_for(act, t_done, n - RING + 1)
                            nc.scalar.copy(idx_now[:, j, 0:1], self.state_idx[:, bass.ds(n, 1)]).then_inc(staged, 1)
                    if first:
                        n = at(it, j, RELU)
                        if n is not None:
                            s = (j - RELU) % 7
                            wait_for(act, norm_set, n + 1)
                            nc.scalar.activation(h[:, s, :, :], h[:, s, :, :], ACT.Relu).then_inc(relu_set, 1)
                    n = at(it, j, MASK)
                    if n is not None:
                        s = (j - MASK) % 2
                        wait_for(act, masked_set, n + 1)
                        wait_for(act, p_done, n - 6)
                        nc.scalar.activation(ht_dst[:, (j - MASK) % 7, :], t_ps[s][:, P:2 * P], ACT.Copy).then_inc(dst_t_set, 1)
                    n = at(it, j, PICK)
                    if n is not None:
                        s = (j - PICK) % 2
                        wait_for(act, y_done, n + 1)
                        wait_for(act, msg_set, n - 1)
                        nc.scalar.activation(odd[:, s, :], y_ps[s][:, P:2 * P], ACT.Copy,
                                             scale=self.odd_col[:, bass.ds(n, 1)]).then_inc(odd_set, 1)
                    n = at(it, j, STATS)
                    if n is not None:
                        s = (j - STATS) % 2
                        wait_for(act, mv_set, n + 1)
                        nc.scalar.activation(std[:, s, 0:PARTS], mv[:, s, 0:PARTS, 1], ACT.Sqrt, bias=self.eps[:, :]).then_inc(std_set, 1)
                    if not first:
                        n = at(it, j, TAIL)
                        if n is not None:
                            r = (j - TAIL) % RING
                            wait_for(act, norm_set, n + 1)
                            nc.scalar.activation(out_h[:, r, :], out_h[:, r, :], ACT.Relu).then_inc(out_relu, 1)

                turns(act, TURNS, RING, step, DRAIN)

            @block.tensor
            def _(pe):
                def step(it, j):
                    n = at(it, j, T)
                    if n is not None:
                        s, r = (j - T) % 2, (j - T) % RING
                        turn = used(it, j, T, RING)
                        if first:
                            wait_for(pe, relu_set, n + 1)
                            pair = (h[:, r % 7, 0, :], h[:, r % 7, 1, :])
                        else:
                            wait_for(pe, gathered[r], GOT * turn + GOT)
                            wait_for(pe, loaded[r // U], 16 * turn + 16)
                            pair = (src_x[:, r, :], dst_x[:, r, :])
                        wait_for(pe, masked_set, n - 1)
                        wait_for(pe, dst_t_set, n - 1)
                        nc.tensor.transpose(t_ps[s][:, 0:P], pair[0], self.ident[:, :])
                        nc.tensor.transpose(t_ps[s][:, P:2 * P], pair[1], self.ident[:, :]).then_inc(t_done, 1)
                    n = at(it, j, Y)
                    if n is not None:
                        s = (j - Y) % 2
                        wait_for(pe, masked_set, n + 1)
                        wait_for(pe, msg_set, n - 1)
                        for q in range(R // 2):
                            last = nc.tensor.matmul(y_ps[s][:, 0:2 * P], ht_masked[:, s, q, :],
                                                    w[:, 2 * q:2 * q + 2, :].rearrange("c r o -> c (r o)"),
                                                    start=(q == 0), stop=(q == R // 2 - 1))
                        last.then_inc(y_done, 1)
                    n = at(it, j, AGG)
                    if n is not None:
                        s = (j - AGG) % 2
                        wait_for(pe, msg_set, n + 1)
                        wait_for(pe, masks_set, n + 1)
                        wait_for(pe, agg_set, n)
                        nc.tensor.matmul(a_ps[s][:, 0:P], msg[:, s, :], same[:, s, :], start=True, stop=True).then_inc(agg_done, 1)
                    n = at(it, j, SELF)
                    if n is not None:
                        s = (j - SELF) % 2
                        wait_for(pe, dst_t_set, n + 1)
                        wait_for(pe, agg_set, n + 2)
                        wait_for(pe, out_set, n - 1)
                        nc.tensor.matmul(p_ps[s][:, 0:P], ht_dst[:, (j - SELF) % 7, :], sw[:, :], start=True, stop=False)
                        nc.tensor.matmul(p_ps[s][:, 0:P], agg_t[:, s, :], self.ident[:, :], start=False, stop=True).then_inc(p_done, 1)

                turns(pe, TURNS, RING, step, DRAIN)

    def conv(self, layer):
        nc, last_layer = self.nc, layer == 5
        with ExitStack() as ctx:
            def sb(name, shape, dt=F32):
                return ctx.enter_context(nc.sbuf_tensor(f"c{layer}_{name}", shape, dt))

            sems = []

            def sem(name):
                sems.append(nc.alloc_semaphore(f"c{layer}_{name}"))
                return sems[-1]

            src_h = sb("src_h", [P, RING, P])
            edge = sb("edge", [P, RING, P])
            res = sb("res", [P, RING, P])
            same = sb("same", [P, 2, P])
            joins = sb("joins", [P, 7, P])
            agg_t = sb("agg_t", [P, 2, P])
            out_h = sb("out_h", [P, RING, P])
            local_h = None if last_layer else sb("local_h", [P, RING, P])
            idx_now = sb("idx_now", [P, RING, 2], I32)
            a_ps = [ctx.enter_context(nc.psum_tensor(f"c{layer}_a_ps{i}", [P, 512], F32)) for i in range(2)]
            p_ps = [ctx.enter_context(nc.psum_tensor(f"c{layer}_p_ps{i}", [P, 512], F32)) for i in range(2)]

            gathered = [sem(f"gathered{i}") for i in range(RING)]
            scattered = [sem(f"scattered{i}") for i in range(RING)] if last_layer else None
            edge_loaded = [sem(f"edge_loaded{i}") for i in range(2)]
            res_loaded = [sem(f"res_loaded{i}") for i in range(2)]
            out_stored = [sem(f"out_stored{i}") for i in range(2)]
            local_stored = [sem(f"local_stored{i}") for i in range(2)]
            staged, masks_set, agg_done, agg_set, p_done, out_set, out_relu, local_set, local_relu, put_staged = (
                sem("staged"), sem("masks"), sem("agg_done"), sem("agg_set"), sem("p_done"), sem("out"),
                sem("out_relu"), sem("local"), sem("local_relu"), sem("put_staged"))
            ctx.callback(self.free, sems)
            block = ctx.enter_context(nc.Block())

            source = {3: self.h2_table, 4: self.h3_table, 5: self.h4_table}[layer]
            target = {3: self.h3_table, 4: self.h4_table, 5: None}[layer]
            idx = self.state_idx if layer == 3 else self.local_idx
            residual = {3: self.h2_table[NP:NP + EP, :], 4: self.h3_table[EP:2 * EP, :], 5: self.x2_slots}[layer]
            w, bias = self.gw[layer - 3], self.gb[layer - 3]
            MASKS, AGG, CARRY, SELF, OUT, RELU = 7, 8, 9, 10, 11, 12
            DRAIN = RELU + 1
            at = lambda it, j, skew: tile_at(it, j, skew, RING, TILES)
            used = lambda it, j, skew, ring: use_of(it, j, skew, ring, RING)

            def slot_rows(table, g):
                return table[bass.ds(g * (U * P), U * P), :].rearrange("(p k) c -> p (k c)", k=U)

            def slots(t, hf):
                return t[:, hf * U:(hf + 1) * U, :].rearrange("p k c -> p (k c)")

            @block.gpsimd
            def _(pool):
                def step(it, j):
                    n = at(it, j, 0)
                    if n is not None:
                        wait_for(pool, staged, n + 1)
                        pool.nop(nofuse=True)
                        pool.indirect_dma_start(src_h[:, j, :], None, source[:, :],
                                                bass.IndirectOffsetOnAxis(ap=idx_now[:, j, 0:1], axis=0)).then_inc(gathered[j], 16)
                    n = at(it, j, RELU)
                    if last_layer and n is not None:
                        r = (j - RELU) % RING
                        wait_for(pool, put_staged, n + 1)
                        wait_for(pool, out_set, n + 1)
                        pool.nop(nofuse=True)
                        pool.indirect_dma_start(self.out[:, :], bass.IndirectOffsetOnAxis(ap=idx_now[:, r, 1:2], axis=0),
                                                out_h[:, r, :], None, bounds_check=NP - 1, oob_is_err=False).then_inc(scattered[r], 16)

                turns(pool, TURNS, RING, step, DRAIN if last_layer else 0)
                if last_layer:
                    for r in range(RING):
                        pool.wait_ge(scattered[r], 16 * TURNS)

            @block.sync
            def _(sp):
                def load(it, hf):
                    g = 2 * it + hf
                    wait_apart(sp, agg_done, U * g - U)
                    sp.dma_start(edge[:, hf * U:(hf + 1) * U, :], self.ins["edge"][bass.ds(g * (U * P), U * P), :]
                                 .rearrange("(k p) c -> p k c", p=P)).then_inc(edge_loaded[hf], 16)
                    wait_apart(sp, out_set, U * g - U)
                    sp.dma_start(slots(res, hf), slot_rows(residual, g)).then_inc(res_loaded[hf], 16)

                def store(it, hf):
                    if last_layer:
                        return
                    g = 2 * it + hf
                    wait_apart(sp, local_relu, U * g + U)
                    sp.dma_start(slot_rows(target[0:EP, :], g), slots(local_h, hf)).then_inc(local_stored[hf], 16)
                    wait_apart(sp, out_relu, U * g + U)
                    sp.dma_start(slot_rows(target[EP:2 * EP, :], g), slots(out_h, hf)).then_inc(out_stored[hf], 16)

                load(0, 0)
                load(0, 1)
                with sp.Fori(1, TURNS) as it:
                    load(it, 0)
                    store(it - 1, 0)
                    load(it, 1)
                    store(it - 1, 1)
                store(TURNS - 1, 0)
                store(TURNS - 1, 1)
                if not last_layer:
                    for hf in range(2):
                        sp.wait_ge(local_stored[hf], 16 * TURNS)
                        sp.wait_ge(out_stored[hf], 16 * TURNS)

            @block.vector
            def _(v):
                def step(it, j):
                    n = at(it, j, MASKS)
                    if n is not None:
                        s = (j - MASKS) % 2
                        wait_for(v, agg_done, n - 1)
                        nc.vector.tensor_scalar(same[:, s, :], self.dst_bc[:, bass.ds(n * P + 1, P)], self.dst_col[:, bass.ds(n, 1)],
                                                None, ALU.is_equal)
                        nc.vector.tensor_scalar(joins[:, (j - MASKS) % 7, :], self.dst_bc[:, bass.ds(n * P + 1, P)],
                                                self.dst_bc[:, bass.ds(n * P, 1)], None, ALU.is_equal).then_inc(masks_set, 1)
                    n = at(it, j, CARRY)
                    if n is not None:
                        s = (j - CARRY) % 2
                        if isinstance(n, int) and n == 0:
                            nc.vector.memset(agg_t[:, 1, :], 0.0).then_inc(agg_set, 1)
                        wait_for(v, agg_done, n + 1)
                        wait_for(v, masks_set, n + 1)
                        wait_for(v, agg_set, n + 1)
                        wait_for(v, p_done, n - 1)
                        nc.vector.scalar_tensor_tensor(out=agg_t[:, s, :], in0=joins[:, (j - CARRY) % 7, :],
                                                       scalar=agg_t[:, 1 - s, P - 1:P], in1=a_ps[s][:, 0:P],
                                                       op0=ALU.mult, op1=ALU.add).then_inc(agg_set, 1)
                    n = at(it, j, AGG)
                    if n is not None and not last_layer:
                        r, u = (j - AGG) % RING, used(it, j, AGG, RING)
                        wait_for(v, gathered[r], 16 * u + 16)
                        wait_for(v, local_stored[r // U], 16 * u)
                        nc.vector.tensor_tensor(local_h[:, r, :], src_h[:, r, :], bias[:, :], ALU.add).then_inc(local_set, 1)
                    n = at(it, j, OUT)
                    if n is not None:
                        s, r, u = (j - OUT) % 2, (j - OUT) % RING, used(it, j, OUT, RING)
                        wait_for(v, p_done, n + 1)
                        wait_for(v, res_loaded[r // U], 16 * u + 16)
                        if last_layer:
                            wait_for(v, scattered[r], 16 * u)
                        else:
                            wait_for(v, out_stored[r // U], 16 * u)
                        nc.vector.scalar_tensor_tensor(out=out_h[:, r, :], in0=p_ps[s][:, 0:P], scalar=self.isd_col[:, bass.ds(n, 1)],
                                                       in1=res[:, r, :], op0=ALU.mult, op1=ALU.add).then_inc(out_set, 1)

                turns(v, TURNS, RING, step, DRAIN)

            @block.scalar
            def _(act):
                def step(it, j):
                    n = at(it, j, 0)
                    if n is not None:
                        wait_for(act, agg_done, n - RING + 1)
                        if not last_layer:
                            wait_for(act, local_set, n - RING + 1)
                        nc.scalar.copy(idx_now[:, j, 0:1], idx[:, bass.ds(n, 1)]).then_inc(staged, 1)
                    if last_layer:
                        n = at(it, j, OUT)
                        if n is not None:
                            r = (j - OUT) % RING
                            wait_for(act, scattered[r], 16 * used(it, j, OUT, RING))
                            nc.scalar.copy(idx_now[:, r, 1:2], self.end_idx[:, bass.ds(n, 1)]).then_inc(put_staged, 1)
                        return
                    n = at(it, j, CARRY)
                    if n is not None:
                        r = (j - CARRY) % RING
                        wait_for(act, local_set, n + 1)
                        nc.scalar.activation(local_h[:, r, :], local_h[:, r, :], ACT.Relu).then_inc(local_relu, 1)
                    n = at(it, j, RELU)
                    if n is not None:
                        r = (j - RELU) % RING
                        wait_for(act, out_set, n + 1)
                        nc.scalar.activation(out_h[:, r, :], out_h[:, r, :], ACT.Relu).then_inc(out_relu, 1)

                turns(act, TURNS, RING, step, DRAIN)

            @block.tensor
            def _(pe):
                def step(it, j):
                    n = at(it, j, AGG)
                    if n is not None:
                        s, r, u = (j - AGG) % 2, (j - AGG) % RING, used(it, j, AGG, RING)
                        wait_for(pe, gathered[r], 16 * u + 16)
                        wait_for(pe, edge_loaded[r // U], 16 * u + 16)
                        wait_for(pe, masks_set, n + 1)
                        wait_for(pe, agg_set, n)
                        nc.tensor.matmul(a_ps[s][:, 0:P], src_h[:, r, :], same[:, s, :], start=True, stop=False)
                        nc.tensor.matmul(a_ps[s][:, 0:P], edge[:, r, :], same[:, s, :], start=False, stop=True).then_inc(agg_done, 1)
                    n = at(it, j, SELF)
                    if n is not None:
                        s = (j - SELF) % 2
                        wait_for(pe, agg_set, n + 2)
                        wait_for(pe, out_set, n - 1)
                        nc.tensor.matmul(p_ps[s][:, 0:P], agg_t[:, s, :], w[:, :], start=True, stop=False)
                        nc.tensor.matmul(p_ps[s][:, 0:P], self.ones[0:1, :], self.gb_row[0:1, layer - 3, :], start=False, stop=True).then_inc(p_done, 1)

                turns(pe, TURNS, RING, step, DRAIN)


def program(nc, ins, out):
    Program(nc, ins, out).build()


def kernel(**inputs):
    import numpy as np
    import concourse.bacc as bacc
    from concourse.bass_utils import run_bass_kernel_spmd as run

    def padded(a, before, after, value):
        a = np.asarray(a)
        front = np.full((before,) + a.shape[1:], value, a.dtype)
        back = np.full((after,) + a.shape[1:], value, a.dtype)
        return np.concatenate([front, a, back])

    extra = EP - E
    dst = padded(inputs["dst"], 0, extra, PAD_NODE)
    arrays = {
        "x": padded(inputs["x"], 0, NP - N, 0),
        "src": padded(inputs["src"], 0, extra, PAD_NODE),
        "dst": padded(dst, 1, 1, -1),
        "typ": padded(inputs["edge_type_8"], 0, extra, 0),
        "edge": padded(inputs["edge_attr_128"], 0, extra, 0),
        "w1": inputs["L0_gnn_w1"], "sw1": inputs["L0_gnn_sw1"], "b1": inputs["L0_gnn_b1"],
        "w2": inputs["L0_gnn_w2"], "sw2": inputs["L0_gnn_sw2"], "b2": inputs["L0_gnn_b2"],
        "W0": inputs["L1_gnn_W0"], "W1": inputs["L1_gnn_W1"], "W2": inputs["L1_gnn_W2"],
        "g0": inputs["L1_gnn_b0"], "g1": inputs["L1_gnn_b1"], "g2": inputs["L1_gnn_b2"],
    }
    arrays = {k: np.ascontiguousarray(v) for k, v in arrays.items()}
    nc = bacc.Bacc("TRN2", target_bir_lowering=False, num_devices=1)
    ins = {k: nc.dram_tensor(f"in_{k}", a.shape, mybir.dt.from_np(a.dtype), kind="ExternalInput").ap()
           for k, a in arrays.items()}
    out = nc.dram_tensor("result", [NP, P], F32, kind="ExternalOutput").ap()
    program(nc, ins, out)
    r = run(nc, [{f"in_{k}": a for k, a in arrays.items()}], core_ids=[0])
    return r.results[0]["result"][:N]
```

```python
from contextlib import ExitStack

import concourse.bass as bass
from concourse import mybir
from concourse.alu_op_type import AluOpType as ALU

ACT = mybir.ActivationFunctionType
F32 = mybir.dt.float32
I32 = mybir.dt.int32

P = 128
N = 50000
E = 25000
R = 8
TILES = 196
EP = TILES * P
U = 7
RING = 2 * U
TURNS = TILES // RING
DG = 4
DRING = 14
DGROUPS = 98
DTURNS = DGROUPS // DRING
NP = DGROUPS * DG * P
PAD_NODE = N
HALF = TILES // 2
SKIP = float(1 << 20)
EPS = 1e-5
assert TILES % RING == 0 and EP >= E and NP > N and DGROUPS % DRING == 0


def turns(eng, count, ring, step, drain):
    for it in range(2):
        for j in range(ring):
            step(it, j)
    with eng.Fori(2, count) as it:
        for j in range(ring):
            step(it, j)
    for j in range(drain):
        step(count + j // ring, j % ring)


def tile_at(it, j, skew, ring, total):
    n = ring * it + (j - skew)
    if isinstance(n, int) and not 0 <= n < total:
        return None
    return n


def use_of(it, j, skew, ring, turn):
    return (turn // ring) * it + (j - skew) // ring


def wait_for(eng, sem, value):
    if isinstance(value, int) and value <= 0:
        return
    eng.wait_ge(sem, value)


def wait_apart(eng, sem, value):
    wait_for(eng, sem, value)
    eng.nop(nofuse=True)


class Program:
    def __init__(self, nc, ins, out):
        self.nc, self.ins, self.out = nc, ins, out
        dram = lambda name, shape, dt=F32: nc.dram_tensor(name, shape, dt, kind="Internal").ap()
        self.h0_table = dram("h0_table", [NP, P])
        self.p1_table = dram("p1_table", [NP + EP, P])
        self.h2_table = dram("h2_table", [NP + EP, P])
        self.h3_table = dram("h3_table", [2 * EP, P])
        self.h4_table = dram("h4_table", [2 * EP, P])
        self.x2_slots = dram("x2_slots", [EP, P])
        self.row_of_node = dram("row_of_node", [NP, 1], I32)
        self.dst_f = dram("dst_f", [EP + 1])
        self.half_f = dram("half_f", [EP])
        self.count_f = dram("count_f", [EP])

    def free(self, sems):
        self.nc.clear_and_free_semaphores(sems)
        self.nc.all_engine_barrier()

    def build(self):
        nc = self.nc
        with ExitStack() as ctx:
            def sb(name, shape, dt=F32):
                return ctx.enter_context(nc.sbuf_tensor(name, shape, dt))
            self.ident = sb("ident", [P, P])
            self.ones = sb("ones", [P, P])
            self.eps = sb("eps", [P, 1])
            self.sw1 = sb("sw1", [P, P])
            self.sw2 = sb("sw2", [P, P])
            self.w1 = sb("w1", [P, R, P])
            self.w2 = sb("w2", [P, R, P])
            self.gw = [sb(f"gw{i}", [P, P]) for i in range(3)]
            self.gb_row = sb("gb_row", [1, 3, P])
            self.b1_col = sb("b1_col", [P, 1])
            self.b2 = sb("b2", [P, P])
            self.gb = [sb(f"gb{i}", [P, P]) for i in range(3)]
            self.dst_col = sb("dst_col", [P, TILES])
            self.end_idx = sb("end_idx", [P, TILES], I32)
            self.ends_idx = sb("ends_idx", [P, TILES, 2], I32)
            self.slot_row = sb("slot_row", [P, TILES], I32)
            self.state_idx = sb("state_idx", [P, TILES], I32)
            self.local_idx = sb("local_idx", [P, TILES], I32)
            self.odd_col = sb("odd_col", [P, TILES])
            self.even_col = sb("even_col", [P, TILES])
            self.isd_col = sb("isd_col", [P, TILES])
            self.setup()
            self.dense_and_slots()
            self.dst_bc = sb("dst_bc", [P, EP + 1])
            self.joins = sb("joins", [P, EP], mybir.dt.uint8)
            self.relational(1)
            self.relational(2)
            self.conv(3)
            self.conv(4)
            self.conv(5)

    def setup(self):
        nc, ins = self.nc, self.ins
        with ExitStack() as ctx:
            def sb(name, shape, dt=F32):
                return ctx.enter_context(nc.sbuf_tensor(name, shape, dt))

            sems = []

            def sem(name):
                sems.append(nc.alloc_semaphore(name))
                return sems[-1]

            dst_r = sb("dst_r", [HALF, 2, P], I32)
            next_r = sb("next_r", [HALF, 2, P], I32)
            src_r = sb("src_r", [HALF, 2, P], I32)
            typ_r = sb("typ_r", [HALF, 2, P], I32)
            half_i = sb("half_i", [HALF, 2, P], I32)
            odd_i = sb("odd_i", [HALF, 2, P], I32)
            dst_rf = sb("dst_rf", [HALF, 2, P])
            next_rf = sb("next_rf", [HALF, 2, P])
            end_rf = sb("end_rf", [HALF, 2, P])
            inner = sb("inner", [HALF, 2, P])
            src_rf = sb("src_rf", [HALF, 2, P])
            half_rf = sb("half_rf", [HALF, 2, P])
            odd_rf = sb("odd_rf", [HALF, 2, P])
            count_rf = sb("count_rf", [HALF, 2, P])
            dst_q = sb("dst_q", [P, TILES], I32)
            prev_q = sb("prev_q", [P, TILES], I32)
            dst_qf = sb("dst_qf", [P, TILES])
            prev_qf = sb("prev_qf", [P, TILES])
            same_q = sb("same_q", [P, TILES])
            ones_q = sb("ones_q", [P, TILES])
            count_q = sb("count_q", [P, TILES])
            firsts = sb("firsts", [P, P])
            later = sb("later", [P, P])
            reach = sb("reach", [P, P])
            carried = sb("carried", [P, P])
            carry = sb("carry", [P, 1])
            in_first = sb("in_first", [P, TILES])
            count_all = sb("count_all", [P, TILES])
            least_one = sb("least_one", [P, TILES])
            root = sb("root", [P, TILES])
            front = sb("front", [1, 1])
            node_ids = sb("node_ids", [P, NP // P], I32)
            cols_ps = [ctx.enter_context(nc.psum_tensor(f"cols_ps{i}", [P, 512], F32)) for i in range(6)]

            edges_loaded, weights_loaded = sem("edges_loaded"), sem("weights_loaded")
            ident_set, ready_rows, cols_done = sem("ident_set"), sem("ready_rows"), sem("cols_done")
            dve = sem("setup_dve")
            firsts_set, firsts_done, reach_set, carry_done = (
                sem("firsts_set"), sem("firsts_done"), sem("reach_set"), sem("carry_done"))
            rows_stored, count_set, count_stored, count_loaded = (
                sem("rows_stored"), sem("count_set"), sem("count_stored"), sem("count_loaded"))
            count_cols, ids_set, later_set, ones_set = (
                sem("count_cols"), sem("ids_set"), sem("later_set"), sem("ones_set"))
            ids_stored = sem("ids_stored")
            least_set, root_set = sem("least_set"), sem("root_set")
            ctx.callback(self.free, sems)
            block = ctx.enter_context(nc.Block())

            def rows(a):
                return a.rearrange("(i q f) -> q i f", i=2, q=HALF)

            def bc(a):
                return a.rearrange("(a c) -> a c", a=1).broadcast_to([P, P])

            dstp = ins["dst"]

            @block.sync
            def _(sp):
                for to, of in ((dst_r, rows(dstp[1:EP + 1])), (next_r, rows(dstp[2:EP + 2])),
                               (src_r, rows(ins["src"])), (typ_r, rows(ins["typ"]))):
                    sp.dma_start(to[:, :, :], of).then_inc(edges_loaded, 16)
                sp.dma_start(dst_q[:, :], dstp[1:EP + 1].rearrange("(p j) -> p j", p=P)).then_inc(edges_loaded, 16)
                sp.dma_start(prev_q[:, :], dstp[0:EP].rearrange("(p j) -> p j", p=P)).then_inc(edges_loaded, 16)
                sp.wait_ge(ready_rows, 1)
                sp.dma_start(self.dst_f[1:EP + 1].rearrange("(i q f) -> q i f", i=2, q=HALF),
                             dst_rf[:, :, :]).then_inc(rows_stored, 16)
                sp.dma_start(self.dst_f[0:1].rearrange("(a c) -> a c", a=1), front[:, :]).then_inc(rows_stored, 16)
                sp.dma_start(rows(self.half_f), half_rf[:, :, :]).then_inc(rows_stored, 16)
                sp.wait_ge(count_set, 1)
                sp.dma_start(self.count_f.rearrange("(p j) -> p j", p=P), count_all[:, :]).then_inc(count_stored, 16)
                sp.wait_ge(count_stored, 16)
                sp.dma_start(count_rf[:, :, :], rows(self.count_f)).then_inc(count_loaded, 16)
                sp.wait_ge(rows_stored, 3 * 16)
                sp.wait_ge(weights_loaded, 15 * 16)

            @block.scalar
            def _(act):
                for to, of in ((self.sw1, ins["sw1"]), (self.sw2, ins["sw2"]), (self.gw[0], ins["W0"]),
                               (self.gw[1], ins["W1"]), (self.gw[2], ins["W2"])):
                    act.dma_start(to[:, :], of).then_inc(weights_loaded, 16)
                act.dma_start(self.w1[:, :, :], ins["w1"].rearrange("r c o -> c r o")).then_inc(weights_loaded, 16)
                act.dma_start(self.w2[:, :, :], ins["w2"].rearrange("r c o -> c r o")).then_inc(weights_loaded, 16)
                for to, of in ((self.b2, ins["b2"]), (self.gb[0], ins["g0"]),
                               (self.gb[1], ins["g1"]), (self.gb[2], ins["g2"])):
                    act.dma_start(to[:, :], bc(of)).then_inc(weights_loaded, 16)
                act.dma_start(self.b1_col[:, :], ins["b1"].rearrange("(c a) -> c a", a=1)).then_inc(weights_loaded, 16)
                for i in range(3):
                    act.dma_start(self.gb_row[0:1, i, :], ins[f"g{i}"].rearrange("(a c) -> a c", a=1)).then_inc(weights_loaded, 16)
                act.wait_ge(least_set, 1)
                nc.scalar.activation(root[:, :], least_one[:, :], ACT.Sqrt).then_inc(root_set, 1)

            @block.gpsimd
            def _(pool):
                pool.memset(self.ident[:, :], 0.0).then_inc(ident_set, 1)
                pool.memset(self.eps[:, :], EPS)
                pool.memset(self.ones[:, :], 1.0).then_inc(ones_set, 1)
                pool.wait_ge(ident_set, 1)
                pool.affine_select(out=self.ident[:, :], in_=self.ident[:, :], compare_op=ALU.not_equal, fill=1.0,
                                   base=0, pattern=[[-1, P]], channel_multiplier=1).then_inc(ident_set, 1)
                pool.wait_ge(ones_set, 1)
                pool.affine_select(out=later[:, :], in_=self.ones[:, :], compare_op=ALU.is_gt, fill=0.0,
                                   base=0, pattern=[[1, P]], channel_multiplier=-1).then_inc(later_set, 1)
                pool.iota(self.slot_row[:, :].rearrange("p (g k) -> p g k", k=U), pattern=[[P * U, TILES // U], [1, U]],
                          base=NP, channel_multiplier=U)
                pool.iota(node_ids[:, :], pattern=[[1, NP // P]], base=0, channel_multiplier=NP // P).then_inc(ids_set, 1)
                pool.wait_ge(ids_set, 1)
                pool.dma_start(self.row_of_node.rearrange("(p j) a -> p (j a)", p=P), node_ids[:, :]).then_inc(ids_stored, 16)
                pool.wait_ge(ids_stored, 16)

            @block.vector
            def _(v):
                done = [0]

                def link(ins_):
                    done[0] += 1
                    ins_.then_inc(dve, 1)
                    v.wait_ge(dve, done[0])

                v.wait_ge(edges_loaded, 6 * 16)
                nc.vector.memset(front[:, :], -1.0)
                nc.vector.memset(ones_q[:, :], 1.0)
                nc.vector.tensor_scalar(odd_i[:, :, :], typ_r[:, :, :], 1, None, ALU.bitwise_and)
                nc.vector.tensor_scalar(half_i[:, :, :], typ_r[:, :, :], 1, None, ALU.arith_shift_right)
                nc.vector.tensor_copy(dst_rf[:, :, :], dst_r[:, :, :])
                nc.vector.tensor_copy(next_rf[:, :, :], next_r[:, :, :])
                nc.vector.tensor_copy(src_rf[:, :, :], src_r[:, :, :])
                nc.vector.tensor_copy(dst_qf[:, :], dst_q[:, :])
                link(nc.vector.tensor_copy(prev_qf[:, :], prev_q[:, :]))
                nc.vector.tensor_copy(odd_rf[:, :, :], odd_i[:, :, :])
                nc.vector.tensor_copy(half_rf[:, :, :], half_i[:, :, :])
                nc.vector.tensor_tensor(inner[:, :, :], dst_rf[:, :, :], next_rf[:, :, :], ALU.is_equal)
                nc.vector.tensor_copy(firsts[:, :], dst_qf[:, 0:1].broadcast_to([P, P])).then_inc(firsts_set, 1)
                link(nc.vector.tensor_tensor(same_q[:, :], dst_qf[:, :], prev_qf[:, :], ALU.is_equal))
                nc.vector.scalar_tensor_tensor(out=end_rf[:, :, :], in0=inner[:, :, :], scalar=SKIP, in1=dst_rf[:, :, :],
                                               op0=ALU.mult, op1=ALU.add).then_inc(ready_rows, 1)
                link(nc.vector.tensor_tensor_scan(count_q[:, :], same_q[:, :], ones_q[:, :], 0.0, ALU.mult, ALU.add))
                v.wait_ge(firsts_done, 1)
                v.wait_ge(later_set, 1)
                link(nc.vector.scalar_tensor_tensor(out=reach[:, :], in0=cols_ps[5][:, 0:P], scalar=dst_qf[:, TILES - 1:TILES],
                                                    in1=later[:, :], op0=ALU.is_equal, op1=ALU.mult))
                nc.vector.tensor_copy(carried[:, :], count_q[:, TILES - 1:TILES].broadcast_to([P, P])).then_inc(reach_set, 1)
                nc.vector.tensor_scalar(in_first[:, :], dst_qf[:, :], dst_qf[:, 0:1], None, ALU.is_equal)
                v.wait_ge(carry_done, 1)
                link(nc.vector.tensor_copy(carry[:, :], cols_ps[4][:, 256:257]))
                nc.vector.scalar_tensor_tensor(out=count_all[:, :], in0=in_first[:, :], scalar=carry[:, :], in1=count_q[:, :],
                                               op0=ALU.mult, op1=ALU.add).then_inc(count_set, 1)
                v.wait_ge(cols_done, 4)
                nc.vector.tensor_copy(self.dst_col[:, :], cols_ps[0][:, 0:TILES])
                nc.vector.tensor_copy(self.ends_idx[:, :, 1], cols_ps[0][:, 0:TILES])
                nc.vector.tensor_copy(self.end_idx[:, :], cols_ps[1][:, 0:TILES])
                nc.vector.tensor_copy(self.ends_idx[:, :, 0], cols_ps[2][:, 0:TILES])
                nc.vector.tensor_copy(self.odd_col[:, :], cols_ps[3][:, 0:TILES])
                nc.vector.tensor_scalar(self.even_col[:, :], cols_ps[3][:, 0:TILES], -1.0, 1.0, ALU.mult, ALU.add)
                v.wait_ge(count_cols, 1)
                nc.vector.tensor_scalar(least_one[:, :], cols_ps[4][:, 0:TILES], 1.0, None, ALU.max).then_inc(least_set, 1)
                v.wait_ge(root_set, 1)
                nc.vector.reciprocal(self.isd_col[:, :], root[:, :])
                v.wait_ge(weights_loaded, 15 * 16)
                v.wait_ge(ident_set, 2)
                nc.vector.tensor_tensor(self.sw1[:, :], self.sw1[:, :], self.ident[:, :], ALU.add)

            @block.tensor
            def _(pe):
                pe.wait_ge(ident_set, 2)
                pe.wait_ge(firsts_set, 1)
                nc.tensor.transpose(cols_ps[5][:, 0:P], firsts[:, :], self.ident[:, :]).then_inc(firsts_done, 1)
                pe.wait_ge(ready_rows, 1)
                for n, rows_f in enumerate((dst_rf, end_rf, src_rf, odd_rf)):
                    for i in range(2):
                        last = nc.tensor.transpose(cols_ps[n][:, i * HALF:(i + 1) * HALF], rows_f[:, i, :],
                                                   self.ident[0:HALF, 0:HALF])
                    last.then_inc(cols_done, 1)
                pe.wait_ge(reach_set, 1)
                nc.tensor.matmul(cols_ps[4][:, 256:256 + P], reach[:, :], carried[:, :], start=True, stop=True).then_inc(carry_done, 1)
                pe.wait_ge(count_loaded, 16)
                pe.wait_ge(count_set, 1)
                for i in range(2):
                    last = nc.tensor.transpose(cols_ps[4][:, i * HALF:(i + 1) * HALF], count_rf[:, i, :],
                                               self.ident[0:HALF, 0:HALF])
                last.then_inc(count_cols, 1)

    def dense_and_slots(self):
        nc = self.nc
        with ExitStack() as ctx:
            def sb(name, shape, dt=F32):
                return ctx.enter_context(nc.sbuf_tensor(name, shape, dt))

            sems = []

            def sem(name):
                sems.append(nc.alloc_semaphore(name))
                return sems[-1]

            W = DG * P
            x = sb("x_ring", [P, DRING, DG, P])
            stats = sb("stats", [P, 7, DG, 6])
            mv = sb("mv", [P, 7, 2, DG, 2])
            std = sb("std", [P, 7, 2, DG])
            rstd = sb("rstd", [P, 7, 2, DG])
            stats2 = sb("stats2", [P, 7, DG, 6])
            shift = sb("shift", [P, 7, 2, DG])
            h0 = sb("h0_ring", [P, 7, W])
            h0t = sb("h0t_ring", [P, 2, W])
            h1t = sb("h1t_ring", [P, 2, W])
            x2 = sb("x2_ring", [P, 7, DG, P])
            p1_out = sb("p1_out_ring", [P, 7, W])
            h2 = sb("h2_ring", [P, 7, W])
            res = sb("res_ring", [P, 7, W])
            t1 = [ctx.enter_context(nc.psum_tensor(f"t1_ps{i}", [P, W], F32)) for i in range(2)]
            p1 = [ctx.enter_context(nc.psum_tensor(f"p1_ps{i}", [P, W], F32)) for i in range(2)]
            t2 = [ctx.enter_context(nc.psum_tensor(f"t2_ps{i}", [P, W], F32)) for i in range(2)]
            p2 = [ctx.enter_context(nc.psum_tensor(f"p2_ps{i}", [P, W], F32)) for i in range(2)]
            id_now = sb("id_now", [P, 2, U], I32)
            row_now = sb("row_now", [P, 2, U], I32)
            row_got = sb("row_got", [P, 2, U], I32)
            is_slot = sb("is_slot", [P, TILES])
            own_f = sb("own_f", [P, TILES])
            slot_f = sb("slot_f", [P, TILES])
            step_f = sb("step_f", [P, TILES])
            pick_f = sb("pick_f", [P, TILES])

            x_loaded = [sem(f"x_loaded{i}") for i in range(DRING)]
            stats_set, mv_set, std_set, rstd_set, h0_set, std2_set = (
                sem("d_stats"), sem("d_mv"), sem("d_std"), sem("d_rstd"), sem("d_h0"), sem("d_std2"))
            t1_done, h0t_set, p1_done, t2_done, h1t_set, p2_done = (
                sem("d_t1"), sem("d_h0t"), sem("d_p1"), sem("d_t2"), sem("d_h1t"), sem("d_p2"))
            xb_set, x2_set, stats2_set, mv2_set, rstd2_set, h2_set, res_set = (
                sem("d_xb"), sem("d_x2"), sem("d_stats2"), sem("d_mv2"), sem("d_rstd2"), sem("d_h2"), sem("d_res"))
            shift_set, shift2_set, p1_out_set = sem("d_shift"), sem("d_shift2"), sem("d_p1_out")
            h0_stored = [sem(f"h0_stored{i}") for i in range(7)]
            p1_stored = [sem(f"p1_stored{i}") for i in range(7)]
            h2_stored = [sem(f"h2_stored{i}") for i in range(7)]
            res_stored = [sem(f"res_stored{i}") for i in range(7)]
            staged = sem("staged")
            slots_put = [sem(f"slots_put{i}") for i in range(2)]
            slots_got = [sem(f"slots_got{i}") for i in range(2)]
            rows_copied, state_rows, pick = sem("rows_copied"), sem("state_rows"), sem("pick")
            ctx.callback(self.free, sems)
            block = ctx.enter_context(nc.Block())

            D = DGROUPS
            LN, NORM, H0, T1, H0T, P1, H1, T2, H1T, P2, LN2, NORM2, H2, STORE2 = 2, 4, 5, 6, 7, 8, 9, 10, 11, 12, 13, 15, 16, 17
            DRAIN = STORE2 + 1
            at = lambda it, j, skew: tile_at(it, j, skew, DRING, D)
            used = lambda it, j, skew, ring: use_of(it, j, skew, ring, DRING)

            def node_rows(table, g):
                return table[bass.ds(g * (DG * P), DG * P), :].rearrange("(p k) c -> p (k c)", k=DG)

            def tiles(a):
                return a.rearrange("p (k c) -> p k c", k=DG)

            def each(bias):
                return bias[:, None, :].broadcast_to([P, DG, P])

            def roots(it, j, late):
                parts = [i for i, skew in enumerate((LN, LN2)) if at(it, j, skew + late) is not None]
                return (j - late) % 7, parts, DRING * it + (j - late) - LN + 1

            @block.sync
            def _(sp):
                def step(it, j):
                    g = at(it, j, 0)
                    if g is not None:
                        wait_apart(sp, x2_set, g - DRING + 1)
                        sp.dma_start(x[:, j % DRING, :, :].rearrange("p k c -> p (k c)"), node_rows(self.ins["x"], g)).then_inc(x_loaded[j % DRING], 16)
                    for skew, ready, ring, stored, table in (
                            (T1, h0_set, h0, h0_stored, self.h0_table),
                            (T2, p1_out_set, p1_out, p1_stored, self.p1_table),
                            (NORM2, res_set, res, res_stored, self.out),
                            (STORE2, h2_set, h2, h2_stored, self.h2_table)):
                        g = at(it, j, skew)
                        if g is None:
                            continue
                        s = (j - skew) % 7
                        wait_apart(sp, ready, g + 1)
                        sp.dma_start(node_rows(table, g), ring[:, s, :]).then_inc(stored[s], 16)

                turns(sp, DTURNS, DRING, step, DRAIN)
                for stored in (h0_stored, p1_stored, h2_stored, res_stored):
                    for s in range(7):
                        sp.wait_ge(stored[s], 16 * D // 7)

            @block.vector
            def _(v):
                def step(it, j):
                    h = at(it, j, H1T)
                    if h is not None:
                        r1 = (j - H1T) % 2
                        wait_for(v, t2_done, h + 1)
                        wait_for(v, p2_done, h - 1)
                        nc.vector.tensor_scalar(h1t[:, r1, :], t2[r1][:, :], 0.0, self.b1_col[:, :], ALU.max, ALU.add).then_inc(h1t_set, 1)
                    g = at(it, j, LN)
                    if g is not None:
                        s, b = (j - LN) % DRING, (j - LN) % 7
                        wait_for(v, x_loaded[s], 16 * used(it, j, LN, DRING) + 16)
                        for k in range(DG):
                            last = nc.vector.bn_stats(stats[:, b, k, :], x[:, s, k, :])
                        last.then_inc(stats_set, 1)
                    q = at(it, j, LN2)
                    if q is not None:
                        r2 = (j - LN2) % 7
                        wait_for(v, p2_done, q + 1)
                        wait_for(v, h2_set, q - 6)
                        nc.vector.tensor_tensor(x2[:, r2, :, :], tiles(p2[(j - LN2) % 2][:, :]), each(self.b2), ALU.add).then_inc(x2_set, 1)
                    if g is not None:
                        wait_apart(v, stats_set, g + 1)
                        for k in range(DG):
                            last = nc.vector.bn_aggr(mv[:, j % 7, 0, k, :], stats[:, b, k, :])
                        last.then_inc(mv_set, 1)
                    if q is not None:
                        wait_for(v, x2_set, q + 1)
                        for k in range(DG):
                            last = nc.vector.bn_stats(stats2[:, r2, k, :], x2[:, r2, k, :])
                        last.then_inc(stats2_set, 1)
                    if q is not None:
                        wait_apart(v, stats2_set, q + 1)
                        for k in range(DG):
                            last = nc.vector.bn_aggr(mv[:, j % 7, 1, k, :], stats2[:, r2, k, :])
                        last.then_inc(mv2_set, 1)
                        wait_for(v, res_stored[r2], 16 * used(it, j, LN2, 7))
                        nc.vector.tensor_tensor(tiles(res[:, r2, :]), x2[:, r2, :, :], each(self.gb[2]), ALU.add).then_inc(res_set, 1)
                    e, parts, count = roots(it, j, NORM - LN)
                    if parts:
                        wait_for(v, std_set, count)
                        nc.vector.reciprocal(rstd[:, e, parts[0]:parts[-1] + 1], std[:, e, parts[0]:parts[-1] + 1]).then_inc(rstd_set, 1)
                        wait_for(v, rstd_set, count)
                        nc.vector.scalar_tensor_tensor(out=shift[:, e, parts[0]:parts[-1] + 1], in0=mv[:, e, parts[0]:parts[-1] + 1, :, 0], scalar=-1.0,
                                                       in1=rstd[:, e, parts[0]:parts[-1] + 1], op0=ALU.mult, op1=ALU.mult).then_inc(shift_set, 1)

                turns(v, DTURNS, DRING, step, DRAIN)
                v.wait_ge(rows_copied, TILES // U)
                nc.vector.tensor_scalar(is_slot[:, :], self.state_idx[:, :], float(NP), None, ALU.is_ge)
                nc.vector.tensor_scalar(own_f[:, :], self.slot_row[:, :], -float(NP), None, ALU.add)
                nc.vector.tensor_scalar(slot_f[:, :], self.state_idx[:, :], float(EP - NP), None, ALU.add).then_inc(pick, 1)
                v.wait_ge(pick, 1)
                nc.vector.tensor_tensor(step_f[:, :], slot_f[:, :], own_f[:, :], ALU.subtract).then_inc(pick, 1)
                v.wait_ge(pick, 2)
                nc.vector.tensor_tensor(pick_f[:, :], step_f[:, :], is_slot[:, :], ALU.mult).then_inc(pick, 1)
                v.wait_ge(pick, 3)
                nc.vector.tensor_tensor(self.local_idx[:, :], pick_f[:, :], own_f[:, :], ALU.add).then_inc(pick, 1)

            @block.scalar
            def _(act):
                def step(it, j):
                    g = at(it, j, H0)
                    if g is not None:
                        s, b = (j - H0) % DRING, (j - H0) % 7
                        wait_for(act, shift_set, g + 1)
                        e = (j - (H0 - LN)) % 7
                        wait_for(act, h0_stored[b], 16 * used(it, j, H0, 7))
                        wait_for(act, t1_done, g - 6)
                        for k in range(DG):
                            last = nc.scalar.activation(h0[:, b, k * P:(k + 1) * P], x[:, s, k, :], ACT.Relu,
                                                        bias=shift[:, e, 0, k:k + 1], scale=rstd[:, e, 0, k:k + 1])
                        last.then_inc(h0_set, 1)
                    g = at(it, j, H0T)
                    if g is not None:
                        s = (j - H0T) % 2
                        wait_for(act, t1_done, g + 1)
                        wait_for(act, p1_done, g - 1)
                        nc.scalar.activation(h0t[:, s, :], t1[s][:, :], ACT.Copy).then_inc(h0t_set, 1)
                    g = at(it, j, H1)
                    if g is not None:
                        wait_for(act, p1_done, g + 1)
                        wait_for(act, t2_done, g - 6)
                        wait_for(act, p1_stored[(j - H1) % 7], 16 * used(it, j, H1, 7))
                        nc.scalar.activation(p1_out[:, (j - H1) % 7, :], p1[(j - H1) % 2][:, :], ACT.Copy).then_inc(p1_out_set, 1)
                    g = at(it, j, H2)
                    if g is not None:
                        b = (j - H2) % 7
                        wait_for(act, shift_set, g + 1 + LN2 - LN)
                        e = (j - (H2 - LN2)) % 7
                        wait_for(act, h2_stored[b], 16 * used(it, j, H2, 7))
                        for k in range(DG):
                            last = nc.scalar.activation(h2[:, b, k * P:(k + 1) * P], x2[:, b, k, :], ACT.Relu,
                                                        bias=shift[:, e, 1, k:k + 1], scale=rstd[:, e, 1, k:k + 1])
                        last.then_inc(h2_set, 1)
                    e, parts, _ = roots(it, j, 0)
                    if parts:
                        for i, skew, ready in ((0, LN, mv_set), (1, LN2, mv2_set)):
                            if i in parts:
                                wait_for(act, ready, at(it, j, skew) + 1)
                        nc.scalar.activation(std[:, e, parts[0]:parts[-1] + 1], mv[:, e, parts[0]:parts[-1] + 1, :, 1],
                                             ACT.Sqrt, bias=self.eps[:, :]).then_inc(std_set, 1)

                turns(act, DTURNS, DRING, step, DRAIN)

            @block.tensor
            def _(pe):
                def step(it, j):
                    g = at(it, j, T1)
                    if g is not None:
                        s = (j - T1) % 2
                        wait_for(pe, h0_set, g + 1)
                        wait_for(pe, h0t_set, g - 1)
                        for k in range(DG):
                            last = nc.tensor.transpose(t1[s][:, k * P:(k + 1) * P], h0[:, (j - T1) % 7, k * P:(k + 1) * P], self.ident[:, :])
                        last.then_inc(t1_done, 1)
                    g = at(it, j, P1)
                    if g is not None:
                        s = (j - P1) % 2
                        wait_for(pe, h0t_set, g + 1)
                        wait_for(pe, p1_out_set, g - 1)
                        for k in range(DG):
                            last = nc.tensor.matmul(p1[s][:, k * P:(k + 1) * P], h0t[:, s, k * P:(k + 1) * P], self.sw1[:, :],
                                                    start=True, stop=True)
                        last.then_inc(p1_done, 1)
                    g = at(it, j, T2)
                    if g is not None:
                        s = (j - T2) % 2
                        wait_for(pe, p1_out_set, g + 1)
                        wait_for(pe, h1t_set, g - 1)
                        for k in range(DG):
                            last = nc.tensor.transpose(t2[s][:, k * P:(k + 1) * P], p1_out[:, (j - T2) % 7, k * P:(k + 1) * P], self.ident[:, :])
                        last.then_inc(t2_done, 1)
                    g = at(it, j, P2)
                    if g is not None:
                        s = (j - P2) % 2
                        wait_for(pe, h1t_set, g + 1)
                        wait_for(pe, x2_set, g - 1)
                        nc.tensor.matmul(p2[s][:, :], self.ident[:, :], x[:, (j - P2) % DRING, :, :].rearrange("p k c -> p (k c)"),
                                         start=True, stop=False)
                        for k in range(DG):
                            last = nc.tensor.matmul(p2[s][:, k * P:(k + 1) * P], h1t[:, s, k * P:(k + 1) * P], self.sw2[:, :],
                                                    start=False, stop=(k == DG - 1))
                        last.then_inc(p2_done, 1)

                turns(pe, DTURNS, DRING, step, DRAIN)

            @block.gpsimd
            def _(pool):
                G = TILES // U

                def put(it, h):
                    g = 2 * it + h
                    wait_for(pool, slots_put[h], 16 * U * it)
                    pool.tensor_copy(id_now[:, h, :], self.end_idx[:, bass.ds(g * U, U)])
                    pool.tensor_copy(row_now[:, h, :], self.slot_row[:, bass.ds(g * U, U)]).then_inc(staged, 1)
                    pool.wait_ge(staged, g + 1)
                    pool.nop(nofuse=True)
                    for k in range(U):
                        pool.indirect_dma_start(self.row_of_node[:, :], bass.IndirectOffsetOnAxis(ap=id_now[:, h, k:k + 1], axis=0),
                                                row_now[:, h, k:k + 1], None, bounds_check=NP - 1, oob_is_err=False).then_inc(slots_put[h], 16)

                def keep(it, h):
                    g = 2 * it + h
                    wait_for(pool, slots_got[h], 16 * U * it + 16 * U)
                    pool.tensor_copy(self.state_idx[:, bass.ds(g * U, U)], row_got[:, h, :]).then_inc(rows_copied, 1)

                def get(it, h):
                    g = 2 * it + h
                    wait_for(pool, rows_copied, g - 1)
                    pool.tensor_copy(id_now[:, h, :], self.ends_idx[:, bass.ds(g * U, U), 0]).then_inc(staged, 1)
                    pool.wait_ge(staged, G + g + 1)
                    pool.nop(nofuse=True)
                    for k in range(U):
                        pool.indirect_dma_start(row_got[:, h, k:k + 1], None, self.row_of_node[:, :],
                                                bass.IndirectOffsetOnAxis(ap=id_now[:, h, k:k + 1], axis=0)).then_inc(slots_got[h], 16)

                put(0, 0)
                put(0, 1)
                with pool.Fori(1, TURNS) as it:
                    put(it, 0)
                    put(it, 1)
                for h in range(2):
                    pool.wait_ge(slots_put[h], 16 * U * TURNS)
                get(0, 0)
                get(0, 1)
                with pool.Fori(1, TURNS) as it:
                    keep(it - 1, 0)
                    get(it, 0)
                    keep(it - 1, 1)
                    get(it, 1)
                keep(TURNS - 1, 0)
                keep(TURNS - 1, 1)

    def relational(self, layer):
        nc, first = self.nc, layer == 1
        with ExitStack() as ctx:
            def sb(name, shape, dt=F32):
                return ctx.enter_context(nc.sbuf_tensor(f"r{layer}_{name}", shape, dt))

            sems = []

            def sem(name):
                sems.append(nc.alloc_semaphore(f"r{layer}_{name}"))
                return sems[-1]

            src_h = sb("src_h", [P, RING, P])
            dst_row = sb("dst_row", [P, RING, P])
            dst_p1 = None if first else sb("dst_p1", [P, RING, P])
            half_bc = sb("half_bc", [P, RING, P])
            ht_masked = sb("ht_masked", [P, 2, R // 2, P])
            ht_relu = None if first else sb("ht_relu", [P, 2, 2 * P])
            ht = None if first else sb("ht", [P, 7, 2 * P])
            odd = sb("odd", [P, 2, P])
            msg = sb("msg", [P, 2, P])
            same = sb("same", [P, 7, P])
            agg_t = sb("agg_t", [P, 2, P])
            out_x = None if first else sb("out_x", [P, RING, P])
            out_h = sb("out_h", [P, RING, P])
            stats = sb("stats", [P, 7, 6])
            mv = sb("mv", [P, 7, 2])
            std = sb("std", [P, 7])
            rstd = sb("rstd", [P, 7])
            shift = sb("shift", [P, 7])
            idx_now = sb("idx_now", [P, RING, 2], I32)
            t_ps = [ctx.enter_context(nc.psum_tensor(f"r{layer}_t_ps{i}", [P, 512], F32)) for i in range(2)]
            y_ps = [ctx.enter_context(nc.psum_tensor(f"r{layer}_y_ps{i}", [P, 512], F32)) for i in range(2)]
            a_ps = [ctx.enter_context(nc.psum_tensor(f"r{layer}_a_ps{i}", [P, 512], F32)) for i in range(2)]
            p_ps = [ctx.enter_context(nc.psum_tensor(f"r{layer}_p_ps{i}", [P, 512], F32)) for i in range(2)]

            src_got = [sem(f"src_got{i}") for i in range(RING)]
            dst_got = [sem(f"dst_got{i}") for i in range(RING)]
            dst_p1_loaded = [sem(f"dst_p1_loaded{i}") for i in range(2)]
            half_loaded = [sem(f"half_loaded{i}") for i in range(2)]
            x_stored = [sem(f"x_stored{i}") for i in range(2)]
            h_stored = [sem(f"h_stored{i}") for i in range(2)]
            dst_loaded = [sem(f"dst_loaded{i}") for i in range(2)]
            staged, front_set = sem("staged"), sem("front")
            stats_set, mv_set, std_set, rstd_set, shift_set = (
                sem("stats"), sem("mv"), sem("std"), sem("rstd"), sem("shift"))
            t_done, masked_set, ht_set, y_done, odd_set, msg_set, same_set = (
                sem("t_done"), sem("masked"), sem("ht"), sem("y_done"), sem("odd"), sem("msg"), sem("same"))
            joins_set, agg_done, agg_set, p_done, relu_set, xb_set, x_set, h_set = (
                sem("joins"), sem("agg_done"), sem("agg_set"), sem("p_done"), sem("relu"), sem("xb"), sem("x"), sem("h"))
            ctx.callback(self.free, sems)
            block = ctx.enter_context(nc.Block())

            w = self.w1 if first else self.w2
            T, BIAS, MASK, Y, PICK, AGG, CARRY, SELF, OUT, STATS, NORM, RELU = (
                4 if first else 3, 4, 5, 6, 7, 8, 9, 10, 11, 12, 13, 14)
            DRAIN = OUT + 2 if first else RELU + 1
            at = lambda it, j, skew: tile_at(it, j, skew, RING, TILES)
            used = lambda it, j, skew, ring: use_of(it, j, skew, ring, RING)

            def slot_rows(table, g):
                return table[bass.ds(g * (U * P), U * P), :].rearrange("(p k) c -> p (k c)", k=U)

            def slots(t, hf):
                return t[:, hf * U:(hf + 1) * U, :].rearrange("p k c -> p (k c)")

            p1_slots = self.p1_table[NP:NP + EP, :]
            h_out = p1_slots if first else self.h2_table[NP:NP + EP, :]

            @block.gpsimd
            def _(pool):
                src_table = self.h0_table if first else self.p1_table
                dst_table = self.p1_table[0:NP, :] if first else self.ins["x"]

                def step(it, j):
                    n = at(it, j, 0)
                    if n is None:
                        return
                    wait_apart(pool, staged, n + 1)
                    pool.indirect_dma_start(src_h[:, j, :], None, src_table[:, :],
                                            bass.IndirectOffsetOnAxis(ap=idx_now[:, j, 0:1], axis=0)).then_inc(src_got[j], 16)
                    pool.indirect_dma_start(dst_row[:, j, :], None, dst_table[:, :],
                                            bass.IndirectOffsetOnAxis(ap=idx_now[:, j, 1:2], axis=0)).then_inc(dst_got[j], 16)

                turns(pool, TURNS, RING, step, 0)

            @block.sync
            def _(sp):
                def load(it, hf):
                    g = 2 * it + hf
                    if not first:
                        wait_apart(sp, t_done, U * g - U)
                        sp.dma_start(slots(dst_p1, hf), slot_rows(p1_slots, g)).then_inc(dst_p1_loaded[hf], 16)
                    wait_apart(sp, masked_set, U * g - U)
                    if first:
                        sp.dma_start(self.dst_bc[:, bass.ds(g * (U * P) + 1, U * P)], self.dst_f[bass.ds(g * (U * P) + 1, U * P)]
                                     .rearrange("(a e) -> a e", a=1).broadcast_to([P, U * P])).then_inc(dst_loaded[hf], 16)
                    sp.dma_start(slots(half_bc, hf), self.half_f[bass.ds(g * (U * P), U * P)].rearrange("(a e) -> a e", a=1)
                                 .broadcast_to([P, U * P])).then_inc(half_loaded[hf], 16)

                def store(it, hf):
                    g = 2 * it + hf
                    if not first:
                        wait_apart(sp, x_set, U * g + U)
                        sp.dma_start(slot_rows(self.x2_slots, g), slots(out_x, hf)).then_inc(x_stored[hf], 16)
                    wait_apart(sp, h_set, U * g + U)
                    sp.dma_start(slot_rows(h_out, g), slots(out_h, hf)).then_inc(h_stored[hf], 16)

                load(0, 0)
                load(0, 1)
                with sp.Fori(1, TURNS) as it:
                    load(it, 0)
                    store(it - 1, 0)
                    load(it, 1)
                    store(it - 1, 1)
                store(TURNS - 1, 0)
                store(TURNS - 1, 1)
                for hf in range(2):
                    if not first:
                        sp.wait_ge(x_stored[hf], 16 * TURNS)
                    sp.wait_ge(h_stored[hf], 16 * TURNS)

            @block.vector
            def _(v):
                if first:
                    nc.vector.memset(self.dst_bc[:, 0:1], -1.0).then_inc(front_set, 1)

                def masks(it, j):
                    n = at(it, j, MASK)
                    if n is None:
                        return
                    s = (j - MASK) % 7
                    wait_for(v, agg_done, n - 6)
                    if first:
                        wait_for(v, dst_loaded[(j - MASK) % RING // U], 16 * used(it, j, MASK, RING) + 16)
                    edges = self.dst_bc[:, bass.ds(n * P + 1, P)]
                    nc.vector.tensor_scalar(same[:, s, :], edges, self.dst_col[:, bass.ds(n, 1)], None, ALU.is_equal).then_inc(same_set, 1)
                    if first:
                        wait_for(v, front_set, 1 if isinstance(n, int) and n == 0 else 0)
                        nc.vector.tensor_scalar(self.joins[:, bass.ds(n * P, P)], edges, self.dst_bc[:, bass.ds(n * P, 1)],
                                                None, ALU.is_equal).then_inc(joins_set, 1)

                def step(it, j):
                    k = at(it, j, NORM)
                    if not first and k is not None:
                        b = (j - NORM) % 7
                        wait_for(v, std_set, k + 1)
                        nc.vector.reciprocal(rstd[:, b:b + 1], std[:, b:b + 1]).then_inc(rstd_set, 1)
                    m = at(it, j, STATS)
                    if not first and m is not None:
                        c = (j - STATS) % RING
                        wait_for(v, x_set, m + 1)
                        nc.vector.bn_stats(stats[:, c % 7, :], out_x[:, c, :]).then_inc(stats_set, 1)
                    n = at(it, j, PICK)
                    if n is not None:
                        s = (j - PICK) % 2
                        wait_for(v, odd_set, n + 1)
                        wait_for(v, agg_done, n - 1)
                        nc.vector.scalar_tensor_tensor(out=msg[:, s, :], in0=y_ps[s][:, 0:P], scalar=self.even_col[:, bass.ds(n, 1)],
                                                       in1=odd[:, s, :], op0=ALU.mult, op1=ALU.add).then_inc(msg_set, 1)
                    if not first and k is not None:
                        wait_for(v, rstd_set, k + 1)
                        nc.vector.scalar_tensor_tensor(out=shift[:, b:b + 1], in0=mv[:, b, 0:1], scalar=-1.0, in1=rstd[:, b:b + 1],
                                                       op0=ALU.mult, op1=ALU.mult).then_inc(shift_set, 1)
                    n = at(it, j, CARRY)
                    if n is not None:
                        s = (j - CARRY) % 2
                        if isinstance(n, int) and n == 0:
                            nc.vector.memset(agg_t[:, 1, :], 0.0).then_inc(agg_set, 1)
                        wait_for(v, agg_done, n + 1)
                        if first:
                            wait_for(v, joins_set, n + 1)
                        wait_for(v, agg_set, n + 1)
                        wait_for(v, p_done, n - 1)
                        nc.vector.scalar_tensor_tensor(out=agg_t[:, s, :], in0=self.joins[:, bass.ds(n * P, P)],
                                                       scalar=agg_t[:, 1 - s, P - 1:P],
                                                       in1=a_ps[s][:, 0:P], op0=ALU.mult, op1=ALU.add).then_inc(agg_set, 1)
                    if not first and m is not None:
                        wait_apart(v, stats_set, m + 1)
                        nc.vector.bn_aggr(mv[:, c % 7, :], stats[:, c % 7, :]).then_inc(mv_set, 1)
                    n = at(it, j, OUT)
                    if n is not None:
                        s, r, u = (j - OUT) % 2, (j - OUT) % RING, used(it, j, OUT, RING)
                        wait_for(v, p_done, n + 1)
                        if first:
                            wait_for(v, dst_got[r], 16 * u + 16)
                            wait_for(v, h_stored[r // U], 16 * u)
                            nc.vector.tensor_tensor(out_h[:, r, :], p_ps[s][:, 0:P], dst_row[:, r, :], ALU.add).then_inc(h_set, 1)
                        else:
                            wait_for(v, x_stored[r // U], 16 * u)
                            wait_for(v, xb_set, n + 1)
                            nc.vector.tensor_tensor(out_x[:, r, :], p_ps[s][:, 0:P], dst_row[:, r, :], ALU.add).then_inc(x_set, 1)
                    masks(it, j)
                    n = at(it, j, MASK)
                    if n is not None:
                        s, r, u = (j - MASK) % 2, (j - MASK) % RING, used(it, j, MASK, RING)
                        wait_for(v, t_done if first else ht_set, n + 1)
                        of = t_ps[s][:, 0:P] if first else ht[:, r % 7, 0:P]
                        wait_for(v, y_done, n - 1)
                        wait_for(v, half_loaded[r // U], 16 * u + 16)
                        for q in range(R // 2):
                            last = nc.vector.scalar_tensor_tensor(out=ht_masked[:, s, q, :], in0=half_bc[:, r, :], scalar=float(q),
                                                                  in1=of, op0=ALU.is_equal, op1=ALU.mult)
                        last.then_inc(masked_set, 1)
                    n = at(it, j, Y)
                    if not first and n is not None:
                        r, u = (j - Y) % RING, used(it, j, Y, RING)
                        wait_for(v, dst_got[r], 16 * u + 16)
                        nc.vector.tensor_tensor(dst_row[:, r, :], dst_row[:, r, :], self.b2[:, :], ALU.add).then_inc(xb_set, 1)

                turns(v, TURNS, RING, step, DRAIN)

            @block.scalar
            def _(act):
                def step(it, j):
                    n = at(it, j, 0)
                    if n is not None:
                        wait_for(act, t_done, n - RING + 1)
                        wait_for(act, h_set if first else x_set, n - RING + 1)
                        if first:
                            nc.scalar.copy(idx_now[:, j, :], self.ends_idx[:, bass.ds(n, 1), :].rearrange("p a k -> p (a k)")).then_inc(staged, 1)
                        else:
                            nc.scalar.copy(idx_now[:, j, 0:1], self.state_idx[:, bass.ds(n, 1)])
                            nc.scalar.copy(idx_now[:, j, 1:2], self.ends_idx[:, bass.ds(n, 1), 1]).then_inc(staged, 1)
                    n = at(it, j, PICK)
                    if n is not None:
                        s = (j - PICK) % 2
                        wait_for(act, y_done, n + 1)
                        wait_for(act, msg_set, n - 1)
                        nc.scalar.activation(odd[:, s, :], y_ps[s][:, P:2 * P], ACT.Copy,
                                             scale=self.odd_col[:, bass.ds(n, 1)]).then_inc(odd_set, 1)
                    if first:
                        return
                    n = at(it, j, RELU)
                    if n is not None:
                        r, b = (j - RELU) % RING, (j - RELU) % 7
                        wait_for(act, shift_set, n + 1)
                        wait_for(act, h_stored[r // U], 16 * used(it, j, RELU, RING))
                        nc.scalar.activation(out_h[:, r, :], out_x[:, r, :], ACT.Relu, bias=shift[:, b:b + 1],
                                             scale=rstd[:, b:b + 1]).then_inc(h_set, 1)
                    n = at(it, j, STATS)
                    if n is not None:
                        b = (j - STATS) % 7
                        wait_for(act, mv_set, n + 1)
                        nc.scalar.activation(std[:, b:b + 1], mv[:, b, 1:2], ACT.Sqrt, bias=self.eps[:, :]).then_inc(std_set, 1)
                    n = at(it, j, BIAS)
                    if n is not None:
                        s, b = (j - BIAS) % 2, (j - BIAS) % 7
                        wait_for(act, t_done, n + 1)
                        nc.scalar.activation(ht_relu[:, s, :], t_ps[s][:, 0:2 * P], ACT.Relu).then_inc(relu_set, 1)
                        wait_for(act, relu_set, n + 1)
                        wait_for(act, p_done, n - 6)
                        wait_for(act, masked_set, n - 6)
                        nc.scalar.activation(ht[:, b, :], ht_relu[:, s, :], ACT.Identity, bias=self.b1_col[:, :]).then_inc(ht_set, 1)

                turns(act, TURNS, RING, step, DRAIN)

            @block.tensor
            def _(pe):
                def step(it, j):
                    n = at(it, j, AGG)
                    if n is not None:
                        s = (j - AGG) % 2
                        wait_for(pe, msg_set, n + 1)
                        wait_for(pe, same_set, n + 1)
                        wait_for(pe, agg_set, n)
                        nc.tensor.matmul(a_ps[s][:, 0:P], msg[:, s, :], same[:, (j - AGG) % 7, :], start=True, stop=True).then_inc(agg_done, 1)
                    n = at(it, j, SELF)
                    if n is not None:
                        s = (j - SELF) % 2
                        wait_for(pe, agg_set, n + 2)
                        if first:
                            wait_for(pe, h_set, n - 1)
                            nc.tensor.transpose(p_ps[s][:, 0:P], agg_t[:, s, :], self.ident[:, :]).then_inc(p_done, 1)
                        else:
                            wait_for(pe, ht_set, n + 1)
                            wait_for(pe, x_set, n - 1)
                            nc.tensor.matmul(p_ps[s][:, 0:P], ht[:, (j - SELF) % 7, P:2 * P], self.sw2[:, :], start=True, stop=False)
                            nc.tensor.matmul(p_ps[s][:, 0:P], agg_t[:, s, :], self.ident[:, :], start=False, stop=True).then_inc(p_done, 1)
                    n = at(it, j, Y)
                    if n is not None:
                        s = (j - Y) % 2
                        wait_for(pe, masked_set, n + 1)
                        wait_for(pe, msg_set, n - 1)
                        for q in range(R // 2):
                            last = nc.tensor.matmul(y_ps[s][:, 0:2 * P], ht_masked[:, s, q, :],
                                                    w[:, 2 * q:2 * q + 2, :].rearrange("c r o -> c (r o)"),
                                                    start=(q == 0), stop=(q == R // 2 - 1))
                        last.then_inc(y_done, 1)
                    n = at(it, j, T)
                    if n is not None:
                        s, r, u = (j - T) % 2, (j - T) % RING, used(it, j, T, RING)
                        wait_for(pe, src_got[r], 16 * u + 16)
                        wait_for(pe, masked_set if first else relu_set, n - 1)
                        last = nc.tensor.transpose(t_ps[s][:, 0:P], src_h[:, r, :], self.ident[:, :])
                        if not first:
                            wait_for(pe, dst_p1_loaded[r // U], 16 * u + 16)
                            last = nc.tensor.transpose(t_ps[s][:, P:2 * P], dst_p1[:, r, :], self.ident[:, :])
                        last.then_inc(t_done, 1)

                turns(pe, TURNS, RING, step, DRAIN)

    def conv(self, layer):
        nc, last_layer = self.nc, layer == 5
        with ExitStack() as ctx:
            def sb(name, shape, dt=F32):
                return ctx.enter_context(nc.sbuf_tensor(f"c{layer}_{name}", shape, dt))

            sems = []

            def sem(name):
                sems.append(nc.alloc_semaphore(f"c{layer}_{name}"))
                return sems[-1]

            src_h = sb("src_h", [P, RING, P])
            edge = sb("edge", [P, RING, P])
            res = sb("res", [P, RING, P])
            same = sb("same", [P, 2, P])
            agg_t = sb("agg_t", [P, 2, P])
            out_h = sb("out_h", [P, RING, P])
            local_h = None if last_layer else sb("local_h", [P, RING, P])
            idx_now = sb("idx_now", [P, RING, 2], I32)
            a_ps = [ctx.enter_context(nc.psum_tensor(f"c{layer}_a_ps{i}", [P, 512], F32)) for i in range(2)]
            p_ps = [ctx.enter_context(nc.psum_tensor(f"c{layer}_p_ps{i}", [P, 512], F32)) for i in range(2)]

            gathered = [sem(f"gathered{i}") for i in range(RING)]
            scattered = [sem(f"scattered{i}") for i in range(RING)] if last_layer else None
            edge_loaded = [sem(f"edge_loaded{i}") for i in range(2)]
            res_loaded = [sem(f"res_loaded{i}") for i in range(2)]
            out_stored = [sem(f"out_stored{i}") for i in range(2)]
            local_stored = [sem(f"local_stored{i}") for i in range(2)]
            staged, same_set, agg_done, agg_set, p_done, out_set, out_relu, local_set, local_relu, put_staged = (
                sem("staged"), sem("same"), sem("agg_done"), sem("agg_set"), sem("p_done"), sem("out"),
                sem("out_relu"), sem("local"), sem("local_relu"), sem("put_staged"))
            ctx.callback(self.free, sems)
            block = ctx.enter_context(nc.Block())

            source = {3: self.h2_table, 4: self.h3_table, 5: self.h4_table}[layer]
            target = {3: self.h3_table, 4: self.h4_table, 5: None}[layer]
            idx = self.state_idx if layer == 3 else self.local_idx
            residual = {3: self.h2_table[NP:NP + EP, :], 4: self.h3_table[EP:2 * EP, :], 5: self.x2_slots}[layer]
            w, bias = self.gw[layer - 3], self.gb[layer - 3]
            MASKS, AGG, CARRY, SELF, OUT, RELU = 7, 8, 9, 10, 11, 12
            DRAIN = RELU + 1
            at = lambda it, j, skew: tile_at(it, j, skew, RING, TILES)
            used = lambda it, j, skew, ring: use_of(it, j, skew, ring, RING)

            def slot_rows(table, g):
                return table[bass.ds(g * (U * P), U * P), :].rearrange("(p k) c -> p (k c)", k=U)

            def slots(t, hf):
                return t[:, hf * U:(hf + 1) * U, :].rearrange("p k c -> p (k c)")

            @block.gpsimd
            def _(pool):
                def step(it, j):
                    n = at(it, j, 0)
                    if n is not None:
                        wait_for(pool, staged, n + 1)
                        pool.nop(nofuse=True)
                        pool.indirect_dma_start(src_h[:, j, :], None, source[:, :],
                                                bass.IndirectOffsetOnAxis(ap=idx_now[:, j, 0:1], axis=0)).then_inc(gathered[j], 16)
                    n = at(it, j, RELU)
                    if last_layer and n is not None:
                        r = (j - RELU) % RING
                        wait_for(pool, put_staged, n + 1)
                        wait_for(pool, out_set, n + 1)
                        pool.nop(nofuse=True)
                        pool.indirect_dma_start(self.out[:, :], bass.IndirectOffsetOnAxis(ap=idx_now[:, r, 1:2], axis=0),
                                                out_h[:, r, :], None, bounds_check=NP - 1, oob_is_err=False).then_inc(scattered[r], 16)

                turns(pool, TURNS, RING, step, DRAIN if last_layer else 0)
                if last_layer:
                    for r in range(RING):
                        pool.wait_ge(scattered[r], 16 * TURNS)

            @block.sync
            def _(sp):
                def load(it, hf):
                    g = 2 * it + hf
                    wait_apart(sp, agg_done, U * g - U)
                    sp.dma_start(edge[:, hf * U:(hf + 1) * U, :], self.ins["edge"][bass.ds(g * (U * P), U * P), :]
                                 .rearrange("(k p) c -> p k c", p=P)).then_inc(edge_loaded[hf], 16)
                    wait_apart(sp, out_set, U * g - U)
                    sp.dma_start(slots(res, hf), slot_rows(residual, g)).then_inc(res_loaded[hf], 16)

                def store(it, hf):
                    if last_layer:
                        return
                    g = 2 * it + hf
                    wait_apart(sp, local_relu, U * g + U)
                    sp.dma_start(slot_rows(target[0:EP, :], g), slots(local_h, hf)).then_inc(local_stored[hf], 16)
                    wait_apart(sp, out_relu, U * g + U)
                    sp.dma_start(slot_rows(target[EP:2 * EP, :], g), slots(out_h, hf)).then_inc(out_stored[hf], 16)

                load(0, 0)
                load(0, 1)
                with sp.Fori(1, TURNS) as it:
                    load(it, 0)
                    store(it - 1, 0)
                    load(it, 1)
                    store(it - 1, 1)
                store(TURNS - 1, 0)
                store(TURNS - 1, 1)
                if not last_layer:
                    for hf in range(2):
                        sp.wait_ge(local_stored[hf], 16 * TURNS)
                        sp.wait_ge(out_stored[hf], 16 * TURNS)

            @block.vector
            def _(v):
                def step(it, j):
                    n = at(it, j, MASKS)
                    if n is not None:
                        s = (j - MASKS) % 2
                        wait_for(v, agg_done, n - 1)
                        nc.vector.tensor_scalar(same[:, s, :], self.dst_bc[:, bass.ds(n * P + 1, P)], self.dst_col[:, bass.ds(n, 1)],
                                                None, ALU.is_equal).then_inc(same_set, 1)
                    n = at(it, j, CARRY)
                    if n is not None:
                        s = (j - CARRY) % 2
                        if isinstance(n, int) and n == 0:
                            nc.vector.memset(agg_t[:, 1, :], 0.0).then_inc(agg_set, 1)
                        wait_for(v, agg_done, n + 1)
                        wait_for(v, agg_set, n + 1)
                        wait_for(v, p_done, n - 1)
                        nc.vector.scalar_tensor_tensor(out=agg_t[:, s, :], in0=self.joins[:, bass.ds(n * P, P)],
                                                       scalar=agg_t[:, 1 - s, P - 1:P], in1=a_ps[s][:, 0:P],
                                                       op0=ALU.mult, op1=ALU.add).then_inc(agg_set, 1)
                    n = at(it, j, AGG)
                    if n is not None and not last_layer:
                        r, u = (j - AGG) % RING, used(it, j, AGG, RING)
                        wait_for(v, gathered[r], 16 * u + 16)
                        wait_for(v, local_stored[r // U], 16 * u)
                        nc.vector.tensor_tensor(local_h[:, r, :], src_h[:, r, :], bias[:, :], ALU.add).then_inc(local_set, 1)
                    n = at(it, j, OUT)
                    if n is not None:
                        s, r, u = (j - OUT) % 2, (j - OUT) % RING, used(it, j, OUT, RING)
                        wait_for(v, p_done, n + 1)
                        wait_for(v, res_loaded[r // U], 16 * u + 16)
                        if last_layer:
                            wait_for(v, scattered[r], 16 * u)
                        else:
                            wait_for(v, out_stored[r // U], 16 * u)
                        nc.vector.scalar_tensor_tensor(out=out_h[:, r, :], in0=p_ps[s][:, 0:P], scalar=self.isd_col[:, bass.ds(n, 1)],
                                                       in1=res[:, r, :], op0=ALU.mult, op1=ALU.add).then_inc(out_set, 1)

                turns(v, TURNS, RING, step, DRAIN)

            @block.scalar
            def _(act):
                def step(it, j):
                    n = at(it, j, 0)
                    if n is not None:
                        wait_for(act, agg_done, n - RING + 1)
                        if not last_layer:
                            wait_for(act, local_set, n - RING + 1)
                        nc.scalar.copy(idx_now[:, j, 0:1], idx[:, bass.ds(n, 1)]).then_inc(staged, 1)
                    if last_layer:
                        n = at(it, j, OUT)
                        if n is not None:
                            r = (j - OUT) % RING
                            wait_for(act, scattered[r], 16 * used(it, j, OUT, RING))
                            nc.scalar.copy(idx_now[:, r, 1:2], self.end_idx[:, bass.ds(n, 1)]).then_inc(put_staged, 1)
                        return
                    n = at(it, j, CARRY)
                    if n is not None:
                        r = (j - CARRY) % RING
                        wait_for(act, local_set, n + 1)
                        nc.scalar.activation(local_h[:, r, :], local_h[:, r, :], ACT.Relu).then_inc(local_relu, 1)
                    n = at(it, j, RELU)
                    if n is not None:
                        r = (j - RELU) % RING
                        wait_for(act, out_set, n + 1)
                        nc.scalar.activation(out_h[:, r, :], out_h[:, r, :], ACT.Relu).then_inc(out_relu, 1)

                turns(act, TURNS, RING, step, DRAIN)

            @block.tensor
            def _(pe):
                def step(it, j):
                    n = at(it, j, AGG)
                    if n is not None:
                        s, r, u = (j - AGG) % 2, (j - AGG) % RING, used(it, j, AGG, RING)
                        wait_for(pe, gathered[r], 16 * u + 16)
                        wait_for(pe, edge_loaded[r // U], 16 * u + 16)
                        wait_for(pe, same_set, n + 1)
                        wait_for(pe, agg_set, n)
                        nc.tensor.matmul(a_ps[s][:, 0:P], src_h[:, r, :], same[:, s, :], start=True, stop=False)
                        nc.tensor.matmul(a_ps[s][:, 0:P], edge[:, r, :], same[:, s, :], start=False, stop=True).then_inc(agg_done, 1)
                    n = at(it, j, SELF)
                    if n is not None:
                        s = (j - SELF) % 2
                        wait_for(pe, agg_set, n + 2)
                        wait_for(pe, out_set, n - 1)
                        nc.tensor.matmul(p_ps[s][:, 0:P], agg_t[:, s, :], w[:, :], start=True, stop=False)
                        nc.tensor.matmul(p_ps[s][:, 0:P], self.ones[0:1, :], self.gb_row[0:1, layer - 3, :], start=False, stop=True).then_inc(p_done, 1)

                turns(pe, TURNS, RING, step, DRAIN)


def program(nc, ins, out):
    Program(nc, ins, out).build()


def kernel(**inputs):
    import numpy as np
    import concourse.bacc as bacc
    from concourse.bass_utils import run_bass_kernel_spmd as run

    def padded(a, before, after, value):
        a = np.asarray(a)
        front = np.full((before,) + a.shape[1:], value, a.dtype)
        back = np.full((after,) + a.shape[1:], value, a.dtype)
        return np.concatenate([front, a, back])

    extra = EP - E
    dst = padded(inputs["dst"], 0, extra, PAD_NODE)
    arrays = {
        "x": padded(inputs["x"], 0, NP - N, 0),
        "src": padded(inputs["src"], 0, extra, PAD_NODE),
        "dst": padded(dst, 1, 1, -1),
        "typ": padded(inputs["edge_type_8"], 0, extra, 0),
        "edge": padded(inputs["edge_attr_128"], 0, extra, 0),
        "w1": inputs["L0_gnn_w1"], "sw1": inputs["L0_gnn_sw1"], "b1": inputs["L0_gnn_b1"],
        "w2": inputs["L0_gnn_w2"], "sw2": inputs["L0_gnn_sw2"], "b2": inputs["L0_gnn_b2"],
        "W0": inputs["L1_gnn_W0"], "W1": inputs["L1_gnn_W1"], "W2": inputs["L1_gnn_W2"],
        "g0": inputs["L1_gnn_b0"], "g1": inputs["L1_gnn_b1"], "g2": inputs["L1_gnn_b2"],
    }
    arrays = {k: np.ascontiguousarray(v) for k, v in arrays.items()}
    nc = bacc.Bacc("TRN2", target_bir_lowering=False, num_devices=1)
    ins = {k: nc.dram_tensor(f"in_{k}", a.shape, mybir.dt.from_np(a.dtype), kind="ExternalInput").ap()
           for k, a in arrays.items()}
    out = nc.dram_tensor("result", [NP, P], F32, kind="ExternalOutput").ap()
    program(nc, ins, out)
    r = run(nc, [{f"in_{k}": a for k, a in arrays.items()}], core_ids=[0])
    return r.results[0]["result"][:N]
```

```python
from contextlib import ExitStack

import concourse.bass as bass
from concourse import mybir
from concourse.alu_op_type import AluOpType as ALU

ACT = mybir.ActivationFunctionType
F32 = mybir.dt.float32
I32 = mybir.dt.int32
U8 = mybir.dt.uint8

P = 128
N = 50000
E = 25000
R = 8
TILES = 196
EP = TILES * P
U = 7
RING = 2 * U
TURNS = TILES // RING
DG = 4
DRING = 14
DGROUPS = 98
DTURNS = DGROUPS // DRING
NP = DGROUPS * DG * P
PAD_NODE = N
HALF = TILES // 2
SKIP = float(1 << 20)
EPS = 1e-5
assert TILES % RING == 0 and EP >= E and NP > N and DGROUPS % DRING == 0


def turns(eng, count, ring, step, drain):
    for it in range(2):
        for j in range(ring):
            step(it, j)
    with eng.Fori(2, count) as it:
        for j in range(ring):
            step(it, j)
    for j in range(drain):
        step(count + j // ring, j % ring)


def tile_at(it, j, skew, ring, total):
    n = ring * it + (j - skew)
    if isinstance(n, int) and not 0 <= n < total:
        return None
    return n


def use_of(it, j, skew, ring, turn):
    return (turn // ring) * it + (j - skew) // ring


def wait_for(eng, sem, value):
    if isinstance(value, int) and value <= 0:
        return
    eng.wait_ge(sem, value)


def wait_apart(eng, sem, value):
    wait_for(eng, sem, value)
    eng.nop(nofuse=True)


def odd_or_even(a, odd):
    return a.rearrange("p (t o) -> p t o", o=2)[:, :, odd]


class Program:
    def __init__(self, nc, ins, out):
        self.nc, self.ins, self.out = nc, ins, out
        dram = lambda name, shape, dt=F32: nc.dram_tensor(name, shape, dt, kind="Internal").ap()
        self.h0_table = dram("h0_table", [NP, P])
        self.p1_table = dram("p1_table", [NP + EP, P])
        self.h2_table = dram("h2_table", [NP + EP, P])
        self.h3_table = dram("h3_table", [2 * EP, P])
        self.h4_table = dram("h4_table", [2 * EP, P])
        self.x2_slots = dram("x2_slots", [EP, P])
        self.row_of_node = dram("row_of_node", [NP, 1], I32)
        self.dst_f = dram("dst_f", [EP])
        self.pairs = dram("pairs", [TILES, R // 2, P], U8)
        self.joins_row = dram("joins_row", [EP], U8)
        self.count_f = dram("count_f", [EP])

    def free(self, sems):
        self.nc.clear_and_free_semaphores(sems)
        self.nc.all_engine_barrier()

    def build(self):
        nc = self.nc
        with ExitStack() as ctx:
            def sb(name, shape, dt=F32):
                return ctx.enter_context(nc.sbuf_tensor(name, shape, dt))
            self.ident = sb("ident", [P, P])
            self.ones = sb("ones", [P, P])
            self.flip = sb("flip", [P, P])
            self.eps = sb("eps", [P, 1])
            self.sw1 = sb("sw1", [P, P])
            self.sw2 = sb("sw2", [P, P])
            self.w1 = sb("w1", [P, R, P])
            self.w2 = sb("w2", [P, R, P])
            self.gw = [sb(f"gw{i}", [P, P]) for i in range(3)]
            self.gb_row = sb("gb_row", [1, 3, P])
            self.b1_col = sb("b1_col", [P, 1])
            self.b2 = sb("b2", [P, P])
            self.gb = [sb(f"gb{i}", [P, P]) for i in range(3)]
            self.dst_col = sb("dst_col", [P, TILES])
            self.end_idx = sb("end_idx", [P, TILES], I32)
            self.ends_idx = sb("ends_idx", [P, TILES, 2], I32)
            self.slot_row = sb("slot_row", [P, TILES], I32)
            self.state_idx = sb("state_idx", [P, TILES], I32)
            self.local_idx = sb("local_idx", [P, TILES], I32)
            self.odd_col = sb("odd_col", [P, TILES])
            self.even_col = sb("even_col", [P, TILES])
            self.isd_col = sb("isd_col", [P, TILES])
            self.join_col = sb("join_col", [P, TILES])
            self.setup()
            self.dense_and_slots()
            self.dst_bc = sb("dst_bc", [P, EP])
            self.relational(1)
            self.relational(2)
            self.joins = sb("joins", [P, EP], U8)
            self.conv(3)
            self.conv(4)
            self.conv(5)

    def setup(self):
        nc, ins = self.nc, self.ins
        with ExitStack() as ctx:
            def sb(name, shape, dt=F32):
                return ctx.enter_context(nc.sbuf_tensor(name, shape, dt))

            sems = []

            def sem(name):
                sems.append(nc.alloc_semaphore(name))
                return sems[-1]

            dst_r = sb("dst_r", [HALF, 2, P], I32)
            next_r = sb("next_r", [HALF, 2, P], I32)
            src_r = sb("src_r", [HALF, 2, P], I32)
            typ_r = sb("typ_r", [HALF, 2, P], I32)
            half_i = sb("half_i", [HALF, 2, P], I32)
            odd_i = sb("odd_i", [HALF, 2, P], I32)
            dst_rf = sb("dst_rf", [HALF, 2, P])
            next_rf = sb("next_rf", [HALF, 2, P])
            end_rf = sb("end_rf", [HALF, 2, P])
            inner = sb("inner", [HALF, 2, P])
            src_rf = sb("src_rf", [HALF, 2, P])
            before_r = sb("before_r", [HALF, 2], I32)
            before_rf = sb("before_rf", [HALF, 2])
            joins_r = sb("joins_r", [HALF, 2, P], U8)
            pair_r = sb("pair_r", [HALF, 2, R // 2, P], U8)
            odd_rf = sb("odd_rf", [HALF, 2, P])
            dst_q = sb("dst_q", [P, TILES], I32)
            prev_q = sb("prev_q", [P, TILES], I32)
            dst_qf = sb("dst_qf", [P, TILES])
            prev_qf = sb("prev_qf", [P, TILES])
            same_q = sb("same_q", [P, TILES])
            ones_q = sb("ones_q", [P, TILES])
            count_q = sb("count_q", [P, TILES])
            firsts = sb("firsts", [P, P])
            later = sb("later", [P, P])
            reach = sb("reach", [P, P])
            carried = sb("carried", [P, P])
            carry = sb("carry", [P, 1])
            in_first = sb("in_first", [P, TILES])
            count_all = sb("count_all", [P, TILES])
            joined = sb("joined", [P, TILES])
            node_ids = sb("node_ids", [P, NP // P], I32)
            cols_ps = [ctx.enter_context(nc.psum_tensor(f"cols_ps{i}", [P, 512], F32)) for i in range(6)]

            dst_loaded, edges_loaded, weights_loaded = sem("dst_loaded"), sem("edges_loaded"), sem("weights_loaded")
            ident_set, ready_rows, cols_done = sem("ident_set"), sem("ready_rows"), sem("cols_done")
            dve = sem("setup_dve")
            firsts_set, firsts_done, reach_set, carry_done = (
                sem("firsts_set"), sem("firsts_done"), sem("reach_set"), sem("carry_done"))
            rows_stored, count_set, count_stored, ids_set, ids_stored, later_set, ones_set, flip_set = (
                sem("rows_stored"), sem("count_set"), sem("count_stored"), sem("ids_set"), sem("ids_stored"),
                sem("later_set"), sem("ones_set"), sem("flip_set"))
            ctx.callback(self.free, sems)
            block = ctx.enter_context(nc.Block())

            def rows(a):
                return a.rearrange("(i q f) -> q i f", i=2, q=HALF)

            def bc(a):
                return a.rearrange("(a c) -> a c", a=1).broadcast_to([P, P])

            dst_line = ins["dst_line"]

            @block.sync
            def _(sp):
                for to, of, loaded in ((dst_r, ins["dst"], dst_loaded), (next_r, ins["dst_next"], dst_loaded),
                                       (src_r, ins["src"], edges_loaded), (typ_r, ins["typ"], edges_loaded)):
                    sp.dma_start(to[:, :, :], rows(of)).then_inc(loaded, 16)
                sp.dma_start(dst_q[:, :], dst_line[1:EP + 1].rearrange("(p j) -> p j", p=P)).then_inc(edges_loaded, 16)
                sp.dma_start(prev_q[:, :], dst_line[0:EP].rearrange("(p j) -> p j", p=P)).then_inc(edges_loaded, 16)
                sp.dma_start(before_r[:, :], ins["dst_before"]).then_inc(edges_loaded, 16)
                sp.wait_ge(ready_rows, 1)
                sp.dma_start(rows(self.dst_f), dst_rf[:, :, :]).then_inc(rows_stored, 16)
                sp.dma_start(rows(self.joins_row), joins_r[:, :, :]).then_inc(rows_stored, 16)
                sp.dma_start(self.pairs.rearrange("(i q) r f -> q i r f", i=2), pair_r[:, :, :, :]).then_inc(rows_stored, 16)
                sp.wait_ge(count_set, 1)
                sp.dma_start(self.count_f.rearrange("(p j) -> p j", p=P), count_all[:, :]).then_inc(count_stored, 16)
                sp.wait_ge(count_stored, 16)
                sp.wait_ge(rows_stored, 3 * 16)
                sp.wait_ge(weights_loaded, 15 * 16)

            @block.scalar
            def _(act):
                act.wait_ge(dst_loaded, 2 * 16)
                for to, of in ((self.sw1, ins["sw1"]), (self.sw2, ins["sw2"]), (self.gw[0], ins["W0"]),
                               (self.gw[1], ins["W1"]), (self.gw[2], ins["W2"])):
                    act.dma_start(to[:, :], of).then_inc(weights_loaded, 16)
                act.dma_start(self.w1[:, :, :], ins["w1"].rearrange("r c o -> c r o")).then_inc(weights_loaded, 16)
                act.dma_start(self.w2[:, :, :], ins["w2"].rearrange("r c o -> c r o")).then_inc(weights_loaded, 16)
                for to, of in ((self.b2, ins["b2"]), (self.gb[0], ins["g0"]),
                               (self.gb[1], ins["g1"]), (self.gb[2], ins["g2"])):
                    act.dma_start(to[:, :], bc(of)).then_inc(weights_loaded, 16)
                act.dma_start(self.b1_col[:, :], ins["b1"].rearrange("(c a) -> c a", a=1)).then_inc(weights_loaded, 16)
                for i in range(3):
                    act.dma_start(self.gb_row[0:1, i, :], ins[f"g{i}"].rearrange("(a c) -> a c", a=1)).then_inc(weights_loaded, 16)

            @block.gpsimd
            def _(pool):
                pool.memset(self.ident[:, :], 0.0).then_inc(ident_set, 1)
                pool.memset(self.eps[:, :], EPS)
                pool.memset(self.ones[:, :], 1.0).then_inc(ones_set, 1)
                pool.wait_ge(ident_set, 1)
                pool.affine_select(out=self.ident[:, :], in_=self.ident[:, :], compare_op=ALU.not_equal, fill=1.0,
                                   base=0, pattern=[[-1, P]], channel_multiplier=1).then_inc(ident_set, 1)
                pool.memset(self.flip[:, :], 0.0).then_inc(flip_set, 1)
                pool.wait_ge(flip_set, 1)
                pool.affine_select(out=self.flip[:, :], in_=self.flip[:, :], compare_op=ALU.not_equal, fill=1.0,
                                   base=1 - P, pattern=[[1, P]], channel_multiplier=1).then_inc(flip_set, 1)
                pool.wait_ge(ones_set, 1)
                pool.affine_select(out=later[:, :], in_=self.ones[:, :], compare_op=ALU.is_gt, fill=0.0,
                                   base=0, pattern=[[1, P]], channel_multiplier=-1).then_inc(later_set, 1)
                pool.iota(self.slot_row[:, :].rearrange("p (g k) -> p g k", k=U), pattern=[[P * U, TILES // U], [1, U]],
                          base=NP, channel_multiplier=U)
                pool.iota(node_ids[:, :], pattern=[[1, NP // P]], base=0, channel_multiplier=NP // P).then_inc(ids_set, 1)
                pool.wait_ge(ids_set, 1)
                pool.dma_start(self.row_of_node.rearrange("(p j) a -> p (j a)", p=P), node_ids[:, :]).then_inc(ids_stored, 16)
                pool.wait_ge(ids_stored, 16)

            @block.vector
            def _(v):
                done = [0]

                def link(ins_):
                    done[0] += 1
                    ins_.then_inc(dve, 1)
                    v.wait_ge(dve, done[0])

                v.wait_ge(dst_loaded, 2 * 16)
                v.wait_ge(edges_loaded, 5 * 16)
                nc.vector.memset(joined[:, 0:1], 0.0)
                nc.vector.memset(ones_q[:, :], 1.0)
                nc.vector.tensor_scalar(odd_i[:, :, :], typ_r[:, :, :], 1, None, ALU.bitwise_and)
                nc.vector.tensor_scalar(half_i[:, :, :], typ_r[:, :, :], 1, None, ALU.arith_shift_right)
                nc.vector.tensor_copy(dst_rf[:, :, :], dst_r[:, :, :])
                nc.vector.tensor_copy(next_rf[:, :, :], next_r[:, :, :])
                nc.vector.tensor_copy(before_rf[:, :], before_r[:, :])
                nc.vector.tensor_copy(src_rf[:, :, :], src_r[:, :, :])
                nc.vector.tensor_copy(dst_qf[:, :], dst_q[:, :])
                link(nc.vector.tensor_copy(prev_qf[:, :], prev_q[:, :]))
                nc.vector.tensor_copy(odd_rf[:, :, :], odd_i[:, :, :])
                for i in range(2):
                    nc.vector.tensor_scalar(joins_r[:, i, :], dst_rf[:, i, :], before_rf[:, i:i + 1], None, ALU.is_equal)
                for pair in range(R // 2):
                    nc.vector.tensor_scalar(pair_r[:, :, pair, :], half_i[:, :, :], float(pair), None, ALU.is_equal)
                nc.vector.tensor_tensor(inner[:, :, :], dst_rf[:, :, :], next_rf[:, :, :], ALU.is_equal)
                nc.vector.tensor_copy(firsts[:, :], dst_qf[:, 0:1].broadcast_to([P, P])).then_inc(firsts_set, 1)
                link(nc.vector.tensor_tensor(same_q[:, :], dst_qf[:, :], prev_qf[:, :], ALU.is_equal))
                nc.vector.scalar_tensor_tensor(out=end_rf[:, :, :], in0=inner[:, :, :], scalar=SKIP, in1=dst_rf[:, :, :],
                                               op0=ALU.mult, op1=ALU.add).then_inc(ready_rows, 1)
                link(nc.vector.tensor_tensor_scan(count_q[:, :], same_q[:, :], ones_q[:, :], 0.0, ALU.mult, ALU.add))
                v.wait_ge(firsts_done, 1)
                v.wait_ge(later_set, 1)
                link(nc.vector.scalar_tensor_tensor(out=reach[:, :], in0=cols_ps[5][:, 0:P], scalar=dst_qf[:, TILES - 1:TILES],
                                                    in1=later[:, :], op0=ALU.is_equal, op1=ALU.mult))
                nc.vector.tensor_copy(carried[:, :], count_q[:, TILES - 1:TILES].broadcast_to([P, P])).then_inc(reach_set, 1)
                nc.vector.tensor_scalar(in_first[:, :], dst_qf[:, :], dst_qf[:, 0:1], None, ALU.is_equal)
                v.wait_ge(carry_done, 1)
                link(nc.vector.tensor_copy(carry[:, :], cols_ps[4][:, 256:257]))
                nc.vector.scalar_tensor_tensor(out=count_all[:, :], in0=in_first[:, :], scalar=carry[:, :], in1=count_q[:, :],
                                               op0=ALU.mult, op1=ALU.add).then_inc(count_set, 1)
                v.wait_ge(cols_done, 4)
                link(nc.vector.tensor_copy(self.dst_col[:, :], cols_ps[0][:, 0:TILES]))
                link(nc.vector.tensor_tensor(joined[:, 1:TILES], self.dst_col[:, 1:TILES], self.dst_col[:, 0:TILES - 1],
                                             ALU.is_equal))
                v.wait_ge(ident_set, 2)
                nc.vector.tensor_scalar(odd_or_even(self.join_col, 0), odd_or_even(joined, 0), self.ident[:, 0:1], None, ALU.mult)
                nc.vector.tensor_scalar(odd_or_even(self.join_col, 1), odd_or_even(joined, 1), self.ident[:, P - 1:P], None, ALU.mult)
                nc.vector.tensor_copy(self.ends_idx[:, :, 1], cols_ps[0][:, 0:TILES])
                nc.vector.tensor_copy(self.end_idx[:, :], cols_ps[1][:, 0:TILES])
                nc.vector.tensor_copy(self.ends_idx[:, :, 0], cols_ps[2][:, 0:TILES])
                nc.vector.tensor_copy(self.odd_col[:, :], cols_ps[3][:, 0:TILES])
                nc.vector.tensor_scalar(self.even_col[:, :], cols_ps[3][:, 0:TILES], -1.0, 1.0, ALU.mult, ALU.add)
                v.wait_ge(weights_loaded, 15 * 16)
                v.wait_ge(ident_set, 2)
                nc.vector.tensor_tensor(self.sw1[:, :], self.sw1[:, :], self.ident[:, :], ALU.add)

            @block.tensor
            def _(pe):
                pe.wait_ge(ident_set, 2)
                pe.wait_ge(firsts_set, 1)
                nc.tensor.transpose(cols_ps[5][:, 0:P], firsts[:, :], self.ident[:, :]).then_inc(firsts_done, 1)
                pe.wait_ge(ready_rows, 1)
                for n, rows_f in enumerate((dst_rf, end_rf, src_rf, odd_rf)):
                    for i in range(2):
                        last = nc.tensor.transpose(cols_ps[n][:, i * HALF:(i + 1) * HALF], rows_f[:, i, :],
                                                   self.ident[0:HALF, 0:HALF])
                    last.then_inc(cols_done, 1)
                pe.wait_ge(reach_set, 1)
                nc.tensor.matmul(cols_ps[4][:, 256:256 + P], reach[:, :], carried[:, :], start=True, stop=True).then_inc(carry_done, 1)

    def dense_and_slots(self):
        nc = self.nc
        with ExitStack() as ctx:
            def sb(name, shape, dt=F32):
                return ctx.enter_context(nc.sbuf_tensor(name, shape, dt))

            sems = []

            def sem(name):
                sems.append(nc.alloc_semaphore(name))
                return sems[-1]

            W = DG * P
            x = sb("x_ring", [P, DRING, DG, P])
            stats = sb("stats", [P, 7, DG, 6])
            mv = sb("mv", [P, 7, 2, DG, 2])
            std = sb("std", [P, 7, 2, DG])
            rstd = sb("rstd", [P, 7, 2, DG])
            stats2 = sb("stats2", [P, 7, DG, 6])
            shift = sb("shift", [P, 7, 2, DG])
            h0 = sb("h0_ring", [P, 7, W])
            h0t = sb("h0t_ring", [P, 2, W])
            h1t = sb("h1t_ring", [P, 2, W])
            x2 = sb("x2_ring", [P, 7, DG, P])
            p1_out = sb("p1_out_ring", [P, 7, W])
            h2 = sb("h2_ring", [P, 7, W])
            res = sb("res_ring", [P, 7, W])
            t1 = [ctx.enter_context(nc.psum_tensor(f"t1_ps{i}", [P, W], F32)) for i in range(2)]
            p1 = [ctx.enter_context(nc.psum_tensor(f"p1_ps{i}", [P, W], F32)) for i in range(2)]
            t2 = [ctx.enter_context(nc.psum_tensor(f"t2_ps{i}", [P, W], F32)) for i in range(2)]
            p2 = [ctx.enter_context(nc.psum_tensor(f"p2_ps{i}", [P, W], F32)) for i in range(2)]
            id_now = sb("id_now", [P, 2, U], I32)
            row_now = sb("row_now", [P, 2, U], I32)
            row_got = sb("row_got", [P, 2, U], I32)
            is_slot = sb("is_slot", [P, TILES])
            own_f = sb("own_f", [P, TILES])
            slot_f = sb("slot_f", [P, TILES])
            step_f = sb("step_f", [P, TILES])
            pick_f = sb("pick_f", [P, TILES])

            x_loaded = [sem(f"x_loaded{i}") for i in range(DRING)]
            stats_set, mv_set, std_set, rstd_set, h0_set = (
                sem("d_stats"), sem("d_mv"), sem("d_std"), sem("d_rstd"), sem("d_h0"))
            t1_done, h0t_set, p1_done, t2_done, h1t_set, p2_done = (
                sem("d_t1"), sem("d_h0t"), sem("d_p1"), sem("d_t2"), sem("d_h1t"), sem("d_p2"))
            x2_set, stats2_set, mv2_set, h2_set, res_set, shift_set, p1_out_set = (
                sem("d_x2"), sem("d_stats2"), sem("d_mv2"), sem("d_h2"), sem("d_res"), sem("d_shift"), sem("d_p1_out"))
            h0_stored = [sem(f"h0_stored{i}") for i in range(7)]
            p1_stored = [sem(f"p1_stored{i}") for i in range(7)]
            h2_stored = [sem(f"h2_stored{i}") for i in range(7)]
            res_stored = [sem(f"res_stored{i}") for i in range(7)]
            staged = sem("staged")
            slots_put = [sem(f"slots_put{i}") for i in range(2)]
            slots_got = [sem(f"slots_got{i}") for i in range(2)]
            rows_copied, pick = sem("rows_copied"), sem("pick")
            ctx.callback(self.free, sems)
            block = ctx.enter_context(nc.Block())

            D = DGROUPS
            LN, NORM, H0, T1, H0T, P1, H1, T2, H1T, P2, LN2, NORM2, H2, STORE2 = 2, 4, 5, 6, 7, 8, 9, 10, 11, 12, 13, 15, 16, 17
            DRAIN = STORE2 + 1
            at = lambda it, j, skew: tile_at(it, j, skew, DRING, D)
            used = lambda it, j, skew, ring: use_of(it, j, skew, ring, DRING)

            def node_rows(table, g):
                return table[bass.ds(g * (DG * P), DG * P), :].rearrange("(p k) c -> p (k c)", k=DG)

            def tiles(a):
                return a.rearrange("p (k c) -> p k c", k=DG)

            def each(bias):
                return bias[:, None, :].broadcast_to([P, DG, P])

            def roots(it, j, late):
                parts = [i for i, skew in enumerate((LN, LN2)) if at(it, j, skew + late) is not None]
                return (j - late) % 7, parts, DRING * it + (j - late) - LN + 1

            @block.sync
            def _(sp):
                def step(it, j):
                    g = at(it, j, 0)
                    if g is not None:
                        wait_apart(sp, x2_set, g - DRING + 1)
                        sp.dma_start(x[:, j % DRING, :, :].rearrange("p k c -> p (k c)"),
                                     node_rows(self.ins["x"], g)).then_inc(x_loaded[j % DRING], 16)
                    for skew, ready, ring, stored, table in (
                            (T1, h0_set, h0, h0_stored, self.h0_table),
                            (T2, p1_out_set, p1_out, p1_stored, self.p1_table),
                            (NORM2, res_set, res, res_stored, self.out),
                            (STORE2, h2_set, h2, h2_stored, self.h2_table)):
                        g = at(it, j, skew)
                        if g is None:
                            continue
                        s = (j - skew) % 7
                        wait_apart(sp, ready, g + 1)
                        sp.dma_start(node_rows(table, g), ring[:, s, :]).then_inc(stored[s], 16)

                turns(sp, DTURNS, DRING, step, DRAIN)
                for stored in (h0_stored, p1_stored, h2_stored, res_stored):
                    for s in range(7):
                        sp.wait_ge(stored[s], 16 * D // 7)

            @block.vector
            def _(v):
                def step(it, j):
                    e, parts, count = roots(it, j, NORM - LN)
                    if parts:
                        wait_for(v, std_set, count)
                        nc.vector.reciprocal(rstd[:, e, parts[0]:parts[-1] + 1], std[:, e, parts[0]:parts[-1] + 1]).then_inc(rstd_set, 1)
                    h = at(it, j, H1T)
                    if h is not None:
                        r1 = (j - H1T) % 2
                        wait_for(v, t2_done, h + 1)
                        wait_for(v, p2_done, h - 1)
                        nc.vector.tensor_scalar(h1t[:, r1, :], t2[r1][:, :], 0.0, self.b1_col[:, :], ALU.max, ALU.add).then_inc(h1t_set, 1)
                    if parts:
                        wait_for(v, rstd_set, count)
                        nc.vector.scalar_tensor_tensor(out=shift[:, e, parts[0]:parts[-1] + 1],
                                                       in0=mv[:, e, parts[0]:parts[-1] + 1, :, 0], scalar=-1.0,
                                                       in1=rstd[:, e, parts[0]:parts[-1] + 1], op0=ALU.mult, op1=ALU.mult).then_inc(shift_set, 1)
                    g = at(it, j, LN)
                    if g is not None:
                        s, b = (j - LN) % DRING, (j - LN) % 7
                        wait_for(v, x_loaded[s], 16 * used(it, j, LN, DRING) + 16)
                        for k in range(DG):
                            last = nc.vector.bn_stats(stats[:, b, k, :], x[:, s, k, :])
                        last.then_inc(stats_set, 1)
                    q = at(it, j, LN2)
                    if q is not None:
                        r2 = (j - LN2) % 7
                        wait_for(v, p2_done, q + 1)
                        wait_for(v, h2_set, q - 6)
                        nc.vector.tensor_tensor(x2[:, r2, :, :], tiles(p2[(j - LN2) % 2][:, :]), each(self.b2), ALU.add).then_inc(x2_set, 1)
                    if g is not None:
                        wait_apart(v, stats_set, g + 1)
                        for k in range(DG):
                            last = nc.vector.bn_aggr(mv[:, j % 7, 0, k, :], stats[:, b, k, :])
                        last.then_inc(mv_set, 1)
                    if q is not None:
                        wait_for(v, x2_set, q + 1)
                        for k in range(DG):
                            last = nc.vector.bn_stats(stats2[:, r2, k, :], x2[:, r2, k, :])
                        last.then_inc(stats2_set, 1)
                    if q is not None:
                        wait_for(v, res_stored[r2], 16 * used(it, j, LN2, 7))
                        nc.vector.tensor_tensor(tiles(res[:, r2, :]), x2[:, r2, :, :], each(self.gb[2]), ALU.add).then_inc(res_set, 1)
                        wait_apart(v, stats2_set, q + 1)
                        for k in range(DG):
                            last = nc.vector.bn_aggr(mv[:, j % 7, 1, k, :], stats2[:, r2, k, :])
                        last.then_inc(mv2_set, 1)

                turns(v, DTURNS, DRING, step, DRAIN)
                v.wait_ge(rows_copied, TILES // U)
                nc.vector.tensor_scalar(is_slot[:, :], self.state_idx[:, :], float(NP), None, ALU.is_ge)
                nc.vector.tensor_scalar(own_f[:, :], self.slot_row[:, :], -float(NP), None, ALU.add)
                nc.vector.tensor_scalar(slot_f[:, :], self.state_idx[:, :], float(EP - NP), None, ALU.add).then_inc(pick, 1)
                v.wait_ge(pick, 1)
                nc.vector.tensor_tensor(step_f[:, :], slot_f[:, :], own_f[:, :], ALU.subtract).then_inc(pick, 1)
                v.wait_ge(pick, 2)
                nc.vector.tensor_tensor(pick_f[:, :], step_f[:, :], is_slot[:, :], ALU.mult).then_inc(pick, 1)
                v.wait_ge(pick, 3)
                nc.vector.tensor_tensor(self.local_idx[:, :], pick_f[:, :], own_f[:, :], ALU.add).then_inc(pick, 1)

            @block.scalar
            def _(act):
                def step(it, j):
                    g = at(it, j, H0)
                    if g is not None:
                        s, b = (j - H0) % DRING, (j - H0) % 7
                        wait_for(act, shift_set, g + 1)
                        e = (j - (H0 - LN)) % 7
                        wait_for(act, h0_stored[b], 16 * used(it, j, H0, 7))
                        wait_for(act, t1_done, g - 6)
                        for k in range(DG):
                            last = nc.scalar.activation(h0[:, b, k * P:(k + 1) * P], x[:, s, k, :], ACT.Relu,
                                                        bias=shift[:, e, 0, k:k + 1], scale=rstd[:, e, 0, k:k + 1])
                        last.then_inc(h0_set, 1)
                    g = at(it, j, H0T)
                    if g is not None:
                        s = (j - H0T) % 2
                        wait_for(act, t1_done, g + 1)
                        wait_for(act, p1_done, g - 1)
                        nc.scalar.activation(h0t[:, s, :], t1[s][:, :], ACT.Copy).then_inc(h0t_set, 1)
                    g = at(it, j, H1)
                    if g is not None:
                        wait_for(act, p1_done, g + 1)
                        wait_for(act, t2_done, g - 6)
                        wait_for(act, p1_stored[(j - H1) % 7], 16 * used(it, j, H1, 7))
                        nc.scalar.activation(p1_out[:, (j - H1) % 7, :], p1[(j - H1) % 2][:, :], ACT.Copy).then_inc(p1_out_set, 1)
                    g = at(it, j, H2)
                    if g is not None:
                        b = (j - H2) % 7
                        wait_for(act, shift_set, g + 1 + LN2 - LN)
                        e = (j - (H2 - LN2)) % 7
                        wait_for(act, h2_stored[b], 16 * used(it, j, H2, 7))
                        for k in range(DG):
                            last = nc.scalar.activation(h2[:, b, k * P:(k + 1) * P], x2[:, b, k, :], ACT.Relu,
                                                        bias=shift[:, e, 1, k:k + 1], scale=rstd[:, e, 1, k:k + 1])
                        last.then_inc(h2_set, 1)
                    e, parts, _ = roots(it, j, 0)
                    if parts:
                        for i, skew, ready in ((0, LN, mv_set), (1, LN2, mv2_set)):
                            if i in parts:
                                wait_for(act, ready, at(it, j, skew) + 1)
                        nc.scalar.activation(std[:, e, parts[0]:parts[-1] + 1], mv[:, e, parts[0]:parts[-1] + 1, :, 1],
                                             ACT.Sqrt, bias=self.eps[:, :]).then_inc(std_set, 1)

                turns(act, DTURNS, DRING, step, DRAIN)

            @block.tensor
            def _(pe):
                def step(it, j):
                    g = at(it, j, T1)
                    if g is not None:
                        s = (j - T1) % 2
                        wait_for(pe, h0_set, g + 1)
                        wait_for(pe, h0t_set, g - 1)
                        for k in range(DG):
                            last = nc.tensor.transpose(t1[s][:, k * P:(k + 1) * P], h0[:, (j - T1) % 7, k * P:(k + 1) * P], self.ident[:, :])
                        last.then_inc(t1_done, 1)
                    g = at(it, j, P1)
                    if g is not None:
                        s = (j - P1) % 2
                        wait_for(pe, h0t_set, g + 1)
                        wait_for(pe, p1_out_set, g - 1)
                        for k in range(DG):
                            last = nc.tensor.matmul(p1[s][:, k * P:(k + 1) * P], h0t[:, s, k * P:(k + 1) * P], self.sw1[:, :],
                                                    start=True, stop=True)
                        last.then_inc(p1_done, 1)
                    g = at(it, j, T2)
                    if g is not None:
                        s = (j - T2) % 2
                        wait_for(pe, p1_out_set, g + 1)
                        wait_for(pe, h1t_set, g - 1)
                        for k in range(DG):
                            last = nc.tensor.transpose(t2[s][:, k * P:(k + 1) * P], p1_out[:, (j - T2) % 7, k * P:(k + 1) * P], self.ident[:, :])
                        last.then_inc(t2_done, 1)
                    g = at(it, j, P2)
                    if g is not None:
                        s = (j - P2) % 2
                        wait_for(pe, h1t_set, g + 1)
                        wait_for(pe, x2_set, g - 1)
                        nc.tensor.matmul(p2[s][:, :], self.ident[:, :], x[:, (j - P2) % DRING, :, :].rearrange("p k c -> p (k c)"),
                                         start=True, stop=False)
                        for k in range(DG):
                            last = nc.tensor.matmul(p2[s][:, k * P:(k + 1) * P], h1t[:, s, k * P:(k + 1) * P], self.sw2[:, :],
                                                    start=False, stop=(k == DG - 1))
                        last.then_inc(p2_done, 1)

                turns(pe, DTURNS, DRING, step, DRAIN)

            @block.gpsimd
            def _(pool):
                G = TILES // U

                def put(it, h):
                    g = 2 * it + h
                    wait_for(pool, slots_put[h], 16 * U * it)
                    pool.tensor_copy(id_now[:, h, :], self.end_idx[:, bass.ds(g * U, U)])
                    pool.tensor_copy(row_now[:, h, :], self.slot_row[:, bass.ds(g * U, U)]).then_inc(staged, 1)
                    pool.wait_ge(staged, g + 1)
                    pool.nop(nofuse=True)
                    for k in range(U):
                        pool.indirect_dma_start(self.row_of_node[:, :], bass.IndirectOffsetOnAxis(ap=id_now[:, h, k:k + 1], axis=0),
                                                row_now[:, h, k:k + 1], None, bounds_check=NP - 1, oob_is_err=False).then_inc(slots_put[h], 16)

                def keep(it, h):
                    g = 2 * it + h
                    wait_for(pool, slots_got[h], 16 * U * it + 16 * U)
                    pool.tensor_copy(self.state_idx[:, bass.ds(g * U, U)], row_got[:, h, :]).then_inc(rows_copied, 1)

                def get(it, h):
                    g = 2 * it + h
                    wait_for(pool, rows_copied, g - 1)
                    pool.tensor_copy(id_now[:, h, :], self.ends_idx[:, bass.ds(g * U, U), 0]).then_inc(staged, 1)
                    pool.wait_ge(staged, G + g + 1)
                    pool.nop(nofuse=True)
                    for k in range(U):
                        pool.indirect_dma_start(row_got[:, h, k:k + 1], None, self.row_of_node[:, :],
                                                bass.IndirectOffsetOnAxis(ap=id_now[:, h, k:k + 1], axis=0)).then_inc(slots_got[h], 16)

                put(0, 0)
                put(0, 1)
                with pool.Fori(1, TURNS) as it:
                    put(it, 0)
                    put(it, 1)
                for h in range(2):
                    pool.wait_ge(slots_put[h], 16 * U * TURNS)
                get(0, 0)
                get(0, 1)
                with pool.Fori(1, TURNS) as it:
                    keep(it - 1, 0)
                    get(it, 0)
                    keep(it - 1, 1)
                    get(it, 1)
                keep(TURNS - 1, 0)
                keep(TURNS - 1, 1)

    def relational(self, layer):
        nc, first = self.nc, layer == 1
        with ExitStack() as ctx:
            def sb(name, shape, dt=F32):
                return ctx.enter_context(nc.sbuf_tensor(f"r{layer}_{name}", shape, dt))

            sems = []

            def sem(name):
                sems.append(nc.alloc_semaphore(f"r{layer}_{name}"))
                return sems[-1]

            src_h = sb("src_h", [P, RING, P])
            dst_row = sb("dst_row", [P, RING, P])
            dst_p1 = None if first else sb("dst_p1", [P, RING, P])
            pair_bc = sb("pair_bc", [P, RING, R // 2, P], U8)
            ht_masked = sb("ht_masked", [P, 7, R // 2, P])
            ht_relu = None if first else sb("ht_relu", [P, 2, 2 * P])
            ht = None if first else sb("ht", [P, 7, 2 * P])
            odd = sb("odd", [P, 2, P])
            msg = sb("msg", [P, 7, P])
            same = sb("same", [P, 7, P])
            out_x = None if first else sb("out_x", [P, RING, P])
            out_h = sb("out_h", [P, RING, P])
            stats = sb("stats", [P, 7, 6])
            mv = sb("mv", [P, RING, 2])
            std = sb("std", [P, RING])
            rstd = sb("rstd", [P, RING])
            shift = sb("shift", [P, RING])
            idx_now = sb("idx_now", [P, RING, 2], I32)
            count_r = sb("count_r", [HALF, 2, P]) if first else None
            least_one = sb("least_one", [P, TILES]) if first else None
            root = sb("root", [P, TILES]) if first else None
            count_ps = ctx.enter_context(nc.psum_tensor("count_ps", [P, 512], F32)) if first else None
            flip_ps = ctx.enter_context(nc.psum_tensor("flip_ps", [P, 512], F32)) if first else None
            t_ps = [ctx.enter_context(nc.psum_tensor(f"r{layer}_t_ps{i}", [P, 512], F32)) for i in range(2)]
            y_ps = [ctx.enter_context(nc.psum_tensor(f"r{layer}_y_ps{i}", [P, 512], F32)) for i in range(2)]
            a_ps = [ctx.enter_context(nc.psum_tensor(f"r{layer}_a_ps{i}", [P, 512], F32)) for i in range(2)]

            src_got = [sem(f"src_got{i}") for i in range(RING)]
            dst_got = [sem(f"dst_got{i}") for i in range(RING)]
            dst_p1_loaded = [sem(f"dst_p1_loaded{i}") for i in range(2)]
            pair_loaded = [sem(f"pair_loaded{i}") for i in range(2)]
            x_stored = [sem(f"x_stored{i}") for i in range(2)]
            h_stored = [sem(f"h_stored{i}") for i in range(2)]
            dst_loaded = [sem(f"dst_loaded{i}") for i in range(2)]
            staged = sem("staged")
            count_loaded, count_cols, least_set, flip_done, odd_copied, root_set = (
                sem("count_loaded"), sem("count_cols"), sem("least_one"), sem("flip_done"), sem("odd_copied"), sem("root"))
            stats_set, mv_set, std_set, rstd_set, shift_set = (
                sem("stats"), sem("mv"), sem("std"), sem("rstd"), sem("shift"))
            t_done, masked_set, ht_set, y_done, odd_set, msg_set, same_set = (
                sem("t_done"), sem("masked"), sem("ht"), sem("y_done"), sem("odd"), sem("msg"), sem("same"))
            agg_done, carry_set, clear_set, relu_set, xb_set, x_set, h_set = (
                sem("agg_done"), sem("carry"), sem("clear"), sem("relu"), sem("xb"), sem("x"), sem("h"))
            ctx.callback(self.free, sems)
            block = ctx.enter_context(nc.Block())

            w = self.w1 if first else self.w2
            T, BIAS, MASK, Y, PICK, CARRY, SUM, OUT, STATS, NORM, RELU = (
                4 if first else 3, 4, 5, 7, 8, 9, 10, 10, 12, 13, 14)
            DRAIN = OUT + 2 if first else RELU + 1
            at = lambda it, j, skew: tile_at(it, j, skew, RING, TILES)
            used = lambda it, j, skew, ring: use_of(it, j, skew, ring, RING)

            def slot_rows(table, g):
                return table[bass.ds(g * (U * P), U * P), :].rearrange("(p k) c -> p (k c)", k=U)

            def slots(t, hf):
                return t[:, hf * U:(hf + 1) * U, :].rearrange("p k c -> p (k c)")

            p1_slots = self.p1_table[NP:NP + EP, :]
            h_out = p1_slots if first else self.h2_table[NP:NP + EP, :]

            @block.gpsimd
            def _(pool):
                src_table = self.h0_table if first else self.p1_table
                dst_table = self.p1_table[0:NP, :] if first else self.ins["x"]

                def step(it, j):
                    n = at(it, j, 0)
                    if n is None:
                        return
                    wait_apart(pool, staged, n + 1)
                    pool.indirect_dma_start(src_h[:, j, :], None, src_table[:, :],
                                            bass.IndirectOffsetOnAxis(ap=idx_now[:, j, 0:1], axis=0)).then_inc(src_got[j], 16)
                    pool.indirect_dma_start(dst_row[:, j, :], None, dst_table[:, :],
                                            bass.IndirectOffsetOnAxis(ap=idx_now[:, j, 1:2], axis=0)).then_inc(dst_got[j], 16)

                turns(pool, TURNS, RING, step, 0)

            @block.sync
            def _(sp):
                def load(it, hf):
                    g = 2 * it + hf
                    if not first:
                        wait_apart(sp, t_done, U * g - U)
                        sp.dma_start(slots(dst_p1, hf), slot_rows(p1_slots, g)).then_inc(dst_p1_loaded[hf], 16)
                    wait_apart(sp, masked_set, U * g - U)
                    if first:
                        sp.dma_start(self.dst_bc[:, bass.ds(g * (U * P), U * P)], self.dst_f[bass.ds(g * (U * P), U * P)]
                                     .rearrange("(a e) -> a e", a=1).broadcast_to([P, U * P])).then_inc(dst_loaded[hf], 16)
                    sp.dma_start(pair_bc[:, hf * U:(hf + 1) * U, :, :].rearrange("p k r e -> p (k r e)"),
                                 self.pairs.rearrange("t r e -> (t r e)")[bass.ds(g * (U * R // 2 * P), U * R // 2 * P)]
                                 .rearrange("(a e) -> a e", a=1).broadcast_to([P, U * R // 2 * P])).then_inc(pair_loaded[hf], 16)

                def store(it, hf):
                    g = 2 * it + hf
                    if not first:
                        wait_apart(sp, x_set, U * g + U)
                        sp.dma_start(slot_rows(self.x2_slots, g), slots(out_x, hf)).then_inc(x_stored[hf], 16)
                    wait_apart(sp, h_set, U * g + U)
                    sp.dma_start(slot_rows(h_out, g), slots(out_h, hf)).then_inc(h_stored[hf], 16)

                if first:
                    sp.dma_start(count_r[:, :, :], self.count_f.rearrange("(i q f) -> q i f", i=2, q=HALF)).then_inc(count_loaded, 16)
                load(0, 0)
                load(0, 1)
                with sp.Fori(1, TURNS) as it:
                    load(it, 0)
                    store(it - 1, 0)
                    load(it, 1)
                    store(it - 1, 1)
                store(TURNS - 1, 0)
                store(TURNS - 1, 1)
                for hf in range(2):
                    if not first:
                        sp.wait_ge(x_stored[hf], 16 * TURNS)
                    sp.wait_ge(h_stored[hf], 16 * TURNS)

            @block.vector
            def _(v):
                def masks(it, j):
                    n = at(it, j, MASK)
                    if n is None:
                        return
                    s = (j - MASK) % 7
                    wait_for(v, agg_done, n - 6)
                    if first:
                        wait_for(v, dst_loaded[(j - MASK) % RING // U], 16 * used(it, j, MASK, RING) + 16)
                    edges = self.dst_bc[:, bass.ds(n * P, P)]
                    nc.vector.tensor_scalar(same[:, s, :], edges, self.dst_col[:, bass.ds(n, 1)], None, ALU.is_equal).then_inc(same_set, 1)

                def step(it, j):
                    n = at(it, j, CARRY)
                    if n is not None and not (isinstance(n, int) and n == 0):
                        s = (j - CARRY) % 7
                        wait_for(v, agg_done, n)
                        wait_for(v, msg_set, n + 1)
                        nc.vector.scalar_tensor_tensor(out=msg[:, s, :], in0=a_ps[(j - CARRY - 1) % 2][:, 0:P],
                                                       scalar=self.join_col[:, bass.ds(n, 1)],
                                                       in1=msg[:, s, :], op0=ALU.mult, op1=ALU.add).then_inc(carry_set, 1)
                    n = at(it, j, OUT)
                    if n is not None:
                        s, r, u = (j - OUT) % 2, (j - OUT) % RING, used(it, j, OUT, RING)
                        wait_for(v, agg_done, n + 1)
                        if first:
                            wait_for(v, dst_got[r], 16 * u + 16)
                            wait_for(v, h_stored[r // U], 16 * u)
                            nc.vector.tensor_tensor(out_h[:, r, :], a_ps[s][:, 0:P], dst_row[:, r, :], ALU.add).then_inc(h_set, 1)
                        else:
                            wait_for(v, x_stored[r // U], 16 * u)
                            wait_for(v, xb_set, n + 1)
                            nc.vector.tensor_tensor(out_x[:, r, :], a_ps[s][:, 0:P], dst_row[:, r, :], ALU.add).then_inc(x_set, 1)
                    k = at(it, j, NORM) if (j - NORM) % 2 == 1 else None
                    if not first and k is not None:
                        b = (j - NORM) % RING
                        wait_for(v, std_set, k + 1)
                        nc.vector.reciprocal(rstd[:, b - 1:b + 1], std[:, b - 1:b + 1]).then_inc(rstd_set, 2)
                    m = at(it, j, STATS)
                    if not first and m is not None:
                        c = (j - STATS) % RING
                        wait_for(v, x_set, m + 1)
                        nc.vector.bn_stats(stats[:, c % 7, :], out_x[:, c, :]).then_inc(stats_set, 1)
                    n = at(it, j, PICK)
                    if n is not None:
                        s = (j - PICK) % 2
                        wait_for(v, odd_set, n + 1)
                        wait_for(v, agg_done, n - 6)
                        nc.vector.scalar_tensor_tensor(out=msg[:, (j - PICK) % 7, :], in0=y_ps[s][:, 0:P], scalar=self.even_col[:, bass.ds(n, 1)],
                                                       in1=odd[:, s, :], op0=ALU.mult, op1=ALU.add).then_inc(msg_set, 1)
                    if not first and k is not None:
                        wait_for(v, rstd_set, k + 1)
                        nc.vector.scalar_tensor_tensor(out=shift[:, b - 1:b + 1], in0=mv[:, b - 1:b + 1, 0], scalar=-1.0,
                                                       in1=rstd[:, b - 1:b + 1], op0=ALU.mult, op1=ALU.mult).then_inc(shift_set, 2)
                    n = at(it, j, PICK)
                    if not first and n is not None and not (isinstance(n, int) and n == TILES - 1):
                        end, b = (P - 1 if (j - PICK) % 2 == 0 else 0), (j - PICK) % 7
                        own = ht[:, b, P + end:P + end + 1]
                        wait_for(v, ht_set, n + 1)
                        nc.vector.scalar_tensor_tensor(out=own, in0=self.dst_bc[:, bass.ds((n + 1) * P + end, 1)],
                                                       scalar=self.dst_bc[:, bass.ds(n * P + end, 1)],
                                                       in1=own, op0=ALU.not_equal, op1=ALU.mult).then_inc(clear_set, 1)
                    masks(it, j)
                    if not first and m is not None:
                        wait_apart(v, stats_set, m + 1)
                        nc.vector.bn_aggr(mv[:, c, :], stats[:, c % 7, :]).then_inc(mv_set, 1)
                    n = at(it, j, MASK)
                    if n is not None:
                        s, r, u = (j - MASK) % 2, (j - MASK) % RING, used(it, j, MASK, RING)
                        wait_for(v, t_done if first else ht_set, n + 1)
                        of = t_ps[s][:, 0:P] if first else ht[:, r % 7, 0:P]
                        wait_for(v, y_done, n - 6)
                        wait_for(v, pair_loaded[r // U], 16 * u + 16)
                        nc.vector.scalar_tensor_tensor(out=ht_masked[:, r % 7, :, :], in0=pair_bc[:, r, :, :], scalar=1.0,
                                                       in1=of[:, None, :].broadcast_to([P, R // 2, P]),
                                                       op0=ALU.mult, op1=ALU.mult).then_inc(masked_set, 1)
                    n = at(it, j, Y)
                    if not first and n is not None and (j - Y) % 2 == 1:
                        r, u = (j - Y) % RING, used(it, j, Y, RING)
                        wait_for(v, dst_got[r - 1], 16 * u + 16)
                        wait_for(v, dst_got[r], 16 * u + 16)
                        nc.vector.tensor_tensor(dst_row[:, r - 1:r + 1, :], dst_row[:, r - 1:r + 1, :],
                                                self.b2[:, :].rearrange("p (a c) -> p a c", a=1).broadcast_to([P, 2, P]),
                                                ALU.add).then_inc(xb_set, 2)

                if first:
                    v.wait_ge(count_cols, 1)
                    nc.vector.tensor_scalar(least_one[:, :], count_ps[:, 0:TILES], 1.0, None, ALU.max).then_inc(least_set, 1)
                    v.wait_ge(flip_done, 1)
                    v.wait_ge(least_set, 1)
                    nc.vector.tensor_copy(odd_or_even(least_one, 1), odd_or_even(flip_ps[:, 0:TILES], 1)).then_inc(odd_copied, 1)
                turns(v, TURNS, RING, step, DRAIN)
                if first:
                    v.wait_ge(root_set, 1)
                    nc.vector.reciprocal(self.isd_col[:, :], root[:, :])

            @block.scalar
            def _(act):
                def step(it, j):
                    n = at(it, j, 0)
                    if n is not None:
                        wait_for(act, t_done, n - RING + 1)
                        wait_for(act, h_set if first else x_set, n - RING + 1)
                        if first:
                            nc.scalar.copy(idx_now[:, j, :], self.ends_idx[:, bass.ds(n, 1), :].rearrange("p a k -> p (a k)")).then_inc(staged, 1)
                        else:
                            nc.scalar.copy(idx_now[:, j, 0:1], self.state_idx[:, bass.ds(n, 1)])
                            nc.scalar.copy(idx_now[:, j, 1:2], self.ends_idx[:, bass.ds(n, 1), 1]).then_inc(staged, 1)
                    n = at(it, j, PICK)
                    if n is not None:
                        s = (j - PICK) % 2
                        wait_for(act, y_done, n + 1)
                        wait_for(act, msg_set, n - 1)
                        nc.scalar.activation(odd[:, s, :], y_ps[s][:, P:2 * P], ACT.Copy,
                                             scale=self.odd_col[:, bass.ds(n, 1)]).then_inc(odd_set, 1)
                    if first:
                        return
                    n = at(it, j, BIAS)
                    if n is not None:
                        s, b = (j - BIAS) % 2, (j - BIAS) % 7
                        wait_for(act, t_done, n + 1)
                        nc.scalar.activation(ht_relu[:, s, :], t_ps[s][:, 0:2 * P], ACT.Relu).then_inc(relu_set, 1)
                        wait_for(act, relu_set, n + 1)
                        wait_for(act, agg_done, n - 6)
                        wait_for(act, masked_set, n - 6)
                        nc.scalar.activation(ht[:, b, :], ht_relu[:, s, :], ACT.Identity, bias=self.b1_col[:, :]).then_inc(ht_set, 1)
                    n = at(it, j, RELU)
                    if n is not None:
                        r = b = (j - RELU) % RING
                        wait_for(act, shift_set, n + 1)
                        wait_for(act, h_stored[r // U], 16 * used(it, j, RELU, RING))
                        nc.scalar.activation(out_h[:, r, :], out_x[:, r, :], ACT.Relu, bias=shift[:, b:b + 1],
                                             scale=rstd[:, b:b + 1]).then_inc(h_set, 1)
                    n = at(it, j, STATS)
                    if n is not None:
                        b = (j - STATS) % RING
                        wait_for(act, mv_set, n + 1)
                        nc.scalar.activation(std[:, b:b + 1], mv[:, b, 1:2], ACT.Sqrt, bias=self.eps[:, :]).then_inc(std_set, 1)

                turns(act, TURNS, RING, step, DRAIN)
                if first:
                    act.wait_ge(odd_copied, 1)
                    nc.scalar.activation(root[:, :], least_one[:, :], ACT.Sqrt).then_inc(root_set, 1)

            @block.tensor
            def _(pe):
                def step(it, j):
                    n = at(it, j, SUM)
                    if n is not None:
                        s, b = (j - SUM) % 2, (j - SUM) % 7
                        wait_for(pe, h_set if first else x_set, n - 1)
                        if not first:
                            wait_for(pe, clear_set, min(n + 1, TILES - 1) if isinstance(n, int) else n + 1)
                            wait_for(pe, ht_set, n + 1)
                            nc.tensor.matmul(a_ps[s][:, 0:P], ht[:, b, P:2 * P], self.sw2[:, :], start=True, stop=False)
                        if isinstance(n, int) and n == 0:
                            wait_for(pe, msg_set, 1)
                        wait_for(pe, carry_set, n)
                        wait_for(pe, same_set, n + 1)
                        nc.tensor.matmul(a_ps[s][:, 0:P], same[:, b, :], msg[:, b, :], start=first, stop=True).then_inc(agg_done, 1)
                    n = at(it, j, Y)
                    if n is not None:
                        s = (j - Y) % 2
                        wait_for(pe, masked_set, n + 1)
                        wait_for(pe, msg_set, n - 1)
                        for q in range(R // 2):
                            last = nc.tensor.matmul(y_ps[s][:, 0:2 * P], ht_masked[:, (j - Y) % 7, q, :],
                                                    w[:, 2 * q:2 * q + 2, :].rearrange("c r o -> c (r o)"),
                                                    start=(q == 0), stop=(q == R // 2 - 1))
                        last.then_inc(y_done, 1)
                    n = at(it, j, T)
                    if n is not None:
                        s, r, u = (j - T) % 2, (j - T) % RING, used(it, j, T, RING)
                        wait_for(pe, src_got[r], 16 * u + 16)
                        wait_for(pe, masked_set if first else relu_set, n - 1)
                        last = nc.tensor.transpose(t_ps[s][:, 0:P], src_h[:, r, :], self.ident[:, :])
                        if not first:
                            wait_for(pe, dst_p1_loaded[r // U], 16 * u + 16)
                            last = nc.tensor.transpose(t_ps[s][:, P:2 * P], dst_p1[:, r, :], self.ident[:, :])
                        last.then_inc(t_done, 1)

                if first:
                    pe.wait_ge(count_loaded, 16)
                    for i in range(2):
                        last = nc.tensor.transpose(count_ps[:, i * HALF:(i + 1) * HALF], count_r[:, i, :], self.ident[0:HALF, 0:HALF])
                    last.then_inc(count_cols, 1)
                    pe.wait_ge(least_set, 1)
                    nc.tensor.matmul(flip_ps[:, 0:TILES], self.flip[:, :], least_one[:, :], start=True, stop=True).then_inc(flip_done, 1)
                turns(pe, TURNS, RING, step, DRAIN)

    def conv(self, layer):
        nc, last_layer = self.nc, layer == 5
        with ExitStack() as ctx:
            def sb(name, shape, dt=F32):
                return ctx.enter_context(nc.sbuf_tensor(f"c{layer}_{name}", shape, dt))

            sems = []

            def sem(name):
                sems.append(nc.alloc_semaphore(f"c{layer}_{name}"))
                return sems[-1]

            src_h = sb("src_h", [P, RING, P])
            edge = sb("edge", [P, RING, P])
            res = sb("res", [P, RING, P])
            same = sb("same", [P, 2, P])
            agg_t = sb("agg_t", [P, 2, P])
            out_h = sb("out_h", [P, RING, P])
            local_h = None if last_layer else sb("local_h", [P, RING, P])
            idx_now = sb("idx_now", [P, RING, 2], I32)
            a_ps = [ctx.enter_context(nc.psum_tensor(f"c{layer}_a_ps{i}", [P, 512], F32)) for i in range(2)]
            p_ps = [ctx.enter_context(nc.psum_tensor(f"c{layer}_p_ps{i}", [P, 512], F32)) for i in range(2)]

            gathered = [sem(f"gathered{i}") for i in range(RING)]
            scattered = [sem(f"scattered{i}") for i in range(RING)] if last_layer else None
            edge_loaded = [sem(f"edge_loaded{i}") for i in range(2)]
            res_loaded = [sem(f"res_loaded{i}") for i in range(2)]
            out_stored = [sem(f"out_stored{i}") for i in range(2)]
            local_stored = [sem(f"local_stored{i}") for i in range(2)]
            joins_loaded = [sem(f"joins_loaded{i}") for i in range(2)]
            staged, same_set, agg_done, agg_set, p_done, out_set, out_relu, local_set, local_relu, put_staged = (
                sem("staged"), sem("same"), sem("agg_done"), sem("agg_set"), sem("p_done"), sem("out"),
                sem("out_relu"), sem("local"), sem("local_relu"), sem("put_staged"))
            ctx.callback(self.free, sems)
            block = ctx.enter_context(nc.Block())

            source = {3: self.h2_table, 4: self.h3_table, 5: self.h4_table}[layer]
            target = {3: self.h3_table, 4: self.h4_table, 5: None}[layer]
            idx = self.state_idx if layer == 3 else self.local_idx
            residual = {3: self.h2_table[NP:NP + EP, :], 4: self.h3_table[EP:2 * EP, :], 5: self.x2_slots}[layer]
            w, bias = self.gw[layer - 3], self.gb[layer - 3]
            MASKS, AGG, CARRY, SELF, OUT, RELU = 7, 8, 9, 10, 11, 12
            DRAIN = RELU + 1
            at = lambda it, j, skew: tile_at(it, j, skew, RING, TILES)
            used = lambda it, j, skew, ring: use_of(it, j, skew, ring, RING)

            def slot_rows(table, g):
                return table[bass.ds(g * (U * P), U * P), :].rearrange("(p k) c -> p (k c)", k=U)

            def slots(t, hf):
                return t[:, hf * U:(hf + 1) * U, :].rearrange("p k c -> p (k c)")

            @block.gpsimd
            def _(pool):
                def step(it, j):
                    n = at(it, j, 0)
                    if n is not None:
                        wait_for(pool, staged, n + 1)
                        pool.nop(nofuse=True)
                        pool.indirect_dma_start(src_h[:, j, :], None, source[:, :],
                                                bass.IndirectOffsetOnAxis(ap=idx_now[:, j, 0:1], axis=0)).then_inc(gathered[j], 16)
                    n = at(it, j, RELU)
                    if last_layer and n is not None:
                        r = (j - RELU) % RING
                        wait_for(pool, put_staged, n + 1)
                        wait_for(pool, out_set, n + 1)
                        pool.nop(nofuse=True)
                        pool.indirect_dma_start(self.out[:, :], bass.IndirectOffsetOnAxis(ap=idx_now[:, r, 1:2], axis=0),
                                                out_h[:, r, :], None, bounds_check=NP - 1, oob_is_err=False).then_inc(scattered[r], 16)

                turns(pool, TURNS, RING, step, DRAIN if last_layer else 0)
                if last_layer:
                    for r in range(RING):
                        pool.wait_ge(scattered[r], 16 * TURNS)

            @block.sync
            def _(sp):
                def load(it, hf):
                    g = 2 * it + hf
                    wait_apart(sp, agg_done, U * g - U)
                    sp.dma_start(edge[:, hf * U:(hf + 1) * U, :], self.ins["edge"][bass.ds(g * (U * P), U * P), :]
                                 .rearrange("(k p) c -> p k c", p=P)).then_inc(edge_loaded[hf], 16)
                    if layer == 3:
                        sp.dma_start(self.joins[:, bass.ds(g * (U * P), U * P)], self.joins_row[bass.ds(g * (U * P), U * P)]
                                     .rearrange("(a e) -> a e", a=1).broadcast_to([P, U * P])).then_inc(joins_loaded[hf], 16)
                    wait_apart(sp, out_set, U * g - U)
                    sp.dma_start(slots(res, hf), slot_rows(residual, g)).then_inc(res_loaded[hf], 16)

                def store(it, hf):
                    if last_layer:
                        return
                    g = 2 * it + hf
                    wait_apart(sp, local_relu, U * g + U)
                    sp.dma_start(slot_rows(target[0:EP, :], g), slots(local_h, hf)).then_inc(local_stored[hf], 16)
                    wait_apart(sp, out_relu, U * g + U)
                    sp.dma_start(slot_rows(target[EP:2 * EP, :], g), slots(out_h, hf)).then_inc(out_stored[hf], 16)

                load(0, 0)
                load(0, 1)
                with sp.Fori(1, TURNS) as it:
                    load(it, 0)
                    store(it - 1, 0)
                    load(it, 1)
                    store(it - 1, 1)
                store(TURNS - 1, 0)
                store(TURNS - 1, 1)
                if not last_layer:
                    for hf in range(2):
                        sp.wait_ge(local_stored[hf], 16 * TURNS)
                        sp.wait_ge(out_stored[hf], 16 * TURNS)

            @block.vector
            def _(v):
                def step(it, j):
                    n = at(it, j, MASKS)
                    if n is not None:
                        s = (j - MASKS) % 2
                        wait_for(v, agg_done, n - 1)
                        edges = self.dst_bc[:, bass.ds(n * P, P)]
                        nc.vector.tensor_scalar(same[:, s, :], edges, self.dst_col[:, bass.ds(n, 1)],
                                                None, ALU.is_equal).then_inc(same_set, 1)
                    n = at(it, j, CARRY)
                    if n is not None:
                        s = (j - CARRY) % 2
                        if isinstance(n, int) and n == 0:
                            nc.vector.memset(agg_t[:, 1, :], 0.0).then_inc(agg_set, 1)
                        ends = 0 if (j - CARRY) % 2 == 0 else P - 1
                        wait_for(v, agg_done, n + 1)
                        wait_for(v, agg_set, n + 1)
                        if layer == 3:
                            wait_for(v, joins_loaded[(j - CARRY) % RING // U], 16 * used(it, j, CARRY, RING) + 16)
                        wait_for(v, p_done, n - 1)
                        nc.vector.scalar_tensor_tensor(out=agg_t[:, s, :], in0=self.joins[:, bass.ds(n * P, P)],
                                                       scalar=agg_t[:, 1 - s, ends:ends + 1], in1=a_ps[s][:, 0:P],
                                                       op0=ALU.mult, op1=ALU.add).then_inc(agg_set, 1)
                    n = at(it, j, AGG)
                    if n is not None and not last_layer:
                        r, u = (j - AGG) % RING, used(it, j, AGG, RING)
                        wait_for(v, gathered[r], 16 * u + 16)
                        wait_for(v, local_stored[r // U], 16 * u)
                        nc.vector.tensor_tensor(local_h[:, r, :], src_h[:, r, :], bias[:, :], ALU.add).then_inc(local_set, 1)
                    n = at(it, j, OUT)
                    if n is not None:
                        s, r, u = (j - OUT) % 2, (j - OUT) % RING, used(it, j, OUT, RING)
                        wait_for(v, p_done, n + 1)
                        wait_for(v, res_loaded[r // U], 16 * u + 16)
                        if last_layer:
                            wait_for(v, scattered[r], 16 * u)
                        else:
                            wait_for(v, out_stored[r // U], 16 * u)
                        nc.vector.scalar_tensor_tensor(out=out_h[:, r, :], in0=p_ps[s][:, 0:P], scalar=self.isd_col[:, bass.ds(n, 1)],
                                                       in1=res[:, r, :], op0=ALU.mult, op1=ALU.add).then_inc(out_set, 1)

                turns(v, TURNS, RING, step, DRAIN)

            @block.scalar
            def _(act):
                def step(it, j):
                    n = at(it, j, 0)
                    if n is not None:
                        wait_for(act, agg_done, n - RING + 1)
                        if not last_layer:
                            wait_for(act, local_set, n - RING + 1)
                        nc.scalar.copy(idx_now[:, j, 0:1], idx[:, bass.ds(n, 1)]).then_inc(staged, 1)
                    if last_layer:
                        n = at(it, j, OUT)
                        if n is not None:
                            r = (j - OUT) % RING
                            wait_for(act, scattered[r], 16 * used(it, j, OUT, RING))
                            nc.scalar.copy(idx_now[:, r, 1:2], self.end_idx[:, bass.ds(n, 1)]).then_inc(put_staged, 1)
                        return
                    n = at(it, j, CARRY)
                    if n is not None:
                        r = (j - CARRY) % RING
                        wait_for(act, local_set, n + 1)
                        nc.scalar.activation(local_h[:, r, :], local_h[:, r, :], ACT.Relu).then_inc(local_relu, 1)
                    n = at(it, j, RELU)
                    if n is not None:
                        r = (j - RELU) % RING
                        wait_for(act, out_set, n + 1)
                        nc.scalar.activation(out_h[:, r, :], out_h[:, r, :], ACT.Relu).then_inc(out_relu, 1)

                turns(act, TURNS, RING, step, DRAIN)

            @block.tensor
            def _(pe):
                def step(it, j):
                    n = at(it, j, AGG)
                    if n is not None:
                        s, r, u = (j - AGG) % 2, (j - AGG) % RING, used(it, j, AGG, RING)
                        wait_for(pe, gathered[r], 16 * u + 16)
                        wait_for(pe, edge_loaded[r // U], 16 * u + 16)
                        wait_for(pe, same_set, n + 1)
                        wait_for(pe, agg_set, n)
                        nc.tensor.matmul(a_ps[s][:, 0:P], src_h[:, r, :], same[:, s, :], start=True, stop=False)
                        nc.tensor.matmul(a_ps[s][:, 0:P], edge[:, r, :], same[:, s, :], start=False, stop=True).then_inc(agg_done, 1)
                    n = at(it, j, SELF)
                    if n is not None:
                        s = (j - SELF) % 2
                        wait_for(pe, agg_set, n + 2)
                        wait_for(pe, out_set, n - 1)
                        nc.tensor.matmul(p_ps[s][:, 0:P], agg_t[:, s, :], w[:, :], start=True, stop=False)
                        nc.tensor.matmul(p_ps[s][:, 0:P], self.ones[0:1, :], self.gb_row[0:1, layer - 3, :],
                                         start=False, stop=True).then_inc(p_done, 1)

                turns(pe, TURNS, RING, step, DRAIN)


def program(nc, ins, out):
    Program(nc, ins, out).build()


def kernel(**inputs):
    import numpy as np
    import concourse.bacc as bacc
    from concourse.bass_utils import run_bass_kernel_spmd as run

    def padded(a, before, after, value):
        a = np.asarray(a)
        front = np.full((before,) + a.shape[1:], value, a.dtype)
        back = np.full((after,) + a.shape[1:], value, a.dtype)
        return np.concatenate([front, a, back])

    def tiled(a):
        a = a.reshape((TILES, P) + a.shape[1:]).copy()
        a[1::2] = a[1::2, ::-1]
        return a.reshape((EP,) + a.shape[2:])

    extra = EP - E
    dst = padded(inputs["dst"], 0, extra, PAD_NODE)
    arrays = {
        "x": padded(inputs["x"], 0, NP - N, 0),
        "src": tiled(padded(inputs["src"], 0, extra, PAD_NODE)),
        "dst": tiled(dst),
        "dst_next": tiled(padded(dst[1:], 0, 1, -1)),
        "dst_line": padded(dst, 1, 0, -1),
        "dst_before": padded(dst, 1, 0, -1)[0:EP:P].reshape(2, HALF).T,
        "typ": tiled(padded(inputs["edge_type_8"], 0, extra, 0)),
        "edge": tiled(padded(inputs["edge_attr_128"], 0, extra, 0)),
        "w1": inputs["L0_gnn_w1"], "sw1": inputs["L0_gnn_sw1"], "b1": inputs["L0_gnn_b1"],
        "w2": inputs["L0_gnn_w2"], "sw2": inputs["L0_gnn_sw2"], "b2": inputs["L0_gnn_b2"],
        "W0": inputs["L1_gnn_W0"], "W1": inputs["L1_gnn_W1"], "W2": inputs["L1_gnn_W2"],
        "g0": inputs["L1_gnn_b0"], "g1": inputs["L1_gnn_b1"], "g2": inputs["L1_gnn_b2"],
    }
    arrays = {k: np.ascontiguousarray(v) for k, v in arrays.items()}
    nc = bacc.Bacc("TRN2", target_bir_lowering=False, num_devices=1)
    ins = {k: nc.dram_tensor(f"in_{k}", a.shape, mybir.dt.from_np(a.dtype), kind="ExternalInput").ap()
           for k, a in arrays.items()}
    out = nc.dram_tensor("result", [NP, P], F32, kind="ExternalOutput").ap()
    program(nc, ins, out)
    r = run(nc, [{f"in_{k}": a for k, a in arrays.items()}], core_ids=[0])
    return r.results[0]["result"][:N]
```
